# Optimizing a Trainium2 kernel written in Bass

```python
import numpy as np
import jax
import jax.numpy as jnp

def _softmax(x, axis=-1):
    return jax.nn.softmax(x, axis=axis)

def _gelu(x):
    return jax.nn.gelu(x, approximate=True)

def _silu(x):
    return jax.nn.silu(x)

def _sigmoid(x):
    return jax.nn.sigmoid(x)

def _layernorm(x, axis=-1, eps=1e-05):
    m = jnp.mean(x, axis=axis, keepdims=True)
    v = jnp.var(x, axis=axis, keepdims=True)
    return (x - m) / jnp.sqrt(v + eps)

def _scatter_add(tgt, idx, src, axis=0):
    return tgt.at[idx].add(src)

def _segment_sum(src, seg, n):
    return jax.ops.segment_sum(src, seg, n)
kernel_name = 'mk_metaformer_d1_conv_nhwc256_r2_977fab'

def setup_inputs(seed: int=0):
    np.random.seed(seed)
    _w = jnp.asarray

    def _rec_inputs():
        import jax
        import jax.numpy as jnp
        _gk = jax.random.key(seed)
        x = -0.0002928 + 1 * jax.random.normal(jax.random.fold_in(_gk, 1), (4, 32, 32, 128), jnp.float32)
        return x
    x = _rec_inputs()

    def _L0_conv_setup():
        import jax, jax.numpy as jnp
        from jax import lax
        import numpy as np
        K = 3
        DG = 1
        PAD = 1

        def _dcn_forward(x, w_offset, b_offset, filt):
            B, H, W, C = x.shape
            F = filt.shape[0]
            KK = K * K
            Cg = C // DG
            HW = H * W
            wi = lax.conv_general_dilated(x, w_offset, window_strides=(1, 1), padding='SAME', dimension_numbers=('NHWC', 'HWIO', 'NHWC')) + b_offset
            wi = jnp.transpose(wi, (0, 3, 1, 2))
            o1, o2, m = jnp.split(wi, 3, axis=1)
            mask = jax.nn.sigmoid(m).reshape(B, DG, KK, 1, HW)
            ki, kj = jnp.divmod(jnp.arange(KK), K)
            base_y = (jnp.arange(H)[None, :, None] - PAD + ki[:, None, None]).astype(jnp.float32)
            base_x = (jnp.arange(W)[None, None, :] - PAD + kj[:, None, None]).astype(jnp.float32)
            py = o1.reshape(B, DG, KK, H, W) + base_y[None, None]
            px = o2.reshape(B, DG, KK, H, W) + base_x[None, None]
            y0f = jnp.floor(py)
            x0f = jnp.floor(px)
            dy = (py - y0f).reshape(B, DG, KK, 1, HW)
            dx = (px - x0f).reshape(B, DG, KK, 1, HW)
            y0 = y0f.astype(jnp.int32)
            x0 = x0f.astype(jnp.int32)
            xg = x.reshape(B, HW, DG, Cg).transpose(0, 2, 3, 1)

            def gather(yi, xi):
                valid = (yi >= 0) & (yi < H) & (xi >= 0) & (xi < W)
                yc = jnp.clip(yi, 0, H - 1)
                xc = jnp.clip(xi, 0, W - 1)
                idx = (yc * W + xc).reshape(B, DG, KK, 1, HW)
                v = jnp.take_along_axis(xg[:, :, None, :, :], idx, axis=-1)
                return v * valid.reshape(B, DG, KK, 1, HW).astype(x.dtype)
            v00 = gather(y0, x0)
            v01 = gather(y0, x0 + 1)
            v10 = gather(y0 + 1, x0)
            v11 = gather(y0 + 1, x0 + 1)
            sampled = (v00 * (1 - dy) * (1 - dx) + v01 * (1 - dy) * dx + v10 * dy * (1 - dx) + v11 * dy * dx) * mask
            col = sampled.transpose(0, 2, 1, 3, 4).reshape(B, KK, C, HW)
            w = filt.reshape(F, C, KK)
            out = jnp.einsum('bkcp,fck->bfp', col, w).reshape(B, F, H, W)
            return jnp.transpose(out, (0, 2, 3, 1))
        key = jax.random.key(seed)
        k1, k2, k3 = jax.random.split(key, 3)
        B, H, W, C, F = (4, 32, 32, 128, 128)
        x = jax.random.normal(k1, (B, H, W, C), jnp.float32)
        w_offset = jax.random.normal(k2, (K, K, C, DG * 3 * K * K), jnp.float32) * 0.01
        b_offset = jnp.zeros((DG * 3 * K * K,), jnp.float32)
        filt = jax.random.normal(k3, (F, C, K, K), jnp.float32) * 0.05
        return {'x': x, 'w_offset': w_offset, 'b_offset': b_offset, 'filt': filt}
    _L0_conv_all = _L0_conv_setup()
    _L0_conv_in = {k: v for k, v in _L0_conv_all.items() if k in ('w_offset', 'b_offset', 'filt')}
    del _L0_conv_all

    def _L0_ffn_setup():
        import jax, jax.numpy as jnp
        import numpy as np
        B, T, D, H, E = (16, 2048, 128, 256, 8)
        key = jax.random.key(seed)
        ks = jax.random.split(key, 5)
        x = jax.random.normal(ks[0], (B, T, D), dtype=jnp.float32)
        gate_w = jax.random.normal(ks[1], (D, E), dtype=jnp.float32) * 0.02
        gate_b = jnp.zeros((E,), dtype=jnp.float32)
        W1 = jax.random.normal(ks[2], (E, D, H), dtype=jnp.float32) * 0.02
        b1 = jnp.zeros((E, H), dtype=jnp.float32)
        W2 = jax.random.normal(ks[3], (E, H, D), dtype=jnp.float32) * 0.02
        b2 = jnp.zeros((E, D), dtype=jnp.float32)
        return {'x': x, 'gate_w': gate_w, 'gate_b': gate_b, 'W1': W1, 'b1': b1, 'W2': W2, 'b2': b2}
    _L0_ffn_all = _L0_ffn_setup()
    _L0_ffn_in = {k: v for k, v in _L0_ffn_all.items() if k in ('gate_w', 'gate_b', 'W1', 'b1', 'W2', 'b2')}
    del _L0_ffn_all
    return {'x': x, 'L0_conv_w_offset': _L0_conv_in['w_offset'], 'L0_conv_b_offset': _L0_conv_in['b_offset'], 'L0_conv_filt': _L0_conv_in['filt'], 'L0_ffn_gate_w': _L0_ffn_in['gate_w'], 'L0_ffn_gate_b': _L0_ffn_in['gate_b'], 'L0_ffn_W1': _L0_ffn_in['W1'], 'L0_ffn_b1': _L0_ffn_in['b1'], 'L0_ffn_W2': _L0_ffn_in['W2'], 'L0_ffn_b2': _L0_ffn_in['b2']}

def reference(x, L0_conv_w_offset, L0_conv_b_offset, L0_conv_filt, L0_ffn_gate_w, L0_ffn_gate_b, L0_ffn_W1, L0_ffn_b1, L0_ffn_W2, L0_ffn_b2):
    import jax
    import jax.numpy as jnp

    def _L0_conv_ref(x, w_offset, b_offset, filt):
        import jax, jax.numpy as jnp
        from jax import lax
        import numpy as np
        K = 3
        DG = 1
        PAD = 1

        def _dcn_forward(x, w_offset, b_offset, filt):
            B, H, W, C = x.shape
            F = filt.shape[0]
            KK = K * K
            Cg = C // DG
            HW = H * W
            wi = lax.conv_general_dilated(x, w_offset, window_strides=(1, 1), padding='SAME', dimension_numbers=('NHWC', 'HWIO', 'NHWC')) + b_offset
            wi = jnp.transpose(wi, (0, 3, 1, 2))
            o1, o2, m = jnp.split(wi, 3, axis=1)
            mask = jax.nn.sigmoid(m).reshape(B, DG, KK, 1, HW)
            ki, kj = jnp.divmod(jnp.arange(KK), K)
            base_y = (jnp.arange(H)[None, :, None] - PAD + ki[:, None, None]).astype(jnp.float32)
            base_x = (jnp.arange(W)[None, None, :] - PAD + kj[:, None, None]).astype(jnp.float32)
            py = o1.reshape(B, DG, KK, H, W) + base_y[None, None]
            px = o2.reshape(B, DG, KK, H, W) + base_x[None, None]
            y0f = jnp.floor(py)
            x0f = jnp.floor(px)
            dy = (py - y0f).reshape(B, DG, KK, 1, HW)
            dx = (px - x0f).reshape(B, DG, KK, 1, HW)
            y0 = y0f.astype(jnp.int32)
            x0 = x0f.astype(jnp.int32)
            xg = x.reshape(B, HW, DG, Cg).transpose(0, 2, 3, 1)

            def gather(yi, xi):
                valid = (yi >= 0) & (yi < H) & (xi >= 0) & (xi < W)
                yc = jnp.clip(yi, 0, H - 1)
                xc = jnp.clip(xi, 0, W - 1)
                idx = (yc * W + xc).reshape(B, DG, KK, 1, HW)
                v = jnp.take_along_axis(xg[:, :, None, :, :], idx, axis=-1)
                return v * valid.reshape(B, DG, KK, 1, HW).astype(x.dtype)
            v00 = gather(y0, x0)
            v01 = gather(y0, x0 + 1)
            v10 = gather(y0 + 1, x0)
            v11 = gather(y0 + 1, x0 + 1)
            sampled = (v00 * (1 - dy) * (1 - dx) + v01 * (1 - dy) * dx + v10 * dy * (1 - dx) + v11 * dy * dx) * mask
            col = sampled.transpose(0, 2, 1, 3, 4).reshape(B, KK, C, HW)
            w = filt.reshape(F, C, KK)
            out = jnp.einsum('bkcp,fck->bfp', col, w).reshape(B, F, H, W)
            return jnp.transpose(out, (0, 2, 3, 1))
        return _dcn_forward(x, w_offset, b_offset, filt)

    def _L0_ffn_ref(x, gate_w, gate_b, W1, b1, W2, b2):
        import jax, jax.numpy as jnp
        import numpy as np
        B, T, D, H, E = (16, 2048, 128, 256, 8)
        Bb, Tt, Dd = x.shape
        Ee = gate_w.shape[1]
        xf = x.reshape(-1, Dd)
        N = xf.shape[0]
        logits = xf @ gate_w + gate_b
        probs = jax.nn.softmax(logits, axis=-1)
        top2_vals, top2_idx = jax.lax.top_k(probs, 2)
        cw = jnp.zeros((N, Ee), dtype=xf.dtype).at[jnp.arange(N)[:, None], top2_idx].add(top2_vals)

        def step(acc, params):
            w1, bb1, w2, bb2, we = params
            h = jax.nn.gelu(xf @ w1 + bb1, approximate=False)
            y = h @ w2 + bb2
            return (acc + we[:, None] * y, None)
        out, _ = jax.lax.scan(step, jnp.zeros_like(xf), (W1, b1, W2, b2, cw.T))
        return out.reshape(Bb, Tt, Dd)

    def _gn(v, G=32, eps=1e-05):
        B_, H_, W_, C_ = v.shape
        g = v.reshape(B_, H_, W_, G, C_ // G)
        m = jnp.mean(g, axis=(1, 2, 4), keepdims=True)
        s = jnp.var(g, axis=(1, 2, 4), keepdims=True)
        return ((g - m) / jnp.sqrt(s + eps)).reshape(v.shape)

    def _ln_c(v, eps=1e-06):
        m = jnp.mean(v, axis=-1, keepdims=True)
        s = jnp.var(v, axis=-1, keepdims=True)
        return (v - m) / jnp.sqrt(s + eps)

    def _ln_t(v, eps=1e-05):
        m = jnp.mean(v, axis=-1, keepdims=True)
        s = jnp.var(v, axis=-1, keepdims=True)
        return (v - m) / jnp.sqrt(s + eps)

    def _to_tokens(v):
        B_, H_, W_, C_ = v.shape
        return v.reshape(B_, H_ * W_, C_)

    def _from_tokens(t, like):
        return t.reshape(like.shape)
    x = x + _L0_conv_ref(_ln_c(x), L0_conv_w_offset, L0_conv_b_offset, L0_conv_filt)
    t = _to_tokens(x)
    t = t + _L0_ffn_ref(_ln_t(t), L0_ffn_gate_w, L0_ffn_gate_b, L0_ffn_W1, L0_ffn_b1, L0_ffn_W2, L0_ffn_b2)
    x = _from_tokens(t, x)
    return x

_drawn_inputs = setup_inputs


def setup_inputs(seed=0):
    import zlib

    import numpy as np

    out = dict(_drawn_inputs(seed))
    spreads = {'L0_conv_b_offset': (0.0, 0.1),
     'L0_ffn_gate_b': (0.0, 0.554),
     'L0_ffn_b1': (0.0, 0.8),
     'L0_ffn_b2': (0.0, 0.412)}
    factors = {'L0_ffn_gate_w': 3.158, 'L0_ffn_W1': 7.348, 'L0_ffn_W2': 6.683}
    for name, (base, spread) in spreads.items():
        noise = np.random.default_rng([zlib.crc32(name.encode()), seed]).standard_normal(out[name].shape)
        drawn = base * np.exp(spread * noise) if base else spread * noise
        out[name] = jnp.asarray(drawn.astype(out[name].dtype))
    for name, factor in factors.items():
        out[name] = (out[name] * factor).astype(out[name].dtype)
    return out
```

```python
from contextlib import ExitStack

import concourse.bass as bass
from concourse import mybir

F32 = mybir.dt.float32
BF16 = mybir.dt.bfloat16
I32 = mybir.dt.int32
U32 = mybir.dt.uint32
ALU = mybir.AluOpType
ACT = mybir.ActivationFunctionType
AX_X = mybir.AxisListType.X

P = 128
IMAGES, SIDE = 4, 32
C = 128
TAPS = 9
OFFS = 3 * TAPS
TILE = 4
TILES = SIDE // TILE
BANDS = IMAGES * SIDE // TILE
BPI = BANDS // IMAGES
REACH = 2
HALO = REACH + 1
WIN = TILE + 2 * HALO
Q = WIN * WIN
PADDED = SIDE + 2 * HALO
HATS = 2 * WIN
PARTS = 3
SLOT = PARTS * HATS
PAIRS = (TAPS + 1) // 2
TT = TILE * TILE
UNITS = [512, 512, 128]
GROUPS = [3, 3, 2]
EXPERTS, HID = 8, 256
HALVES = HID // P
FU = 4
LN_C_EPS, LN_T_EPS = 1e-6, 1e-5
N_CONSTS = 14
N_CLEARED = 8
SLOW_LINKS = 55


def window_constants():
    import numpy as np

    p = np.arange(P)
    dy, dx = (p % TT) // TILE, p % TILE
    tile = p // TT
    k = np.arange(TAPS)
    ky, kx = k // 3 - 1, k % 3 - 1
    j = np.arange(WIN)
    rel = np.zeros((P, TAPS, 2, WIN), np.float32)
    rel[:, :, 0, :] = (dy[:, None] + ky[None, :] + HALO)[:, :, None] - j
    rel[:, :, 1, :] = (dx[:, None] + kx[None, :] + HALO)[:, :, None] - j
    spread = np.zeros((2, PARTS, 2, WIN, 2, 2, Q), np.float32)
    q = np.arange(Q)
    for odd in range(2):
        for part in range(PARTS):
            spread[odd, part, 0, q // WIN, odd, 0, q] = 1
            spread[odd, part, 1, q % WIN, odd, 1, q] = 1
    spread = spread.reshape(2 * SLOT, 4 * Q)
    fold = np.zeros((4, 32, OFFS), np.float32)
    fold[:, np.arange(OFFS), np.arange(OFFS)] = 1
    base = np.zeros((BANDS, P, 2 * TAPS + 2), np.float32)
    for b in range(BANDS):
        base[b, :, 0:TAPS] = (TILE * (b % BPI) + dy)[:, None] + ky + HALO
        base[b, :, TAPS:2 * TAPS] = (TILE * tile + dx)[:, None] + kx + HALO
        base[b, :, 2 * TAPS:] = (b // BPI) * PADDED * PADDED
    return {
        "rel": rel.reshape(P, TAPS * HATS),
        "spread": spread,
        "fold": fold.reshape(P, OFFS),
        "base": base,
        "ident": np.eye(P, dtype=np.float32),
        "rank": np.broadcast_to(np.arange(EXPERTS, 0, -1, dtype=np.float32), (P, EXPERTS)).copy(),
    }


def program(nc, x_rows, x_tiles, w_offset, b_offset, filt, gate_w, gate_b, w1, b1, w2, b2,
            rel, spread, fold, base, ident, rank, out):
    with ExitStack() as ctx:
        def sb(name, shape, dt=F32):
            return ctx.enter_context(nc.sbuf_tensor(name, shape, dt))

        def sem(name):
            return ctx.enter_context(nc.semaphore(name))

        xpad = nc.dram_tensor("xpad", [IMAGES, PADDED, PADDED, C], F32, kind="Internal").ap()

        rel_sb = sb("rel_sb", [P, TAPS * HATS])
        spread_f = sb("spread_f", [2 * SLOT, 4, Q])
        spread_sb = sb("spread_sb", [2 * SLOT, 4, Q], BF16)
        fold_sb = sb("fold_sb", [P, OFFS])
        ident_sb = sb("ident_sb", [P, P])
        identb_sb = sb("identb_sb", [P, P], BF16)
        rank_sb = sb("rank_sb", [P, EXPERTS])
        woff_sb = sb("woff_sb", [C, TAPS, 32])
        boff_sb = sb("boff_sb", [P, OFFS])
        filt_sb = sb("filt_sb", [C, TAPS, C])
        gw_sb = sb("gw_sb", [C, EXPERTS])
        gb_sb = sb("gb_sb", [P, EXPERTS])
        w1_sb = sb("w1_sb", [C, EXPERTS, HID])
        b1_sb = sb("b1_sb", [P, EXPERTS * HALVES])
        w2_sb = sb("w2_sb", [P, EXPERTS, HALVES, C])
        b2_sb = sb("b2_sb", [EXPERTS, C])
        eps_c = sb("eps_c", [P, 1])
        eps_t = sb("eps_t", [P, 1])
        ones = sb("ones", [P, 1])
        zero = sb("zero", [P, HALO * C])

        x_nat = sb("x_nat", [P, BANDS, C])
        x1 = sb("x1", [P, BANDS, C])
        xnT = sb("xnT", [C, SIDE + 2, SIDE + 2])
        offs = sb("offs", [P, BANDS, OFFS])
        mask = sb("mask", [P, BANDS, TAPS, 2])
        tT = sb("tT", [C, BANDS, P])
        logits = sb("logits", [P, BANDS, EXPERTS])
        wts = sb("wts", [P, BANDS, EXPERTS])

        xn8 = sb("xn8", [P, BPI, C])
        st8 = sb("st8", [P, BPI, 6])
        mv8 = sb("mv8", [P, BPI, 2])
        sd8 = sb("sd8", [P, BPI])
        rs8 = sb("rs8", [P, BPI])
        conv_sb = sb("conv_sb", [P, 2, 512])
        near = sb("near", [P, BANDS * 2 * TAPS])
        near_n = sb("near_n", [P, 1])
        far = sb("far", [1, 1], I32)
        dist = sb("dist", [P, 2, TAPS * HATS])
        tent = sb("tent", [P, 2, TAPS * HATS])
        hat = sb("hat", [P, 2, TAPS * HATS])
        rest = sb("rest", [P, 2, TAPS * HATS])
        hat3 = sb("hat3", [P, 2, TAPS + 1, SLOT], BF16)
        hatT = sb("hatT", [2 * SLOT, PAIRS, P], BF16)
        ysp = sb("ysp", [Q, 2, 512])
        S = sb("S", [Q, 2, TAPS * P])
        xwin = sb("xwin", [Q, 2, TILES, C])
        samp = sb("samp", [C, 2, TAPS, P])
        st1 = sb("st1", [P, 2, 6])
        mv1 = sb("mv1", [P, 2, 2])
        sd1 = sb("sd1", [P, 2])
        rs1 = sb("rs1", [P, 2])
        xn2 = sb("xn2", [P, 2, C])
        xn2T = sb("xn2T", [C, 2, P])

        base_sb = sb("base_sb", [P, 2 * TAPS + 2])
        pos = sb("pos", [P, 2 * TAPS])
        posi = sb("posi", [P, 2 * TAPS], I32)
        posf = sb("posf", [P, 2 * TAPS])
        over = sb("over", [P, 2 * TAPS])
        low = sb("low", [P, 2 * TAPS])
        frac = sb("frac", [P, 2, 2, TAPS])
        line = sb("line", [P, TAPS])
        cell = sb("cell", [P, 4, TAPS])
        idx = sb("idx", [P, 4, TAPS], U32)
        wx = sb("wx", [P, 2, TAPS])
        cw = sb("cw", [P, 4, TAPS])
        corner = sb("corner", [P, 4, TAPS, C])
        gsum = sb("gsum", [P, TAPS, C])

        R = sb("R", [P, 8, BANDS * EXPERTS])
        r1 = sb("r1", [P, 6, BANDS])
        hid = sb("hid", [P, 4, 512])
        wcol = sb("wcol", [P, FU, EXPERTS])
        wT = sb("wT", [EXPERTS, FU, P])
        acc = sb("acc", [P, 2, FU, C])

        bank = [ctx.enter_context(nc.psum_tensor(f"bank{n}", [P, 512], F32)) for n in range(8)]
        bank4b = bank[4][:, :].bitcast(BF16)

        S_ = {}
        for name in (
            "settled tables_ready zeroed border_written x_loaded x1_loaded consts_loaded  "
            "stats8 std8 rstd8 xn8_ready xn_stored xnT_psum xnT_ready conv_psum conv_ready fold_psum "
            "offs_ready mask_ready near_ready near_psum far_ready dve_stat8 dve_hat dve_stat dve_rstd dve_slow dve_route dve_acc pool_step "
            "dist_ready hat_ready hi_ready hat3_ready hatT_psum hatT_ready y_psum x_psum y_ready S_ready "
            "win_even win_odd samp_psum samp_act samp_dve e_psum x1_ready std1_ready mean1_ready xn2_ready "
            "t_psum xn2T_ready l_psum logit_ready tT_ready "
            "base_loaded idx_ready gathered gsum_ready g_psum samp_slow "
            "exp_in exp_out wts_ready wcol_ready wT_psum wT_ready h_psum h_ready y2_psum y2_used b_psum "
            "stored stored_odd"
        ).split():
            S_[name] = sem(name)
        s = type("Sems", (), S_)

        block = ctx.enter_context(nc.Block())

        def image_view(bank_ap):
            return bank_ap.rearrange("c (r w) -> c r w", w=SIDE)

        HEAD = 3
        PAIRS_OF_BANDS = (BANDS - HEAD - 2) // 2
        TAIL = HEAD + 2 * PAIRS_OF_BANDS

        def settle(eng):
            eng.sem_inc(s.settled, 1)

        def is_far(eng):
            eng.wait_ge(s.far_ready, 1)
            return eng.value_load(far[0:1, 0:1], min_val=0, max_val=1)

        def at_least(eng, semaphore, value):
            if not isinstance(value, int) or value > 0:
                eng.wait_ge(semaphore, value)

        @block.sync
        def _(sp):
            for m in range(IMAGES):
                sp.dma_start(x_nat[:, m * BPI:(m + 1) * BPI, :],
                             x_rows[m * BPI:(m + 1) * BPI].rearrange("b p c -> p b c")).then_inc(s.x_loaded, 16)
                sp.wait_ge(s.x_loaded, 16 * (m + 1))
            sp.wait_ge(s.zeroed, 1)
            for m in range(IMAGES):
                for r0 in (0, HALO + SIDE):
                    sp.dma_start(xpad[m, r0:r0 + HALO, :, :], zero[0:HALO * PADDED, 0:C]).then_inc(s.border_written, 16)
                for c0 in (0, HALO + SIDE):
                    sp.dma_start(xpad[m, HALO:HALO + SIDE, c0:c0 + HALO, :],
                                 zero[0:SIDE, :]).then_inc(s.border_written, 16)
            with sp.Fori(0, IMAGES) as m:
                sp.wait_ge(s.xn8_ready, m + 1)
                for b in range(BPI):
                    sp.dma_start(xpad[m, HALO + TILE * b:HALO + TILE * (b + 1), HALO:HALO + SIDE, :],
                                 xn8[:, b, :]).then_inc(s.xn_stored, 16)
            sp.dma_start(x1[:, :, :], x_tiles.rearrange("b p c -> p b c")).then_inc(s.x1_loaded, 16)
            sp.wait_ge(s.border_written, 16 * 4 * IMAGES)
            sp.wait_ge(s.xn_stored, 16 * BANDS)

            def load_windows(b, par, image, row):
                at_least(sp, s.samp_psum, 3 * (b - 1))
                for t in range(TILES):
                    sp.dma_start(xwin[:, par, t, :], xpad[image, bass.ds(row, WIN), TILE * t:TILE * t + WIN, :]
                                 ).then_inc((s.win_even, s.win_odd)[par], 16)

            flag = is_far(sp)
            with sp.If(flag):
                with sp.Fori(0, BANDS) as b:
                    at_least(sp, s.logit_ready, b)
                    sp.dma_start(base_sb[:, :], base[b]).then_inc(s.base_loaded, 16)
            with sp.Else():
                for b in range(BPI):
                    load_windows(b, b % 2, 0, TILE * b)
                with sp.Fori(1, IMAGES) as m:
                    for r in range(BPI):
                        load_windows(m * BPI + r, r % 2, m, TILE * r)

            out_v = out.rearrange("(u b) p c -> u p b c", b=FU)
            with sp.Fori(0, BANDS // FU // 2) as i:
                for par in range(2):
                    sp.wait_ge(s.dve_acc, (i * 2 + par + 1) * (EXPERTS + 1))
                    sp.dma_start(out_v[i * 2 + par], acc[:, par, :, :]).then_inc((s.stored, s.stored_odd)[par], 16)
            sp.wait_ge(s.stored, 16 * (BANDS // FU // 2))
            sp.wait_ge(s.stored_odd, 16 * (BANDS // FU // 2))

        @block.gpsimd
        def _(pool):
            nc.gpsimd.memset(zero[:, :], 0.0).then_inc(s.zeroed, 1)
            nc.gpsimd.memset(woff_sb[:, :, :], 0.0).then_inc(s.zeroed, 1)
            nc.gpsimd.memset(xnT[:, :, :], 0.0).then_inc(s.zeroed, 1)
            nc.gpsimd.memset(eps_c[:, :], LN_C_EPS).then_inc(s.zeroed, 1)
            nc.gpsimd.memset(eps_t[:, :], LN_T_EPS).then_inc(s.zeroed, 1)
            nc.gpsimd.memset(ones[:, :], 1.0).then_inc(s.zeroed, 1)
            nc.gpsimd.memset(mask[:, :, :, :], 1.0).then_inc(s.zeroed, 1)
            nc.gpsimd.memset(hat3[:, :, TAPS, :], 0.0).then_inc(s.zeroed, 1)

            pool.wait_ge(s.consts_loaded, 16 * N_CONSTS)
            nc.gpsimd.tensor_copy(spread_sb[:, :, :], spread_f[:, :, :]).then_inc(s.tables_ready, 1)
            nc.gpsimd.tensor_copy(identb_sb[:, :], ident_sb[:, :]).then_inc(s.tables_ready, 1)

            def distances(b, par):
                o = offs[:, b, 0:2 * TAPS].rearrange("p (yx k one) -> p k yx one", yx=2, one=1)
                d = dist[:, par, :].rearrange("p (k yx j) -> p k yx j", k=TAPS, yx=2)
                r = rel_sb[:, :].rearrange("p (k yx j) -> p k yx j", k=TAPS, yx=2)
                nc.gpsimd.tensor_tensor(d, o.broadcast_to([P, TAPS, 2, WIN]), r, ALU.add
                                        ).then_inc(s.dist_ready, 1)

            def split(b, par):
                h3 = hat3[:, par, 0:TAPS, :].rearrange("p k (part h) -> p part k h", part=PARTS)
                h = hat[:, par, :].rearrange("p (k h) -> p k h", k=TAPS)
                r = rest[:, par, :].rearrange("p (k h) -> p k h", k=TAPS)
                pool.wait_ge(s.hi_ready, b + 1)
                nc.gpsimd.tensor_tensor(r, h, h3[:, 0], ALU.subtract).then_inc(s.pool_step, 1)
                nc.gpsimd.tensor_tensor(h3[:, 1], h, h3[:, 0], ALU.subtract).then_inc(s.pool_step, 1)
                pool.wait_ge(s.pool_step, b * 2 + 2)
                nc.gpsimd.tensor_tensor(h3[:, 2], r, h3[:, 1], ALU.subtract).then_inc(s.hat3_ready, 1)

            def keep_tokens(b, par):
                pool.wait_ge(s.xn2T_ready, b + 1)
                settle(pool)
                nc.gpsimd.tensor_copy(tT[:, b, :], xn2T[:, par, :]).then_inc(s.tT_ready, 1)

            flag = is_far(pool)
            with pool.If(flag):
                with pool.Fori(0, BANDS) as b:
                    pool.wait_ge(s.idx_ready, b + 1)
                    settle(pool)
                    for c4 in range(4):
                        for k in range(TAPS):
                            nc.gpsimd.indirect_dma_start(
                                corner[:, c4, k, :], None, xpad.rearrange("m r w c -> (m r w) c"),
                                bass.IndirectOffsetOnAxis(idx[:, c4, k:k + 1], 0)).then_inc(s.gathered, 16)
                    keep_tokens(b, 0)
            with pool.Else():
                distances(0, 0)
                distances(1, 1)
                for b in range(2):
                    split(b, b)
                distances(2, 0)
                def step(b, par):
                    if not isinstance(b, int) or b + 2 < BANDS:
                        split(b + 2, par)
                    if not isinstance(b, int) or b + 3 < BANDS:
                        distances(b + 3, 1 - par)
                    if not isinstance(b, int) or b >= 2:
                        keep_tokens(b - 2, par)

                for b in range(HEAD):
                    step(b, b % 2)
                with pool.Fori(0, PAIRS_OF_BANDS) as i:
                    step(i * 2 + HEAD, 1)
                    step(i * 2 + HEAD + 1, 0)
                for b in range(TAIL, BANDS):
                    step(b, b % 2)
                keep_tokens(BANDS - 2, 0)
                keep_tokens(BANDS - 1, 1)

        @block.scalar
        def _(act):
            def load(dst, src):
                act.dma_start(dst, src).then_inc(s.consts_loaded, 16)

            load(ident_sb[:, :], ident)
            act.wait_ge(s.zeroed, 2)
            load(woff_sb[:, :, 0:OFFS], w_offset.rearrange("a b c o -> c (a b) o"))
            load(boff_sb[:, :], b_offset.rearrange("(one o) -> one o", one=1).broadcast_to([P, OFFS]))
            load(fold_sb[:, :], fold)
            load(rel_sb[:, :], rel)
            load(spread_f[:, :, :], spread.rearrange("r (f q) -> r f q", f=4))
            load(rank_sb[:, :], rank)
            load(filt_sb[:, :, :], filt)
            load(gw_sb[:, :], gate_w)
            load(gb_sb[:, :], gate_b.rearrange("(one o) -> one o", one=1).broadcast_to([P, EXPERTS]))
            load(w1_sb[:, :, :], w1.rearrange("e c h -> c e h"))
            load(b1_sb[:, :], b1)
            load(w2_sb[:, :, :, :], w2)
            load(b2_sb[:, :], b2)

            def std_image(m):
                act.wait_ge(s.stats8, m * BPI + BPI)
                nc.scalar.activation(sd8[:, :], mv8[:, :, 1], ACT.Sqrt, bias=eps_c[:, :]).then_inc(s.std8, 1)

            def evacuate_xnT(m):
                for h in range(2):
                    act.wait_ge(s.xnT_psum, m * 2 + h + 1)
                    nc.scalar.activation(xnT[:, 1 + 16 * h:17 + 16 * h, 1:1 + SIDE], image_view(bank[h][:, :]),
                                         ACT.Copy).then_inc(s.xnT_ready, 1)

            def evacuate_conv(m):
                for h in range(2):
                    act.wait_ge(s.conv_psum, m * 2 + h + 1)
                    for b in range(4):
                        nc.scalar.activation(
                            conv_sb[:, h, b * P:(b + 1) * P].rearrange("g (t dy dx) -> g t dy dx", t=TILES, dy=TILE),
                            bank[2 + h][:, b * P:(b + 1) * P].rearrange("g (dy t dx) -> g t dy dx", dy=TILE, t=TILES),
                            ACT.Copy).then_inc(s.conv_ready, 1)

            act.wait_ge(s.zeroed, N_CLEARED)
            std_image(0)
            with act.Fori(0, IMAGES - 1) as m:
                evacuate_xnT(m)
                std_image(m + 1)
                evacuate_conv(m)
            evacuate_xnT(IMAGES - 1)
            evacuate_conv(IMAGES - 1)
            act.wait_ge(s.offs_ready, IMAGES)
            nc.scalar.activation(mask[:, :, :, 1], offs[:, :, 2 * TAPS:], ACT.Sigmoid).then_inc(s.mask_ready, 1)

            def hi_part(b, par):
                act.wait_ge(s.hat_ready, b + 1)
                nc.scalar.activation(hat3[:, par, 0:TAPS, 0:HATS],
                                     hat[:, par, :].rearrange("p (k h) -> p k h", k=TAPS),
                                     ACT.Copy).then_inc(s.hi_ready, 1)

            def evacuate_hatT(b):
                act.wait_ge(s.hatT_psum, b + 1)
                nc.scalar.activation(hatT[:, :, :],
                                     bank4b[0:2 * SLOT, 0:PAIRS * P].rearrange("r (i t) -> r i t", i=PAIRS),
                                     ACT.Copy).then_inc(s.hatT_ready, 1)

            def copy_y(b, par):
                for u, n in enumerate(UNITS):
                    act.wait_ge(s.y_psum, b * 3 + u + 1)
                    at_least(act, s.S_ready, b * 3 + u - 1)
                    slot = (par + u) % 2
                    nc.scalar.activation(ysp[:, slot, 0:n], bank[slot][0:Q, 0:n], ACT.Copy).then_inc(s.y_ready, 1)

            def sample_view(par, g):
                t0 = sum(GROUPS[:g])
                return samp[:, par, :, :].rearrange("c k (t p) -> c t k p", t=TILES)[:, t0:t0 + GROUPS[g]]

            def evacuate_samples(b, par):
                at_least(act, s.e_psum, b - 1)
                for g in range(2):
                    act.wait_ge(s.samp_psum, b * 3 + g + 1)
                    nc.scalar.activation(
                        sample_view(par, g),
                        bank[5 + (par + g) % 2][:, 0:GROUPS[g] * TAPS * TT].rearrange(
                            "c (t k p) -> c t k p", k=TAPS, p=TT), ACT.Copy).then_inc(s.samp_act, 1)

            def std_band(b, par):
                act.wait_ge(s.mean1_ready, b + 1)
                nc.scalar.activation(sd1[:, par:par + 1], mv1[:, par, 1:2], ACT.Sqrt,
                                     bias=eps_t[:, :]).then_inc(s.std1_ready, 1)

            def evacuate_tokens(b, par, ring=True):
                act.wait_ge(s.t_psum, b + 1)
                lag = 1 if ring else 0
                at_least(act, s.l_psum, b - lag)
                at_least(act, s.tT_ready, b - lag)
                nc.scalar.activation(xn2T[:, par, :], bank[4][:, 0:P], ACT.Copy).then_inc(s.xn2T_ready, 1)

            flag = is_far(act)
            with act.If(flag):
                with act.Fori(0, BANDS) as b:
                    for k in range(TAPS):
                        act.wait_ge(s.g_psum, b * TAPS + k + 1)
                        nc.scalar.activation(samp[:, 0, k, :], bank[k % 2][:, 0:P], ACT.Copy
                                             ).then_inc(s.samp_slow, 1)
                    std_band(b, 0)
                    evacuate_tokens(b, 0, ring=False)
            with act.Else():
                hi_part(0, 0)
                hi_part(1, 1)
                evacuate_hatT(0)

                def step(b, par):
                    known = isinstance(b, int)
                    copy_y(b, par)
                    if not known or b >= 2:
                        evacuate_tokens(b - 2, par)
                    if not known or b + 2 < BANDS:
                        hi_part(b + 2, par)
                    if not known or b >= 1:
                        std_band(b - 1, 1 - par)
                    evacuate_samples(b, par)
                    if not known or b + 1 < BANDS:
                        evacuate_hatT(b + 1)

                for b in range(HEAD):
                    step(b, b % 2)
                with act.Fori(0, PAIRS_OF_BANDS) as i:
                    step(i * 2 + HEAD, 1)
                    step(i * 2 + HEAD + 1, 0)
                for b in range(TAIL, BANDS):
                    step(b, b % 2)
                evacuate_tokens(BANDS - 2, 0)
                std_band(BANDS - 1, 1)
                evacuate_tokens(BANDS - 1, 1)

            act.wait_ge(s.exp_in, 1)
            nc.scalar.activation(R[:, 1, :], R[:, 1, :], ACT.Exp).then_inc(s.exp_out, 1)

            with act.Fori(0, BANDS // FU) as u:
                act.wait_ge(s.wT_psum, u + 1)
                nc.scalar.activation(wT[:, :, :], bank[4][0:EXPERTS, :].rearrange("e (b p) -> e b p", b=FU),
                                     ACT.Copy).then_inc(s.wT_ready, 1)
                for e in range(EXPERTS):
                    for h in range(HALVES):
                        n = e * HALVES + h
                        act.wait_ge(s.h_psum, u * (EXPERTS * HALVES) + n + 1)
                        if e >= 2:
                            act.wait_ge(s.y2_psum, u * EXPERTS + e - 1)
                        nc.scalar.activation(hid[:, n % 4, :], bank[n % 2][:, :], ACT.Gelu,
                                             bias=b1_sb[:, n:n + 1]).then_inc(s.h_ready, 1)

        @block.vector
        def _(dve):
            def stats_image(m):
                dve.wait_ge(s.x_loaded, m * 16 + 16)
                settle(dve)
                for b in range(BPI):
                    last = nc.vector.bn_stats(st8[:, b, :], x_nat[:, m * BPI + b, :])
                last.then_inc(s.dve_stat8, 1)
                dve.wait_ge(s.dve_stat8, m + 1)
                settle(dve)
                for b in range(BPI):
                    nc.vector.bn_aggr(mv8[:, b, :], st8[:, b, :]).then_inc(s.stats8, 1)

            def normalise_image(m):
                dve.wait_ge(s.std8, m + 1)
                nc.vector.reciprocal(rs8[:, :], sd8[:, :]).then_inc(s.rstd8, 1)
                dve.wait_ge(s.rstd8, m + 1)
                at_least(dve, s.xnT_psum, m * 2)
                at_least(dve, s.xn_stored, m * (16 * BPI))
                for b in range(BPI):
                    last = nc.vector.tensor_scalar(xn8[:, b, :], x_nat[:, m * BPI + b, :], mv8[:, b, 0:1],
                                                   rs8[:, b:b + 1], ALU.subtract, ALU.mult)
                last.then_inc(s.xn8_ready, 1)

            def offsets_image(m):
                dve.wait_ge(s.fold_psum, m + 1)
                nc.vector.tensor_tensor(
                    offs[:, bass.ds(m * BPI, BPI), :], bank[5][:, 0:BPI * OFFS].rearrange("p (b o) -> p b o", o=OFFS),
                    boff_sb[:, :].unsqueeze(1).broadcast_to([P, BPI, OFFS]), ALU.add).then_inc(s.offs_ready, 1)

            dve.wait_ge(s.consts_loaded, 16 * N_CONSTS)
            stats_image(0)
            normalise_image(0)
            with dve.Fori(1, IMAGES) as m:
                stats_image(m)
                normalise_image(m)
                offsets_image(m - 1)
            offsets_image(IMAGES - 1)

            dve.wait_ge(s.offs_ready, IMAGES)
            nc.vector.tensor_tensor(near[:, :].rearrange("p (b o) -> p b o", b=BANDS), offs[:, :, 0:2 * TAPS],
                                    offs[:, :, 0:2 * TAPS], ALU.mult).then_inc(s.near_ready, 1)
            dve.wait_ge(s.near_ready, 1)
            nc.vector.tensor_scalar(near[:, :], near[:, :], float(REACH * REACH), None, ALU.is_le
                                    ).then_inc(s.near_ready, 1)
            dve.wait_ge(s.near_ready, 2)
            nc.vector.tensor_reduce(near_n[:, :], near[:, :], AX_X, ALU.add).then_inc(s.near_ready, 1)
            dve.wait_ge(s.near_psum, 1)
            nc.vector.tensor_scalar(far[:, :], bank[6][0:1, 0:1], float(P * BANDS * 2 * TAPS), None,
                                    ALU.is_lt).then_inc(s.far_ready, 1)

            def hats(b, par):
                dve.wait_ge(s.dist_ready, b + 1)
                nc.vector.scalar_tensor_tensor(tent[:, par, :], dist[:, par, :], -1.0, dist[:, par, :],
                                               ALU.mult, ALU.max).then_inc(s.dve_hat, 1)
                dve.wait_ge(s.dve_hat, b * 2 + 1)
                nc.vector.tensor_scalar(tent[:, par, :], tent[:, par, :], -1.0, 0.0, ALU.add, ALU.min
                                        ).then_inc(s.dve_hat, 1)
                dve.wait_ge(s.dve_hat, b * 2 + 2)
                nc.vector.tensor_tensor(
                    hat[:, par, :].rearrange("p (k j) -> p k j", j=WIN),
                    tent[:, par, :].rearrange("p (k j) -> p k j", j=WIN),
                    mask[:, b, :, :].rearrange("p k yx -> p (k yx)").unsqueeze(2).broadcast_to([P, 2 * TAPS, WIN]),
                    ALU.mult).then_inc(s.hat_ready, 1)

            def multiply(b, par):
                at_least(dve, s.samp_psum, (b - 1) * 3)
                c0 = 0
                for u, n in enumerate(UNITS):
                    dve.wait_ge(s.y_ready, b * 3 + u + 1)
                    dve.wait_ge(s.x_psum, b * 3 + u + 1)
                    slot = (par + u) % 2
                    nc.vector.tensor_tensor(S[:, par, c0:c0 + n], ysp[:, slot, 0:n], bank[2 + slot][0:Q, 0:n],
                                            ALU.mult).then_inc(s.S_ready, 1)
                    c0 += n

            def samples(b, par):
                at_least(dve, s.e_psum, b - 1)
                dve.wait_ge(s.samp_psum, b * 3 + 3)
                t0 = sum(GROUPS[:2])
                nc.vector.tensor_copy(
                    samp[:, par, :, :].rearrange("c k (t p) -> c t k p", t=TILES)[:, t0:],
                    bank[5 + par][:, 0:GROUPS[2] * TAPS * TT].rearrange("c (t k p) -> c t k p", k=TAPS, p=TT)
                ).then_inc(s.samp_dve, 1)

            def residual(b, par):
                dve.wait_ge(s.e_psum, b + 1)
                nc.vector.tensor_tensor(x1[:, b, :], x1[:, b, :], bank[7][:, 0:C], ALU.add).then_inc(s.x1_ready, 1)
                dve.wait_ge(s.x1_ready, b + 1)
                settle(dve)
                nc.vector.bn_stats(st1[:, par, :], x1[:, b, :]).then_inc(s.dve_stat, 1)
                dve.wait_ge(s.dve_stat, b + 1)
                settle(dve)
                nc.vector.bn_aggr(mv1[:, par, :], st1[:, par, :]).then_inc(s.mean1_ready, 1)

            def normalise(b, par, ring=True):
                dve.wait_ge(s.std1_ready, b + 1)
                nc.vector.reciprocal(rs1[:, par:par + 1], sd1[:, par:par + 1]).then_inc(s.dve_rstd, 1)
                dve.wait_ge(s.dve_rstd, b + 1)
                if ring:
                    at_least(dve, s.t_psum, b - 1)
                nc.vector.tensor_scalar(xn2[:, par, :], x1[:, b, :], mv1[:, par, 0:1], rs1[:, par:par + 1],
                                        ALU.subtract, ALU.mult).then_inc(s.xn2_ready, 1)

            def keep_logits(b):
                dve.wait_ge(s.l_psum, b + 1)
                nc.vector.tensor_tensor(logits[:, b, :], bank[4][:, 0:EXPERTS], gb_sb[:, :], ALU.add
                                        ).then_inc(s.logit_ready, 1)

            dve.wait_ge(s.mask_ready, 1)
            dve.wait_ge(s.x1_loaded, 16)
            flag = is_far(dve)
            with dve.If(flag):
                with dve.Fori(0, BANDS) as b:
                    n = [0]

                    def link(ins, total=SLOW_LINKS):
                        ins.then_inc(s.dve_slow, 1)
                        n[0] += 1
                        dve.wait_ge(s.dve_slow, b * total + n[0])

                    dve.wait_ge(s.base_loaded, b * 16 + 16)
                    link(nc.vector.tensor_tensor(pos[:, :], offs[:, b, 0:2 * TAPS], base_sb[:, 0:2 * TAPS], ALU.add))
                    link(nc.vector.tensor_scalar(pos[:, :], pos[:, :], 1.0, float(PADDED - 2), ALU.max, ALU.min))
                    link(nc.vector.tensor_copy(posi[:, :], pos[:, :]))
                    link(nc.vector.tensor_copy(posf[:, :], posi[:, :]))
                    link(nc.vector.tensor_tensor(over[:, :], posf[:, :], pos[:, :], ALU.is_gt))
                    link(nc.vector.tensor_tensor(low[:, :], posf[:, :], over[:, :], ALU.subtract))
                    fr1 = frac[:, :, 1, :]
                    link(nc.vector.tensor_tensor(fr1, pos[:, :].rearrange("p (a k) -> p a k", a=2),
                                                 low[:, :].rearrange("p (a k) -> p a k", a=2), ALU.subtract))
                    link(nc.vector.tensor_scalar(frac[:, :, 0, :], fr1, -1.0, 1.0, ALU.mult, ALU.add))
                    link(nc.vector.scalar_tensor_tensor(line[:, :], low[:, 0:TAPS], float(PADDED),
                                                        low[:, TAPS:2 * TAPS], ALU.mult, ALU.add))
                    for c4 in range(4):
                        link(nc.vector.tensor_scalar(cell[:, c4, :], line[:, :], base_sb[:, 2 * TAPS:2 * TAPS + 1],
                                                     float((c4 // 2) * PADDED + c4 % 2), ALU.add, ALU.add))
                    nc.vector.tensor_copy(idx[:, :, :], cell[:, :, :]).then_inc(s.idx_ready, 1)
                    for a in range(2):
                        link(nc.vector.tensor_tensor(wx[:, a, :], frac[:, 1, a, :], mask[:, b, :, 1], ALU.mult))
                    for c4 in range(4):
                        link(nc.vector.tensor_tensor(cw[:, c4, :], frac[:, 0, c4 // 2, :], wx[:, c4 % 2, :], ALU.mult))
                    dve.wait_ge(s.gathered, b * (16 * 4 * TAPS) + 16 * 4 * TAPS)
                    for k in range(TAPS):
                        link(nc.vector.tensor_scalar(gsum[:, k, :], corner[:, 0, k, :], cw[:, 0, k:k + 1], None,
                                                     ALU.mult))
                    for c4 in range(1, 4):
                        for k in range(TAPS):
                            link(nc.vector.scalar_tensor_tensor(gsum[:, k, :], corner[:, c4, k, :],
                                                                cw[:, c4, k:k + 1], gsum[:, k, :],
                                                                ALU.mult, ALU.add))
                    assert n[0] == SLOW_LINKS
                    nc.vector.tensor_copy(over[:, 0:1], gsum[:, 0, 0:1]).then_inc(s.gsum_ready, 1)
                    residual(b, 0)
                    normalise(b, 0, ring=False)
                    keep_logits(b)
            with dve.Else():
                hats(0, 0)
                hats(1, 1)

                def step(b, par):
                    known = isinstance(b, int)
                    multiply(b, par)
                    if not known or b + 2 < BANDS:
                        hats(b + 2, par)
                    if not known or b >= 1:
                        residual(b - 1, 1 - par)
                    if not known or b >= 2:
                        keep_logits(b - 2)
                    if not known or b >= 1:
                        normalise(b - 1, 1 - par)
                    samples(b, par)

                for b in range(HEAD):
                    step(b, b % 2)
                with dve.Fori(0, PAIRS_OF_BANDS) as i:
                    step(i * 2 + HEAD, 1)
                    step(i * 2 + HEAD + 1, 0)
                for b in range(TAIL, BANDS):
                    step(b, b % 2)
                keep_logits(BANDS - 2)
                residual(BANDS - 1, 1)
                normalise(BANDS - 1, 1)
                keep_logits(BANDS - 1)

            m = [0]

            def then(ins):
                ins.then_inc(s.dve_route, 1)
                m[0] += 1
                dve.wait_ge(s.dve_route, m[0])

            def R3(j):
                return R[:, j, :].rearrange("p (b e) -> p b e", e=EXPERTS)

            def over_e(ap):
                return ap.unsqueeze(2).broadcast_to([P, BANDS, EXPERTS])

            rank3 = rank_sb[:, :].unsqueeze(1).broadcast_to([P, BANDS, EXPERTS])
            dve.wait_ge(s.logit_ready, BANDS)
            then(nc.vector.tensor_reduce(r1[:, 0, :], logits[:, :, :], AX_X, ALU.max))
            nc.vector.tensor_tensor(R3(1), logits[:, :, :], over_e(r1[:, 0, :]), ALU.subtract).then_inc(s.exp_in, 1)
            dve.wait_ge(s.exp_out, 1)
            then(nc.vector.tensor_reduce(r1[:, 1, :], R3(1), AX_X, ALU.add))
            then(nc.vector.reciprocal(r1[:, 2, :], r1[:, 1, :]))
            then(nc.vector.tensor_tensor(R3(2), R3(1), over_e(r1[:, 2, :]), ALU.mult))
            then(nc.vector.tensor_reduce(r1[:, 3, :], R3(2), AX_X, ALU.max))
            then(nc.vector.tensor_tensor(R3(3), R3(2), over_e(r1[:, 3, :]), ALU.is_ge))
            then(nc.vector.tensor_tensor(R3(3), R3(3), rank3, ALU.mult))
            then(nc.vector.tensor_reduce(r1[:, 4, :], R3(3), AX_X, ALU.max))
            then(nc.vector.tensor_tensor(R3(4), R3(3), over_e(r1[:, 4, :]), ALU.is_equal))
            then(nc.vector.scalar_tensor_tensor(R[:, 5, :], R[:, 4, :], -2.0, R[:, 2, :], ALU.mult, ALU.add))
            then(nc.vector.tensor_reduce(r1[:, 3, :], R3(5), AX_X, ALU.max))
            then(nc.vector.tensor_tensor(R3(3), R3(5), over_e(r1[:, 3, :]), ALU.is_ge))
            then(nc.vector.tensor_tensor(R3(3), R3(3), rank3, ALU.mult))
            then(nc.vector.tensor_reduce(r1[:, 4, :], R3(3), AX_X, ALU.max))
            then(nc.vector.tensor_tensor(R3(6), R3(3), over_e(r1[:, 4, :]), ALU.is_equal))
            then(nc.vector.tensor_tensor(R[:, 7, :], R[:, 4, :], R[:, 6, :], ALU.add))
            nc.vector.tensor_tensor(wts[:, :, :].rearrange("p b e -> p (b e)"), R[:, 7, :], R[:, 2, :], ALU.mult
                                    ).then_inc(s.wts_ready, 1)
            dve.wait_ge(s.wts_ready, 1)

            with dve.Fori(0, BANDS // FU // 2) as i:
                for par in range(2):
                    u = i * 2 + par
                    dve.wait_ge(s.wT_psum, u)
                    dve.wait_ge(s.dve_acc, u * (EXPERTS + 1))
                    nc.vector.tensor_copy(wcol[:, :, :], wts[:, bass.ds(u * FU, FU), :]).then_inc(s.wcol_ready, 1)
                    dve.wait_ge((s.stored, s.stored_odd)[par], i * 16)
                    dve.wait_ge(s.b_psum, u + 1)
                    nc.vector.tensor_tensor(acc[:, par, :, :], x1[:, bass.ds(u * FU, FU), :],
                                            bank[5][:, :].rearrange("p (b c) -> p b c", b=FU), ALU.add
                                            ).then_inc(s.dve_acc, 1)
                    for e in range(EXPERTS):
                        dve.wait_ge(s.y2_psum, u * EXPERTS + e + 1)
                        dve.wait_ge(s.dve_acc, u * (EXPERTS + 1) + e + 1)
                        for j in range(FU):
                            last = nc.vector.scalar_tensor_tensor(
                                acc[:, par, j, :], bank[2 + e % 2][:, j * C:(j + 1) * C], wcol[:, j, e:e + 1],
                                acc[:, par, j, :], ALU.mult, ALU.add)
                        last.then_inc(s.dve_acc, 1)

        @block.tensor
        def _(pe):
            pe.wait_ge(s.consts_loaded, 16 * N_CONSTS)
            pe.wait_ge(s.zeroed, N_CLEARED)
            with pe.Fori(0, IMAGES) as m:
                pe.wait_ge(s.xn8_ready, m + 1)
                for b in range(BPI):
                    last = nc.tensor.transpose(bank[b // 4][:, (b % 4) * P:(b % 4 + 1) * P], xn8[:, b, :], ident_sb[:, :])
                    if b % 4 == 3:
                        last.then_inc(s.xnT_psum, 1)
                pe.wait_ge(s.xnT_ready, m * 2 + 2)
                for h in range(2):
                    for k in range(TAPS):
                        g = k % 4
                        last = nc.tensor.matmul(
                            bank[2 + h][32 * g:32 * g + 32, :], woff_sb[:, k, :],
                            xnT[:, 16 * h + k // 3:16 * h + k // 3 + 16, k % 3:k % 3 + SIDE],
                            start=(k < 4), stop=(k + 4 >= TAPS))
                    last.then_inc(s.conv_psum, 1)
                at_least(pe, s.offs_ready, m)
                for h in range(2):
                    pe.wait_ge(s.conv_ready, m * 8 + h * 4 + 4)
                    for b in range(4):
                        c0 = (4 * h + b) * OFFS
                        last = nc.tensor.matmul(bank[5][:, c0:c0 + OFFS], conv_sb[:, h, b * P:(b + 1) * P], fold_sb[:, :], start=True, stop=True)
                last.then_inc(s.fold_psum, 1)
            pe.wait_ge(s.near_ready, 3)
            nc.tensor.matmul(bank[6][0:1, 0:1], near_n[:, :], ones[:, :], start=True, stop=True
                             ).then_inc(s.near_psum, 1)

            def transpose_hats(b, par):
                pe.wait_ge(s.hat3_ready, b + 1)
                at_least(pe, s.logit_ready, b - 2)
                for i in range(PAIRS):
                    last = nc.tensor.transpose(bank4b[0:2 * SLOT, i * P:(i + 1) * P],
                                               hat3[:, par, 2 * i:2 * i + 2, :].rearrange("p k r -> p (k r)"),
                                               identb_sb[:, :])
                last.then_inc(s.hatT_psum, 1)

            def spread_hats(b, par):
                pe.wait_ge(s.hatT_ready, b + 1)
                for u, n in enumerate(UNITS):
                    slot = (par + u) % 2
                    moving = hatT[:, 4, :] if u == 2 else hatT[:, 0:4, :].rearrange("r i t -> r (i t)")
                    odd = u % 2
                    at_least(pe, s.y_ready, b * 3 + u - 1)
                    nc.tensor.matmul(bank[slot][0:Q, 0:n], spread_sb[:, 2 * odd, :], moving,
                                     start=True, stop=True).then_inc(s.y_psum, 1)
                    at_least(pe, s.S_ready, b * 3 + u - 1)
                    nc.tensor.matmul(bank[2 + slot][0:Q, 0:n], spread_sb[:, 2 * odd + 1, :], moving,
                                     start=True, stop=True).then_inc(s.x_psum, 1)

            ORDER = [0, 2, 4, 6, 1, 3, 5, 7, 8]

            def sample(b, par, loads):
                pe.wait_ge(s.S_ready, b * 3 + 3)
                pe.wait_ge((s.win_even, s.win_odd)[par], loads * (16 * TILES))
                t = 0
                weights = S[:, par, :].rearrange("q (k t p) -> q t k p", k=TAPS, t=TILES)
                for g, n in enumerate(GROUPS):
                    if g == 0:
                        at_least(pe, s.samp_act, b * 2)
                    elif g == 1:
                        at_least(pe, s.samp_dve, b)
                    else:
                        pe.wait_ge(s.samp_act, b * 2 + 1)
                    for i in range(n):
                        last = nc.tensor.matmul(bank[5 + (par + g) % 2][:, i * TAPS * TT:(i + 1) * TAPS * TT],
                                                xwin[:, par, t, :], weights[:, t], start=True, stop=True)
                        t += 1
                    last.then_inc(s.samp_psum, 1)

            def project(b, par, fast=True):
                if fast:
                    pe.wait_ge(s.samp_act, b * 2 + 2)
                    pe.wait_ge(s.samp_dve, b + 1)
                else:
                    pe.wait_ge(s.samp_slow, (b + 1) * TAPS)
                at_least(pe, s.x1_ready, b)
                for j in range(TAPS):
                    k = ORDER[j] if fast else j
                    last = nc.tensor.matmul(bank[7][:, 0:C], samp[:, par, j, :], filt_sb[:, k, :],
                                            start=(j == 0), stop=(j == TAPS - 1))
                last.then_inc(s.e_psum, 1)

            def transpose_tokens(b, par):
                pe.wait_ge(s.xn2_ready, b + 1)
                nc.tensor.transpose(bank[4][:, 0:P], xn2[:, par, :], ident_sb[:, :]).then_inc(s.t_psum, 1)

            def gate(b, par):
                pe.wait_ge(s.xn2T_ready, b + 1)
                nc.tensor.matmul(bank[4][:, 0:EXPERTS], xn2T[:, par, :], gw_sb[:, :],
                                 start=True, stop=True).then_inc(s.l_psum, 1)

            flag = is_far(pe)
            with pe.If(flag):
                with pe.Fori(0, BANDS) as b:
                    pe.wait_ge(s.gsum_ready, b + 1)
                    for k in range(TAPS):
                        if k >= 2:
                            pe.wait_ge(s.samp_slow, b * TAPS + k - 1)
                        nc.tensor.transpose(bank[k % 2][:, 0:P], gsum[:, k, :], ident_sb[:, :]
                                            ).then_inc(s.g_psum, 1)
                    project(b, 0, fast=False)
                    transpose_tokens(b, 0)
                    gate(b, 0)
            with pe.Else():
                pe.wait_ge(s.tables_ready, 2)
                transpose_hats(0, 0)

                def step(b, par, loads):
                    known = isinstance(b, int)
                    spread_hats(b, par)
                    if not known or b >= 2:
                        transpose_tokens(b - 2, par)
                    if not known or b >= 1:
                        project(b - 1, 1 - par)
                    if not known or b >= 2:
                        gate(b - 2, par)
                    sample(b, par, loads)
                    if not known or b + 1 < BANDS:
                        transpose_hats(b + 1, 1 - par)

                for b in range(HEAD):
                    step(b, b % 2, b // 2 + 1)
                with pe.Fori(0, PAIRS_OF_BANDS) as i:
                    step(i * 2 + HEAD, 1, i + 2)
                    step(i * 2 + HEAD + 1, 0, i + 3)
                for b in range(TAIL, BANDS):
                    step(b, b % 2, b // 2 + 1)
                transpose_tokens(BANDS - 2, 0)
                project(BANDS - 1, 1)
                gate(BANDS - 2, 0)
                pe.wait_ge(s.logit_ready, BANDS - 1)
                transpose_tokens(BANDS - 1, 1)
                gate(BANDS - 1, 1)

            pe.wait_ge(s.tT_ready, BANDS)
            with pe.Fori(0, BANDS // FU) as u:
                pe.wait_ge(s.wcol_ready, u + 1)
                for j in range(FU):
                    last = nc.tensor.transpose(bank[4][0:EXPERTS, j * P:(j + 1) * P], wcol[:, j, :], ident_sb[:, :])
                last.then_inc(s.wT_psum, 1)
                pe.wait_ge(s.wT_ready, u + 1)
                for j in range(FU):
                    last = nc.tensor.matmul(bank[5][:, j * C:(j + 1) * C], wT[:, j, :], b2_sb[:, :],
                                            start=True, stop=True)
                last.then_inc(s.b_psum, 1)

                def up(e):
                    for h in range(HALVES):
                        n = e * HALVES + h
                        at_least(pe, s.h_ready, u * (EXPERTS * HALVES) + n - 1 if n >= 2 else u * (EXPERTS * HALVES))
                        nc.tensor.matmul(bank[n % 2][:, :], w1_sb[:, e, h * P:(h + 1) * P],
                                         tT[:, bass.ds(u * FU, FU), :].rearrange("c b p -> c (b p)"),
                                         start=True, stop=True).then_inc(s.h_psum, 1)

                def down(e):
                    pe.wait_ge(s.h_ready, u * (EXPERTS * HALVES) + 2 * e + 2)
                    if e >= 2:
                        pe.wait_ge(s.dve_acc, u * (EXPERTS + 1) + e)
                    for j in range(FU):
                        for h in range(HALVES):
                            last = nc.tensor.matmul(bank[2 + e % 2][:, j * C:(j + 1) * C],
                                                    hid[:, (2 * e + h) % 4, j * P:(j + 1) * P], w2_sb[:, e, h, :],
                                                    start=(h == 0), stop=(h == HALVES - 1))
                    last.then_inc(s.y2_psum, 1)

                up(0)
                for e in range(EXPERTS):
                    if e + 1 < EXPERTS:
                        up(e + 1)
                    down(e)


def kernel(x, L0_conv_w_offset, L0_conv_b_offset, L0_conv_filt, L0_ffn_gate_w, L0_ffn_gate_b,
           L0_ffn_W1, L0_ffn_b1, L0_ffn_W2, L0_ffn_b2):
    import numpy as np
    import concourse.bacc as bacc
    from concourse.bass_utils import run_bass_kernel_spmd

    x = np.asarray(x)
    rows = x.reshape(BANDS, P, C)
    tiles = x.reshape(BANDS, TILE, TILES, TILE, C).transpose(0, 2, 1, 3, 4).reshape(BANDS, P, C)
    arrays = {
        "x_rows": rows,
        "x_tiles": tiles,
        "w_offset": np.asarray(L0_conv_w_offset),
        "b_offset": np.asarray(L0_conv_b_offset),
        "filt": np.asarray(L0_conv_filt).reshape(C, C, TAPS).transpose(1, 2, 0),
        "gate_w": np.asarray(L0_ffn_gate_w),
        "gate_b": np.asarray(L0_ffn_gate_b),
        "w1": np.asarray(L0_ffn_W1),
        "b1": np.asarray(L0_ffn_b1).reshape(EXPERTS * HALVES, P).T,
        "w2": np.asarray(L0_ffn_W2).reshape(EXPERTS, HALVES, P, C).transpose(2, 0, 1, 3),
        "b2": np.asarray(L0_ffn_b2),
        **window_constants(),
    }
    arrays = {k: np.ascontiguousarray(v) for k, v in arrays.items()}
    nc = bacc.Bacc("TRN2", target_bir_lowering=False, num_devices=1)
    args = {k: nc.dram_tensor(f"in_{k}", v.shape, mybir.dt.from_np(v.dtype), kind="ExternalInput").ap()
            for k, v in arrays.items()}
    out = nc.dram_tensor("out_tiles", (BANDS, P, C), F32, kind="ExternalOutput").ap()
    program(nc, **args, out=out)
    result = run_bass_kernel_spmd(nc, [{f"in_{k}": v for k, v in arrays.items()}], core_ids=[0])
    got = result.results[0]["out_tiles"]
    return got.reshape(BANDS, TILES, TILE, TILE, C).transpose(0, 2, 1, 3, 4).reshape(IMAGES, SIDE, SIDE, C)
```

```python
from contextlib import ExitStack

import concourse.bass as bass
from concourse import mybir

F32 = mybir.dt.float32
BF16 = mybir.dt.bfloat16
I32 = mybir.dt.int32
U32 = mybir.dt.uint32
ALU = mybir.AluOpType
ACT = mybir.ActivationFunctionType
AX_X = mybir.AxisListType.X

P = 128
IMAGES, SIDE = 4, 32
C = 128
TAPS = 9
OFFS = 3 * TAPS
TILE = 4
TILES = SIDE // TILE
BANDS = IMAGES * SIDE // TILE
BPI = BANDS // IMAGES
REACH = 2
HALO = REACH + 1
WIN = TILE + 2 * HALO
Q = WIN * WIN
PADDED = SIDE + 2 * HALO
HATS = 2 * WIN
PARTS = 3
SLOT = PARTS * HATS
PAIRS = (TAPS + 1) // 2
TT = TILE * TILE
UNITS = [512, 512, 128]
GROUPS = [3, 3, 2]
EXPERTS, HID = 8, 256
HALVES = HID // P
BLOCK = 256
SUBS = BLOCK // P
REGION = P * BANDS + BLOCK
BLOCKS = (2 * P * BANDS + EXPERTS * (BLOCK - 1)) // BLOCK
ROW = C + 1
W_UP = HID + HALVES
WROW = W_UP + HALVES * C + C
RING = 3
GB = 4
T_RANK, T_REGION, T_THRESH = 0, EXPERTS, 2 * EXPERTS
T_TRI = T_THRESH + P * BANDS // BLOCK
T_BLK = T_TRI + EXPERTS * EXPERTS
T_BLKROW = T_BLK + BLOCKS
T_COLS = T_BLKROW + BLOCKS
LN_C_EPS, LN_T_EPS = 1e-6, 1e-5
N_CONSTS = 10
N_CLEARED = 10
SLOW_LINKS = 55


def window_constants():
    import numpy as np

    p = np.arange(P)
    dy, dx = (p % TT) // TILE, p % TILE
    tile = p // TT
    k = np.arange(TAPS)
    ky, kx = k // 3 - 1, k % 3 - 1
    j = np.arange(WIN)
    rel = np.zeros((P, TAPS, 2, WIN), np.float32)
    rel[:, :, 0, :] = (dy[:, None] + ky[None, :] + HALO)[:, :, None] - j
    rel[:, :, 1, :] = (dx[:, None] + kx[None, :] + HALO)[:, :, None] - j
    spread = np.zeros((2, PARTS, 2, WIN, 2, 2, Q), np.float32)
    q = np.arange(Q)
    for odd in range(2):
        for part in range(PARTS):
            spread[odd, part, 0, q // WIN, odd, 0, q] = 1
            spread[odd, part, 1, q % WIN, odd, 1, q] = 1
    spread = spread.reshape(2 * SLOT, 4 * Q)
    fold = np.zeros((4, 32, OFFS), np.float32)
    fold[:, np.arange(OFFS), np.arange(OFFS)] = 1
    base = np.zeros((BANDS, P, 2 * TAPS + 2), np.float32)
    for b in range(BANDS):
        base[b, :, 0:TAPS] = (TILE * (b % BPI) + dy)[:, None] + ky + HALO
        base[b, :, TAPS:2 * TAPS] = (TILE * tile + dx)[:, None] + kx + HALO
        base[b, :, 2 * TAPS:] = (b // BPI) * PADDED * PADDED
    e = np.arange(EXPERTS)
    table = np.concatenate([
        e, e * REGION, np.arange(P * BANDS // BLOCK) * BLOCK, np.tril(np.ones((EXPERTS, EXPERTS))).ravel(),
        np.arange(BLOCKS), np.arange(BLOCKS) * BLOCK]).astype(np.float32)
    token = np.arange(BANDS)[None, :, None] * P + p[:, None, None]
    dest = (token + np.arange(2) * (P * BANDS)).astype(np.int32)
    padding = np.zeros((P, SUBS, ROW), np.int32)
    padding[:, :, C] = 2 * P * BANDS + np.arange(SUBS) * P + p[:, None]
    return {
        "rel": rel.reshape(P, TAPS * HATS),
        "spread": spread,
        "fold": fold.reshape(P, OFFS),
        "base": base,
        "ident": np.eye(P, dtype=np.float32),
        "before": np.triu(np.ones((P, P), np.float32), 1),
        "table": np.broadcast_to(table, (P, T_COLS)).copy(),
        "dest": dest,
        "padding": padding,
    }


def program(nc, x_rows, x_tiles, w_offset, b_offset, filt, gate_w, gate_b, experts,
            rel, spread, fold, base, ident, before, table, dest, padding, out):
    with ExitStack() as ctx:
        def sb(name, shape, dt=F32):
            return ctx.enter_context(nc.sbuf_tensor(name, shape, dt))

        def sem(name):
            return ctx.enter_context(nc.semaphore(name))

        xpad = nc.dram_tensor("xpad", [IMAGES, PADDED, PADDED, C], F32, kind="Internal").ap()
        routed = nc.dram_tensor("routed", [EXPERTS * REGION + BLOCK, ROW], F32, kind="Internal").ap()
        result = nc.dram_tensor("result", [2 * P * BANDS + BLOCK, C], F32, kind="Internal").ap()

        rel_sb = sb("rel_sb", [P, TAPS * HATS])
        spread_f = sb("spread_f", [2 * SLOT, 4, Q])
        spread_sb = sb("spread_sb", [2 * SLOT, 4, Q], BF16)
        fold_sb = sb("fold_sb", [P, OFFS])
        ident_sb = sb("ident_sb", [P, P])
        identb_sb = sb("identb_sb", [P, P], BF16)
        before_f = sb("before_f", [P, P])
        before_sb = sb("before_sb", [P, P], BF16)
        every_sb = sb("every_sb", [P, P], BF16)
        table_sb = sb("table_sb", [P, T_COLS])
        dest_sb = sb("dest_sb", [P, BANDS, 2], I32)
        padding_sb = sb("padding_sb", [P, SUBS, ROW], I32)
        woff_sb = sb("woff_sb", [C, TAPS, 32])
        boff_sb = sb("boff_sb", [P, OFFS])
        filt_sb = sb("filt_sb", [C, TAPS, C])
        gw_sb = sb("gw_sb", [C, EXPERTS])
        gb_sb = sb("gb_sb", [P, EXPERTS])
        w_all = sb("w_all", [P, EXPERTS, WROW])
        eps_c = sb("eps_c", [P, 1])
        eps_t = sb("eps_t", [P, 1])
        ones = sb("ones", [P, 1])
        zero = sb("zero", [P, HALO * C])

        wide = sb("wide", [P, 4 * TAPS * C])
        x_nat = wide[:, 0:BANDS * C].rearrange("p (b c) -> p b c", c=C)
        x1 = sb("x1", [P, BANDS, C])
        xnT = sb("xnT", [C, SIDE + 2, SIDE + 2])
        offs = sb("offs", [P, BANDS, OFFS])
        mask = sb("mask", [P, BANDS, TAPS, 2])
        top_all = sb("top_all", [P, BANDS, EXPERTS])

        xn8 = sb("xn8", [P, BPI, C])
        st8 = sb("st8", [P, BPI, 6])
        mv8 = sb("mv8", [P, BPI, 2])
        sd8 = sb("sd8", [P, BPI])
        rs8 = sb("rs8", [P, BPI])
        conv_sb = sb("conv_sb", [P, 2, 512])
        near = sb("near", [P, BANDS * 2 * TAPS])
        near_n = sb("near_n", [P, 1])
        far = sb("far", [1, 1], I32)
        dist = sb("dist", [P, 2, TAPS * HATS])
        tent = sb("tent", [P, 2, TAPS * HATS])
        hat = sb("hat", [P, 2, TAPS * HATS])
        rest = sb("rest", [P, 2, TAPS * HATS])
        hat3 = sb("hat3", [P, 2, TAPS + 1, SLOT], BF16)
        hatT = sb("hatT", [2 * SLOT, PAIRS, P], BF16)
        ysp = sb("ysp", [Q, 2, 512])
        S = sb("S", [Q, 2, TAPS * P])
        xwin = sb("xwin", [Q, 2, TILES, C])
        samp = sb("samp", [C, 2, TAPS, P])
        st1 = sb("st1", [P, 2, 6])
        mv1 = sb("mv1", [P, 2, 2])
        sd1 = sb("sd1", [P, 2])
        rs1 = sb("rs1", [P, 2])
        xn2 = sb("xn2", [P, 2, C])
        xn2T = sb("xn2T", [C, 2, P])

        base_sb = sb("base_sb", [P, 2 * TAPS + 2])
        pos = sb("pos", [P, 2 * TAPS])
        posi = sb("posi", [P, 2 * TAPS], I32)
        posf = sb("posf", [P, 2 * TAPS])
        over = sb("over", [P, 2 * TAPS])
        low = sb("low", [P, 2 * TAPS])
        frac = sb("frac", [P, 2, 2, TAPS])
        line = sb("line", [P, TAPS])
        cell = sb("cell", [P, 4, TAPS])
        idx = sb("idx", [P, 4, TAPS], U32)
        wx = sb("wx", [P, 2, TAPS])
        cw = sb("cw", [P, 4, TAPS])
        corner = wide[:, :].rearrange("p (q k c) -> p q k c", q=4, k=TAPS)
        gsum = sb("gsum", [P, TAPS, C])

        lg = sb("lg", [P, 2, EXPERTS])
        top = sb("top", [P, 2, EXPERTS])
        topi = sb("topi", [P, 2, EXPERTS], U32)
        chosen = sb("chosen", [P, 2, 2, EXPERTS])
        both = sb("both", [P, 2, EXPERTS], BF16)
        seen = sb("seen", [P, 2, EXPERTS], BF16)
        place = sb("place", [P, EXPERTS])
        placed = sb("placed", [P, 2, EXPERTS])
        slot_f = sb("slot_f", [P, 2])
        slot = sb("slot", [P, 2, 2], U32)
        payload = sb("payload", [P, 2, 2, ROW])
        e_all = sb("e_all", [P, BANDS, EXPERTS])
        e_sum = sb("e_sum", [P, BANDS])
        share = sb("share", [P, 2, BANDS])
        count = sb("count", [1, EXPERTS])
        over_t = sb("over_t", [1, EXPERTS, P * BANDS // BLOCK])
        nblk = sb("nblk", [1, EXPERTS])
        tri_t = sb("tri_t", [1, EXPERTS, EXPERTS])
        upto = sb("upto", [1, EXPERTS])
        past = sb("past", [1, BLOCKS, EXPERTS])
        past_n = sb("past_n", [1, BLOCKS, EXPERTS])
        blk_e = sb("blk_e", [1, BLOCKS])
        blk_first = sb("blk_first", [1, BLOCKS])
        blk_row = sb("blk_row", [1, BLOCKS])
        blk_i = sb("blk_i", [1, BLOCKS, 2], I32)
        pad_row = sb("pad_row", [1, EXPERTS], I32)

        w_blk = sb("w_blk", [P, RING, W_UP])
        rows_in = sb("rows_in", [P, RING, SUBS, ROW])
        to_a = sb("to_a", [P, RING, SUBS], I32)
        to_b = sb("to_b", [P, RING, SUBS], I32)
        rowsT = sb("rowsT", [C, RING, BLOCK])
        hid = sb("hid", [P, RING, HALVES, BLOCK])
        y = sb("y", [P, RING, SUBS, C])
        y_back = sb("y_back", [P, 2, 2, GB, C])
        res = sb("res", [P, 2, GB, C])

        bank = [ctx.enter_context(nc.psum_tensor(f"bank{n}", [P, 512], F32)) for n in range(8)]
        bank4b = bank[4][:, :].bitcast(BF16)

        S_ = {}
        for name in (
            "settled tables_ready zeroed border_written x_loaded x1_loaded early_loaded consts_loaded "
            "fold_free stats8 std8 rstd8 xn8_ready xn_stored xnT_psum xnT_ready conv_psum conv_ready fold_psum "
            "offs_ready mask_ready near_ready near_psum far_ready dve_stat8 dve_hat dve_stat dve_rstd dve_slow "
            "pool_step dist_ready hat_ready hi_ready hat3_ready hatT_psum hatT_ready y_psum x_psum y_ready S_ready "
            "win_even win_odd samp_psum samp_act samp_dve e_psum x1_ready std1_ready mean1_ready xn2_ready "
            "t_psum xn2T_ready l_psum base_free base_loaded idx_ready gathered gsum_ready g_psum samp_slow "
            "route stashed place_psum place_ready placed_ready slot_f_ready slot_ready payload_ready scat_even scat_odd "
            "exp_in exp_out share_step count_psum plan_step plan_ready idle_written pads_written "
            "w_in_0 w_in_1 w_in_2 rows_in_0 rows_in_1 rows_in_2 rowsT_psum rowsT_ready h_psum h_ready y_psum2 y_ready2 to_ready y_done "
            "back_even back_odd sent_0 sent_1 sent_2 res_step stored_even stored_odd"
        ).split():
            S_[name] = sem(name)
        s = type("Sems", (), S_)

        block = ctx.enter_context(nc.Block())

        def image_view(bank_ap):
            return bank_ap.rearrange("c (r w) -> c r w", w=SIDE)

        HEAD = 4
        PAIRS_OF_BANDS = (BANDS - HEAD - 3) // 2
        TAIL = HEAD + 2 * PAIRS_OF_BANDS

        def settle(eng):
            eng.sem_inc(s.settled, 1)

        def block_at(turn, place):
            return turn * RING + place, place % RING, turn + place // RING

        TURNS = BLOCKS // RING
        assert BLOCKS % RING == 0

        def block_loop(eng, step):
            for place in range(RING):
                step(0, place)
            with eng.Fori(1, TURNS - 1) as turn:
                for place in range(RING):
                    step(turn, place)
            for place in range(RING):
                step(TURNS - 1, place)

        def previous(turn, place):
            return (turn - 1, RING - 1) if place == 0 else (turn, place - 1)

        def is_first(turn, place):
            return isinstance(turn, int) and turn * RING + place == 0

        def is_last(turn, place):
            return isinstance(turn, int) and turn * RING + place == BLOCKS - 1

        w_arrived = (s.w_in_0, s.w_in_1, s.w_in_2)
        rows_arrived = (s.rows_in_0, s.rows_in_1, s.rows_in_2)
        sent = (s.sent_0, s.sent_1, s.sent_2)

        def expert_of(eng, i):
            return eng.value_load(blk_i[0:1, i, 1:2], min_val=0, max_val=EXPERTS - 1)

        def is_far(eng):
            eng.wait_ge(s.far_ready, 1)
            return eng.value_load(far[0:1, 0:1], min_val=0, max_val=1)

        def at_least(eng, semaphore, value):
            if not isinstance(value, int) or value > 0:
                eng.wait_ge(semaphore, value)

        @block.sync
        def _(sp):
            for m in range(IMAGES):
                sp.dma_start(x_nat[:, m * BPI:(m + 1) * BPI, :],
                             x_rows[m * BPI:(m + 1) * BPI].rearrange("b p c -> p b c")).then_inc(s.x_loaded, 16)
                sp.wait_ge(s.x_loaded, 16 * (m + 1))
            sp.wait_ge(s.zeroed, 1)
            for m in range(IMAGES):
                for r0 in (0, HALO + SIDE):
                    sp.dma_start(xpad[m, r0:r0 + HALO, :, :], zero[0:HALO * PADDED, 0:C]).then_inc(s.border_written, 16)
                for c0 in (0, HALO + SIDE):
                    sp.dma_start(xpad[m, HALO:HALO + SIDE, c0:c0 + HALO, :],
                                 zero[0:SIDE, :]).then_inc(s.border_written, 16)
            with sp.Fori(0, IMAGES) as m:
                sp.wait_ge(s.xn8_ready, m + 1)
                for b in range(BPI):
                    sp.dma_start(xpad[m, HALO + TILE * b:HALO + TILE * (b + 1), HALO:HALO + SIDE, :],
                                 xn8[:, b, :]).then_inc(s.xn_stored, 16)
            sp.dma_start(x1[:, :, :], x_tiles.rearrange("b p c -> p b c")).then_inc(s.x1_loaded, 16)
            sp.wait_ge(s.border_written, 16 * 4 * IMAGES)
            sp.wait_ge(s.xn_stored, 16 * BANDS)

            sp.wait_ge(s.consts_loaded, 16 * N_CONSTS)
            sp.dma_start(routed[EXPERTS * REGION:, :].rearrange("(j p) w -> p j w", p=P),
                         padding_sb[:, :, :].bitcast(F32)).then_inc(s.idle_written, 16)

            def load_windows(b, par, image, row):
                at_least(sp, s.samp_psum, 3 * (b - 1))
                for t in range(TILES):
                    sp.dma_start(xwin[:, par, t, :], xpad[image, bass.ds(row, WIN), TILE * t:TILE * t + WIN, :]
                                 ).then_inc((s.win_even, s.win_odd)[par], 16)

            flag = is_far(sp)
            with sp.If(flag):
                with sp.Fori(0, BANDS) as b:
                    sp.wait_ge(s.base_free, b + 1)
                    sp.dma_start(base_sb[:, :], base[b]).then_inc(s.base_loaded, 16)
            with sp.Else():
                for b in range(BPI):
                    load_windows(b, b % 2, 0, TILE * b)
                with sp.Fori(1, IMAGES) as m:
                    for r in range(BPI):
                        load_windows(m * BPI + r, r % 2, m, TILE * r)

            sp.wait_ge(s.plan_ready, 1)
            for e in range(EXPERTS):
                row = sp.value_load(pad_row[0:1, e:e + 1], min_val=e * REGION, max_val=e * REGION + P * BANDS)
                sp.dma_start(routed[bass.ds(row, BLOCK), :].rearrange("(j p) w -> p j w", p=P),
                             padding_sb[:, :, :].bitcast(F32)).then_inc(s.pads_written, 16)

            def load_rows(turn, place):
                i, slot, uses = block_at(turn, place)
                row = sp.value_load(blk_i[0:1, i, 0:1], min_val=0, max_val=EXPERTS * REGION)
                at_least(sp, s.rowsT_psum, i - 2)
                at_least(sp, s.to_ready, i - 2)
                sp.dma_start(rows_in[:, slot, :, :], routed[bass.ds(row, BLOCK), :].rearrange("(j p) w -> p j w", p=P)
                             ).then_inc(rows_arrived[slot], 16)

            sp.wait_ge(s.idle_written, 16)
            sp.wait_ge(s.pads_written, 16 * EXPERTS)
            sp.wait_ge(s.scat_even, 32 * (BANDS // 2))
            sp.wait_ge(s.scat_odd, 32 * (BANDS // 2))
            for place in range(RING):
                load_rows(0, place)
            with sp.Fori(1, TURNS) as turn:
                for place in range(RING):
                    load_rows(turn, place)

            for slot in range(RING):
                sp.wait_ge(sent[slot], 16 * SUBS * TURNS)
            back = result[0:2 * P * BANDS, :].rearrange("(c g b p) d -> c g p b d", c=2, b=GB, p=P)
            out_v = out.rearrange("(g b) p c -> g p b c", b=GB)

            def load_back(g, par):
                for c2 in range(2):
                    sp.dma_start(y_back[:, par, c2, :, :], back[c2, g]).then_inc((s.back_even, s.back_odd)[par], 16)

            def store_out(g, par):
                sp.wait_ge(s.res_step, (g + 1) * (2 * GB))
                sp.dma_start(out_v[g], res[:, par, :, :]).then_inc((s.stored_even, s.stored_odd)[par], 16)

            load_back(0, 0)
            load_back(1, 1)
            with sp.Fori(0, BANDS // GB // 2 - 1) as i:
                for par in range(2):
                    store_out(i * 2 + par, par)
                    load_back(i * 2 + par + 2, par)
            for par in range(2):
                store_out(BANDS // GB - 2 + par, par)
            sp.wait_ge(s.stored_even, 16 * (BANDS // GB // 2))
            sp.wait_ge(s.stored_odd, 16 * (BANDS // GB // 2))

        @block.gpsimd
        def _(pool):
            nc.gpsimd.memset(zero[:, :], 0.0).then_inc(s.zeroed, 1)
            nc.gpsimd.memset(woff_sb[:, :, :], 0.0).then_inc(s.zeroed, 1)
            nc.gpsimd.memset(xnT[:, :, :], 0.0).then_inc(s.zeroed, 1)
            nc.gpsimd.memset(eps_c[:, :], LN_C_EPS).then_inc(s.zeroed, 1)
            nc.gpsimd.memset(eps_t[:, :], LN_T_EPS).then_inc(s.zeroed, 1)
            nc.gpsimd.memset(ones[:, :], 1.0).then_inc(s.zeroed, 1)
            nc.gpsimd.memset(mask[:, :, :, :], 1.0).then_inc(s.zeroed, 1)
            nc.gpsimd.memset(hat3[:, :, TAPS, :], 0.0).then_inc(s.zeroed, 1)
            nc.gpsimd.memset(every_sb[:, :], 1.0).then_inc(s.zeroed, 1)
            nc.gpsimd.memset(seen[:, 0, :], 0.0).then_inc(s.zeroed, 1)

            pool.wait_ge(s.consts_loaded, 16 * N_CONSTS)
            nc.gpsimd.tensor_copy(spread_sb[:, :, :], spread_f[:, :, :]).then_inc(s.tables_ready, 1)
            nc.gpsimd.tensor_copy(identb_sb[:, :], ident_sb[:, :]).then_inc(s.tables_ready, 1)
            nc.gpsimd.tensor_copy(before_sb[:, :], before_f[:, :]).then_inc(s.tables_ready, 1)

            def distances(b, par):
                o = offs[:, b, 0:2 * TAPS].rearrange("p (yx k one) -> p k yx one", yx=2, one=1)
                d = dist[:, par, :].rearrange("p (k yx j) -> p k yx j", k=TAPS, yx=2)
                r = rel_sb[:, :].rearrange("p (k yx j) -> p k yx j", k=TAPS, yx=2)
                nc.gpsimd.tensor_tensor(d, o.broadcast_to([P, TAPS, 2, WIN]), r, ALU.add
                                        ).then_inc(s.dist_ready, 1)

            def split(b, par):
                h3 = hat3[:, par, 0:TAPS, :].rearrange("p k (part h) -> p part k h", part=PARTS)
                h = hat[:, par, :].rearrange("p (k h) -> p k h", k=TAPS)
                r = rest[:, par, :].rearrange("p (k h) -> p k h", k=TAPS)
                pool.wait_ge(s.hi_ready, b + 1)
                nc.gpsimd.tensor_tensor(r, h, h3[:, 0], ALU.subtract).then_inc(s.pool_step, 1)
                nc.gpsimd.tensor_tensor(h3[:, 1], h, h3[:, 0], ALU.subtract).then_inc(s.pool_step, 1)
                pool.wait_ge(s.pool_step, b * 2 + 2)
                nc.gpsimd.tensor_tensor(h3[:, 2], r, h3[:, 1], ALU.subtract).then_inc(s.hat3_ready, 1)

            def pack(b, par):
                pool.wait_ge(s.xn2_ready, b + 1)
                settle(pool)
                at_least(pool, (s.scat_even, s.scat_odd)[par], (b // 2) * 32 if isinstance(b, int) else (b - par) * 16)
                if not isinstance(b, int):
                    settle(pool)
                nc.gpsimd.tensor_copy(payload[:, par, :, 0:C], xn2[:, par, :].unsqueeze(1).broadcast_to([P, 2, C])
                                      ).then_inc(s.payload_ready, 1)
                nc.gpsimd.tensor_copy(payload[:, par, :, C:C + 1].bitcast(I32), dest_sb[:, b, :].unsqueeze(2)
                                      ).then_inc(s.payload_ready, 1)

            def scatter(b, par):
                pool.wait_ge(s.slot_ready, b + 1)
                settle(pool)
                pool.wait_ge(s.payload_ready, b * 2 + 2)
                settle(pool)
                for c2 in range(2):
                    nc.gpsimd.indirect_dma_start(
                        routed, bass.IndirectOffsetOnAxis(slot[:, par, c2:c2 + 1], 0), payload[:, par, c2, :], None
                    ).then_inc((s.scat_even, s.scat_odd)[par], 16)

            flag = is_far(pool)
            with pool.If(flag):
                def gather(b, par):
                    pool.wait_ge(s.idx_ready, b + 1)
                    settle(pool)
                    for c4 in range(4):
                        for k in range(TAPS):
                            nc.gpsimd.indirect_dma_start(
                                corner[:, c4, k, :], None, xpad.rearrange("m r w c -> (m r w) c"),
                                bass.IndirectOffsetOnAxis(idx[:, c4, k:k + 1], 0)).then_inc(s.gathered, 16)
                    pack(b, par)
                    scatter(b, par)

                for b in range(2):
                    gather(b, b)
                with pool.Fori(1, BANDS // 2) as i:
                    gather(i * 2, 0)
                    gather(i * 2 + 1, 1)
            with pool.Else():
                distances(0, 0)
                distances(1, 1)
                for b in range(2):
                    split(b, b)
                distances(2, 0)

                def step(b, par):
                    known = isinstance(b, int)
                    if not known or b + 2 < BANDS:
                        split(b + 2, par)
                    if not known or b >= 3:
                        scatter(b - 3, 1 - par)
                    if not known or b >= 2:
                        pack(b - 2, par)
                    if not known or b + 3 < BANDS:
                        distances(b + 3, 1 - par)

                for b in range(HEAD):
                    step(b, b % 2)
                with pool.Fori(0, PAIRS_OF_BANDS) as i:
                    step(i * 2 + HEAD, 0)
                    step(i * 2 + HEAD + 1, 1)
                for b in range(TAIL, BANDS):
                    step(b, b % 2)
                scatter(BANDS - 3, 1)
                pack(BANDS - 2, 0)
                scatter(BANDS - 2, 0)
                pack(BANDS - 1, 1)
                scatter(BANDS - 1, 1)

            def send(turn, place):
                i, slot, uses = block_at(turn, place)
                pool.wait_ge(s.y_done, i + 1)
                settle(pool)
                for j in range(SUBS):
                    nc.gpsimd.indirect_dma_start(
                        result, bass.IndirectOffsetOnAxis(to_b[:, slot, j:j + 1].bitcast(U32), 0), y[:, slot, j, :],
                        None, bounds_check=2 * P * BANDS - 1, oob_is_err=False
                    ).then_inc(sent[slot], 16)

            with pool.Fori(0, TURNS) as turn:
                for place in range(RING):
                    send(turn, place)

        @block.scalar
        def _(act):
            def load(dst, src, loaded):
                act.dma_start(dst, src).then_inc(loaded, 16)

            def rows_of(ap, n):
                return ap.rearrange("(one o) -> one o", one=1).broadcast_to([P, n])

            early, late = s.early_loaded, s.consts_loaded
            load(ident_sb[:, :], ident, early)
            act.wait_ge(s.zeroed, 2)
            load(woff_sb[:, :, 0:OFFS], w_offset.rearrange("a b c o -> c (a b) o"), early)
            load(boff_sb[:, :], rows_of(b_offset, OFFS), early)
            load(fold_sb[:, :], fold, early)
            load(rel_sb[:, :], rel, late)
            load(spread_f[:, :, :], spread.rearrange("r (f q) -> r f q", f=4), late)
            load(before_f[:, :], before, late)
            load(table_sb[:, :], table, late)
            load(dest_sb[:, :, :], dest, late)
            load(padding_sb[:, :, :], padding, late)
            load(filt_sb[:, :, :], filt, late)
            load(gw_sb[:, :], gate_w, late)
            load(gb_sb[:, :], rows_of(gate_b, EXPERTS), late)
            load(w_all[:, :, :], experts, late)

            def std_image(m):
                act.wait_ge(s.stats8, m * BPI + BPI)
                nc.scalar.activation(sd8[:, :], mv8[:, :, 1], ACT.Sqrt, bias=eps_c[:, :]).then_inc(s.std8, 1)

            def evacuate_xnT(m):
                for h in range(2):
                    act.wait_ge(s.xnT_psum, m * 2 + h + 1)
                    nc.scalar.activation(xnT[:, 1 + 16 * h:17 + 16 * h, 1:1 + SIDE], image_view(bank[h][:, :]),
                                         ACT.Copy).then_inc(s.xnT_ready, 1)

            def evacuate_conv(m):
                for h in range(2):
                    act.wait_ge(s.conv_psum, m * 2 + h + 1)
                    for b in range(4):
                        nc.scalar.activation(
                            conv_sb[:, h, b * P:(b + 1) * P].rearrange("g (t dy dx) -> g t dy dx", t=TILES, dy=TILE),
                            bank[2 + h][:, b * P:(b + 1) * P].rearrange("g (dy t dx) -> g t dy dx", dy=TILE, t=TILES),
                            ACT.Copy).then_inc(s.conv_ready, 1)

            act.wait_ge(s.zeroed, N_CLEARED)
            std_image(0)
            with act.Fori(0, IMAGES - 1) as m:
                evacuate_xnT(m)
                std_image(m + 1)
                evacuate_conv(m)
            evacuate_xnT(IMAGES - 1)
            evacuate_conv(IMAGES - 1)
            act.wait_ge(s.offs_ready, IMAGES)
            nc.scalar.activation(mask[:, :, :, 1], offs[:, :, 2 * TAPS:], ACT.Sigmoid).then_inc(s.mask_ready, 1)

            def hi_part(b, par):
                act.wait_ge(s.hat_ready, b + 1)
                nc.scalar.activation(hat3[:, par, 0:TAPS, 0:HATS],
                                     hat[:, par, :].rearrange("p (k h) -> p k h", k=TAPS),
                                     ACT.Copy).then_inc(s.hi_ready, 1)

            def evacuate_hatT(b):
                act.wait_ge(s.hatT_psum, b + 1)
                nc.scalar.activation(hatT[:, :, :],
                                     bank4b[0:2 * SLOT, 0:PAIRS * P].rearrange("r (i t) -> r i t", i=PAIRS),
                                     ACT.Copy).then_inc(s.hatT_ready, 1)

            def copy_y(b, par, u):
                act.wait_ge(s.y_psum, b * 3 + u + 1)
                at_least(act, s.S_ready, b * 3 + u - 1)
                slot, n = (par + u) % 2, UNITS[u]
                nc.scalar.activation(ysp[:, slot, 0:n], bank[slot][0:Q, 0:n], ACT.Copy).then_inc(s.y_ready, 1)

            def sample_view(par, g):
                t0 = sum(GROUPS[:g])
                return samp[:, par, :, :].rearrange("c k (t p) -> c t k p", t=TILES)[:, t0:t0 + GROUPS[g]]

            def evacuate_samples(b, par, g):
                at_least(act, s.e_psum, b - 1)
                act.wait_ge(s.samp_psum, b * 3 + g + 1)
                nc.scalar.activation(
                    sample_view(par, g),
                    bank[5 + (par + g) % 2][:, 0:GROUPS[g] * TAPS * TT].rearrange(
                        "c (t k p) -> c t k p", k=TAPS, p=TT), ACT.Copy).then_inc(s.samp_act, 1)

            def std_band(b, par):
                act.wait_ge(s.mean1_ready, b + 1)
                nc.scalar.activation(sd1[:, par:par + 1], mv1[:, par, 1:2], ACT.Sqrt,
                                     bias=eps_t[:, :]).then_inc(s.std1_ready, 1)

            def evacuate_tokens(b, par):
                act.wait_ge(s.t_psum, b + 1)
                nc.scalar.activation(xn2T[:, par, :], bank[4][:, 0:P], ACT.Copy).then_inc(s.xn2T_ready, 1)

            flag = is_far(act)
            with act.If(flag):
                with act.Fori(0, BANDS // 2) as i:
                    for par in range(2):
                        b = i * 2 + par
                        for k in range(TAPS):
                            act.wait_ge(s.g_psum, b * TAPS + k + 1)
                            nc.scalar.activation(samp[:, par, k, :], bank[k % 2][:, 0:P], ACT.Copy
                                                 ).then_inc(s.samp_slow, 1)
                        std_band(b, par)
                        evacuate_tokens(b, par)
            with act.Else():
                hi_part(0, 0)
                hi_part(1, 1)
                evacuate_hatT(0)

                def step(b, par):
                    known = isinstance(b, int)
                    copy_y(b, par, 0)
                    copy_y(b, par, 1)
                    if not known or b >= 2:
                        evacuate_tokens(b - 2, par)
                    copy_y(b, par, 2)
                    if not known or b + 2 < BANDS:
                        hi_part(b + 2, par)
                    evacuate_samples(b, par, 0)
                    if not known or b >= 1:
                        std_band(b - 1, 1 - par)
                    if not known or b + 1 < BANDS:
                        evacuate_hatT(b + 1)
                    evacuate_samples(b, par, 1)

                for b in range(HEAD):
                    step(b, b % 2)
                with act.Fori(0, PAIRS_OF_BANDS) as i:
                    step(i * 2 + HEAD, 0)
                    step(i * 2 + HEAD + 1, 1)
                for b in range(TAIL, BANDS):
                    step(b, b % 2)
                evacuate_tokens(BANDS - 2, 0)
                std_band(BANDS - 1, 1)
                evacuate_tokens(BANDS - 1, 1)

            act.wait_ge(s.exp_in, 1)
            nc.scalar.activation(e_all[:, :, :], e_all[:, :, :], ACT.Exp).then_inc(s.exp_out, 1)

            def load_weights(turn, place):
                i, slot, uses = block_at(turn, place)
                at_least(act, s.h_psum, i - 2)
                e = expert_of(act, i)
                at_least(act, s.h_ready, (i - 2) * HALVES)
                act.dma_start(w_blk[:, slot, :], w_all[:, e, 0:W_UP]).then_inc(w_arrived[slot], 16)

            def evacuate_rows(turn, place):
                i, slot, uses = block_at(turn, place)
                act.wait_ge(s.rowsT_psum, i + 1)
                at_least(act, s.h_psum, i - 2)
                nc.scalar.activation(rowsT[:, slot, :], bank[slot][:, 0:BLOCK], ACT.Copy).then_inc(s.rowsT_ready, 1)

            def gelu(turn, place):
                i, slot, uses = block_at(turn, place)
                act.wait_ge(s.h_psum, i + 1)
                at_least(act, s.y_psum2, i - 2)
                for h in range(HALVES):
                    nc.scalar.activation(hid[:, slot, h, :], bank[3 + slot][:, h * BLOCK:(h + 1) * BLOCK], ACT.Gelu,
                                         bias=w_blk[:, slot, HID + h:HID + h + 1]).then_inc(s.h_ready, 1)

            def block_step(turn, place):
                if not is_last(turn, place):
                    evacuate_rows(turn, place + 1)
                gelu(turn, place)
                if not isinstance(turn, int) or turn < TURNS - 1:
                    load_weights(turn + 1, place)

            act.wait_ge(s.plan_ready, 1)
            for place in range(RING):
                load_weights(0, place)
            evacuate_rows(0, 0)
            block_loop(act, block_step)

        @block.vector
        def _(dve):
            def stats_image(m):
                dve.wait_ge(s.x_loaded, m * 16 + 16)
                settle(dve)
                for b in range(BPI):
                    last = nc.vector.bn_stats(st8[:, b, :], x_nat[:, m * BPI + b, :])
                last.then_inc(s.dve_stat8, 1)
                dve.wait_ge(s.dve_stat8, m + 1)
                settle(dve)
                for b in range(BPI):
                    nc.vector.bn_aggr(mv8[:, b, :], st8[:, b, :]).then_inc(s.stats8, 1)

            def normalise_image(m):
                dve.wait_ge(s.std8, m + 1)
                nc.vector.reciprocal(rs8[:, :], sd8[:, :]).then_inc(s.rstd8, 1)
                dve.wait_ge(s.rstd8, m + 1)
                at_least(dve, s.xnT_psum, m * 2)
                at_least(dve, s.xn_stored, m * (16 * BPI))
                for b in range(BPI):
                    last = nc.vector.tensor_scalar(xn8[:, b, :], x_nat[:, m * BPI + b, :], mv8[:, b, 0:1],
                                                   rs8[:, b:b + 1], ALU.subtract, ALU.mult)
                last.then_inc(s.xn8_ready, 1)

            def offsets_image(m):
                at_least(dve, s.early_loaded, 16 * 4)
                dve.wait_ge(s.fold_psum, m + 1)
                nc.vector.tensor_tensor(
                    offs[:, bass.ds(m * BPI, BPI), :], bank[5][:, 0:BPI * OFFS].rearrange("p (b o) -> p b o", o=OFFS),
                    boff_sb[:, :].unsqueeze(1).broadcast_to([P, BPI, OFFS]), ALU.add).then_inc(s.offs_ready, 1)
                dve.wait_ge(s.offs_ready, m + 1)
                dve.sem_inc(s.fold_free, 1)

            dve.sem_inc(s.fold_free, 1)
            stats_image(0)
            normalise_image(0)
            with dve.Fori(1, IMAGES) as m:
                stats_image(m)
                normalise_image(m)
                offsets_image(m - 1)
            offsets_image(IMAGES - 1)

            dve.wait_ge(s.offs_ready, IMAGES)
            nc.vector.tensor_tensor(near[:, :].rearrange("p (b o) -> p b o", b=BANDS), offs[:, :, 0:2 * TAPS],
                                    offs[:, :, 0:2 * TAPS], ALU.mult).then_inc(s.near_ready, 1)
            dve.wait_ge(s.near_ready, 1)
            nc.vector.tensor_scalar(near[:, :], near[:, :], float(REACH * REACH), None, ALU.is_le
                                    ).then_inc(s.near_ready, 1)
            dve.wait_ge(s.near_ready, 2)
            nc.vector.tensor_reduce(near_n[:, :], near[:, :], AX_X, ALU.add).then_inc(s.near_ready, 1)
            dve.wait_ge(s.near_psum, 1)
            nc.vector.tensor_scalar(far[:, :], bank[6][0:1, 0:1], float(P * BANDS * 2 * TAPS), None,
                                    ALU.is_lt).then_inc(s.far_ready, 1)

            def hats(b, par):
                dve.wait_ge(s.dist_ready, b + 1)
                nc.vector.scalar_tensor_tensor(tent[:, par, :], dist[:, par, :], -1.0, dist[:, par, :],
                                               ALU.mult, ALU.max).then_inc(s.dve_hat, 1)
                dve.wait_ge(s.dve_hat, b * 2 + 1)
                nc.vector.tensor_scalar(tent[:, par, :], tent[:, par, :], -1.0, 0.0, ALU.add, ALU.min
                                        ).then_inc(s.dve_hat, 1)
                dve.wait_ge(s.dve_hat, b * 2 + 2)
                nc.vector.tensor_tensor(
                    hat[:, par, :].rearrange("p (k j) -> p k j", j=WIN),
                    tent[:, par, :].rearrange("p (k j) -> p k j", j=WIN),
                    mask[:, b, :, :].rearrange("p k yx -> p (k yx)").unsqueeze(2).broadcast_to([P, 2 * TAPS, WIN]),
                    ALU.mult).then_inc(s.hat_ready, 1)

            def multiply(b, par, u):
                at_least(dve, s.samp_psum, (b - 1) * 3)
                dve.wait_ge(s.y_ready, b * 3 + u + 1)
                dve.wait_ge(s.x_psum, b * 3 + u + 1)
                slot, n, c0 = (par + u) % 2, UNITS[u], sum(UNITS[:u])
                nc.vector.tensor_tensor(S[:, par, c0:c0 + n], ysp[:, slot, 0:n], bank[2 + slot][0:Q, 0:n],
                                        ALU.mult).then_inc(s.S_ready, 1)

            def samples(b, par):
                at_least(dve, s.e_psum, b - 1)
                dve.wait_ge(s.samp_psum, b * 3 + 3)
                t0 = sum(GROUPS[:2])
                nc.vector.tensor_copy(
                    samp[:, par, :, :].rearrange("c k (t p) -> c t k p", t=TILES)[:, t0:],
                    bank[5 + par][:, 0:GROUPS[2] * TAPS * TT].rearrange("c (t k p) -> c t k p", k=TAPS, p=TT)
                ).then_inc(s.samp_dve, 1)

            def residual(b, par):
                dve.wait_ge(s.e_psum, b + 1)
                nc.vector.tensor_tensor(x1[:, b, :], x1[:, b, :], bank[7][:, 0:C], ALU.add).then_inc(s.x1_ready, 1)
                dve.wait_ge(s.x1_ready, b + 1)
                settle(dve)
                nc.vector.bn_stats(st1[:, par, :], x1[:, b, :]).then_inc(s.dve_stat, 1)
                dve.wait_ge(s.dve_stat, b + 1)
                settle(dve)
                nc.vector.bn_aggr(mv1[:, par, :], st1[:, par, :]).then_inc(s.mean1_ready, 1)

            def normalise(b, par):
                dve.wait_ge(s.std1_ready, b + 1)
                nc.vector.reciprocal(rs1[:, par:par + 1], sd1[:, par:par + 1]).then_inc(s.dve_rstd, 1)
                dve.wait_ge(s.dve_rstd, b + 1)
                at_least(dve, s.t_psum, b - 1)
                at_least(dve, s.payload_ready, 2 * (b - 1))
                nc.vector.tensor_scalar(xn2[:, par, :], x1[:, b, :], mv1[:, par, 0:1], rs1[:, par:par + 1],
                                        ALU.subtract, ALU.mult).then_inc(s.xn2_ready, 1)

            CHAIN = 6

            def add_gate_bias(b, par):
                dve.wait_ge(s.l_psum, b + 1)
                nc.vector.tensor_tensor(lg[:, par, :], bank[4][:, 0:EXPERTS], gb_sb[:, :], ALU.add
                                        ).then_inc(s.route, 1)

            def choose(b, par):
                dve.wait_ge(s.route, b * CHAIN + 1)
                settle(dve)
                nc.vector.max(top[:, par, :], lg[:, par, :]).then_inc(s.route, 1)
                dve.wait_ge(s.route, b * CHAIN + 2)
                settle(dve)
                nc.vector.max_index(topi[:, par, :], top[:, par, :], lg[:, par, :]).then_inc(s.route, 1)
                nc.vector.tensor_copy(top_all[:, b, :], top[:, par, :]).then_inc(s.stashed, 1)
                dve.wait_ge(s.route, b * CHAIN + 3)
                nc.vector.tensor_tensor(
                    chosen[:, par, :, :], table_sb[:, T_RANK:T_RANK + EXPERTS].unsqueeze(1).broadcast_to([P, 2, EXPERTS]),
                    topi[:, par, 0:2].unsqueeze(2).broadcast_to([P, 2, EXPERTS]), ALU.is_equal).then_inc(s.route, 1)
                dve.wait_ge(s.route, b * CHAIN + 4)
                nc.vector.tensor_tensor(both[:, par, :], chosen[:, par, 0, :], chosen[:, par, 1, :], ALU.add
                                        ).then_inc(s.route, 1)
                dve.wait_ge(s.route, b * CHAIN + 5)
                at_least(dve, s.place_psum, b)
                nc.vector.tensor_tensor(seen[:, 1 - par, :], seen[:, par, :], both[:, par, :], ALU.add
                                        ).then_inc(s.route, 1)

            def place_rows(b, par):
                dve.wait_ge(s.place_psum, b + 1)
                nc.vector.tensor_tensor(place[:, :], bank[7][:, 256:256 + EXPERTS],
                                        table_sb[:, T_REGION:T_REGION + EXPERTS], ALU.add).then_inc(s.place_ready, 1)
                dve.wait_ge(s.place_ready, b + 1)
                nc.vector.tensor_tensor(placed[:, :, :], chosen[:, par, :, :],
                                        place[:, :].unsqueeze(1).broadcast_to([P, 2, EXPERTS]), ALU.mult
                                        ).then_inc(s.placed_ready, 1)
                dve.wait_ge(s.placed_ready, b + 1)
                at_least(dve, s.slot_ready, b)
                if not isinstance(b, int) or b >= 2:
                    dve.wait_ge((s.scat_even, s.scat_odd)[par],
                                (b // 2) * 32 if isinstance(b, int) else (b - par) * 16)
                nc.vector.tensor_reduce(slot_f[:, :], placed[:, :, :], AX_X, ALU.add).then_inc(s.slot_f_ready, 1)
                dve.wait_ge(s.slot_f_ready, b + 1)
                nc.vector.tensor_copy(slot[:, par, :], slot_f[:, :]).then_inc(s.slot_ready, 1)

            dve.wait_ge(s.mask_ready, 1)
            dve.wait_ge(s.consts_loaded, 16 * N_CONSTS)
            dve.wait_ge(s.zeroed, N_CLEARED)
            dve.wait_ge(s.x1_loaded, 16)
            flag = is_far(dve)
            with dve.If(flag):
                def gathered_band(b, par):
                    n = [0]

                    def link(ins, total=SLOW_LINKS):
                        ins.then_inc(s.dve_slow, 1)
                        n[0] += 1
                        dve.wait_ge(s.dve_slow, b * total + n[0])

                    dve.wait_ge(s.base_loaded, b * 16 + 16)
                    link(nc.vector.tensor_tensor(pos[:, :], offs[:, b, 0:2 * TAPS], base_sb[:, 0:2 * TAPS], ALU.add))
                    link(nc.vector.tensor_scalar(pos[:, :], pos[:, :], 1.0, float(PADDED - 2), ALU.max, ALU.min))
                    link(nc.vector.tensor_copy(posi[:, :], pos[:, :]))
                    link(nc.vector.tensor_copy(posf[:, :], posi[:, :]))
                    link(nc.vector.tensor_tensor(over[:, :], posf[:, :], pos[:, :], ALU.is_gt))
                    link(nc.vector.tensor_tensor(low[:, :], posf[:, :], over[:, :], ALU.subtract))
                    fr1 = frac[:, :, 1, :]
                    link(nc.vector.tensor_tensor(fr1, pos[:, :].rearrange("p (a k) -> p a k", a=2),
                                                 low[:, :].rearrange("p (a k) -> p a k", a=2), ALU.subtract))
                    link(nc.vector.tensor_scalar(frac[:, :, 0, :], fr1, -1.0, 1.0, ALU.mult, ALU.add))
                    link(nc.vector.scalar_tensor_tensor(line[:, :], low[:, 0:TAPS], float(PADDED),
                                                        low[:, TAPS:2 * TAPS], ALU.mult, ALU.add))
                    for c4 in range(4):
                        link(nc.vector.tensor_scalar(cell[:, c4, :], line[:, :], base_sb[:, 2 * TAPS:2 * TAPS + 1],
                                                     float((c4 // 2) * PADDED + c4 % 2), ALU.add, ALU.add))
                    nc.vector.tensor_copy(idx[:, :, :], cell[:, :, :]).then_inc(s.idx_ready, 1)
                    for a in range(2):
                        link(nc.vector.tensor_tensor(wx[:, a, :], frac[:, 1, a, :], mask[:, b, :, 1], ALU.mult))
                    for c4 in range(4):
                        link(nc.vector.tensor_tensor(cw[:, c4, :], frac[:, 0, c4 // 2, :], wx[:, c4 % 2, :], ALU.mult))
                    dve.wait_ge(s.gathered, b * (16 * 4 * TAPS) + 16 * 4 * TAPS)
                    for k in range(TAPS):
                        link(nc.vector.tensor_scalar(gsum[:, k, :], corner[:, 0, k, :], cw[:, 0, k:k + 1], None,
                                                     ALU.mult))
                    for c4 in range(1, 4):
                        for k in range(TAPS):
                            link(nc.vector.scalar_tensor_tensor(gsum[:, k, :], corner[:, c4, k, :],
                                                                cw[:, c4, k:k + 1], gsum[:, k, :],
                                                                ALU.mult, ALU.add))
                    assert n[0] == SLOW_LINKS
                    nc.vector.tensor_copy(over[:, 0:1], gsum[:, 0, 0:1]).then_inc(s.gsum_ready, 1)
                    dve.sem_inc(s.base_free, 1)
                    residual(b, par)
                    normalise(b, par)
                    add_gate_bias(b, par)
                    choose(b, par)
                    place_rows(b, par)

                dve.sem_inc(s.base_free, 1)
                for b in range(2):
                    gathered_band(b, b)
                with dve.Fori(1, BANDS // 2) as i:
                    gathered_band(i * 2, 0)
                    gathered_band(i * 2 + 1, 1)
            with dve.Else():
                hats(0, 0)
                hats(1, 1)

                def step(b, par):
                    known = isinstance(b, int)
                    multiply(b, par, 0)
                    multiply(b, par, 1)
                    if not known or b >= 2:
                        add_gate_bias(b - 2, par)
                    multiply(b, par, 2)
                    if not known or b + 2 < BANDS:
                        hats(b + 2, par)
                    if not known or b >= 1:
                        residual(b - 1, 1 - par)
                    if not known or b >= 2:
                        choose(b - 2, par)
                    if not known or b >= 1:
                        normalise(b - 1, 1 - par)
                    samples(b, par)
                    if not known or b >= 2:
                        place_rows(b - 2, par)

                for b in range(HEAD):
                    step(b, b % 2)
                with dve.Fori(0, PAIRS_OF_BANDS) as i:
                    step(i * 2 + HEAD, 0)
                    step(i * 2 + HEAD + 1, 1)
                for b in range(TAIL, BANDS):
                    step(b, b % 2)
                residual(BANDS - 1, 1)
                add_gate_bias(BANDS - 2, 0)
                choose(BANDS - 2, 0)
                normalise(BANDS - 1, 1)
                place_rows(BANDS - 2, 0)
                add_gate_bias(BANDS - 1, 1)
                choose(BANDS - 1, 1)
                place_rows(BANDS - 1, 1)

            m = [0]

            def then(ins):
                ins.then_inc(s.plan_step, 1)
                m[0] += 1
                dve.wait_ge(s.plan_step, m[0])

            def row_of(first, n):
                return table_sb[0:1, first:first + n]

            n_thr = P * BANDS // BLOCK
            dve.wait_ge(s.count_psum, 1)
            then(nc.vector.tensor_copy(count[:, :], bank[6][0:1, 0:EXPERTS]))
            then(nc.vector.tensor_tensor(over_t[:, :, :], count[:, :].unsqueeze(2).broadcast_to([1, EXPERTS, n_thr]),
                                         row_of(T_THRESH, n_thr).unsqueeze(1).broadcast_to([1, EXPERTS, n_thr]),
                                         ALU.is_gt))
            then(nc.vector.tensor_reduce(nblk[:, :], over_t[:, :, :], AX_X, ALU.add))
            then(nc.vector.tensor_tensor(tri_t[:, :, :], nblk[:, :].unsqueeze(1).broadcast_to([1, EXPERTS, EXPERTS]),
                                         row_of(T_TRI, EXPERTS * EXPERTS).rearrange("o (a b) -> o a b", a=EXPERTS),
                                         ALU.mult))
            then(nc.vector.tensor_reduce(upto[:, :], tri_t[:, :, :], AX_X, ALU.add))
            then(nc.vector.tensor_tensor(past[:, :, :], row_of(T_BLK, BLOCKS).unsqueeze(2).broadcast_to([1, BLOCKS, EXPERTS]),
                                         upto[:, :].unsqueeze(1).broadcast_to([1, BLOCKS, EXPERTS]), ALU.is_ge))
            then(nc.vector.tensor_reduce(blk_e[:, :], past[:, :, :], AX_X, ALU.add))
            then(nc.vector.tensor_tensor(past_n[:, :, :], past[:, :, :],
                                         nblk[:, :].unsqueeze(1).broadcast_to([1, BLOCKS, EXPERTS]), ALU.mult))
            then(nc.vector.tensor_reduce(blk_first[:, :], past_n[:, :, :], AX_X, ALU.add))
            then(nc.vector.scalar_tensor_tensor(blk_row[:, :], blk_first[:, :], -float(BLOCK), row_of(T_BLKROW, BLOCKS),
                                                ALU.mult, ALU.add))
            then(nc.vector.scalar_tensor_tensor(blk_row[:, :], blk_e[:, :], float(REGION), blk_row[:, :],
                                                ALU.mult, ALU.add))
            then(nc.vector.tensor_scalar(blk_i[:, :, 0], blk_row[:, :], float(EXPERTS * REGION), None, ALU.min))
            then(nc.vector.tensor_scalar(blk_i[:, :, 1], blk_e[:, :], float(EXPERTS - 1), None, ALU.min))
            nc.vector.tensor_tensor(pad_row[:, :], count[:, :], row_of(T_REGION, EXPERTS), ALU.add
                                    ).then_inc(s.plan_ready, 1)

            dve.wait_ge(s.stashed, BANDS)
            nc.vector.tensor_tensor(e_all[:, :, :], top_all[:, :, :],
                                    top_all[:, :, 0:1].broadcast_to([P, BANDS, EXPERTS]), ALU.subtract
                                    ).then_inc(s.exp_in, 1)
            dve.wait_ge(s.exp_out, 1)
            nc.vector.tensor_reduce(e_sum[:, :], e_all[:, :, :], AX_X, ALU.add).then_inc(s.share_step, 1)
            dve.wait_ge(s.share_step, 1)
            nc.vector.reciprocal(share[:, 0, :], e_sum[:, :]).then_inc(s.share_step, 1)
            dve.wait_ge(s.share_step, 2)
            nc.vector.tensor_tensor(share[:, 1, :], e_all[:, :, 1], share[:, 0, :], ALU.mult).then_inc(s.share_step, 1)

            def keep_dest(turn, place):
                i, slot, uses = block_at(turn, place)
                dve.wait_ge(rows_arrived[slot], uses * 16 + 16)
                at_least(dve, s.y_done, i - 2)
                if not isinstance(i, int):
                    settle(dve)
                nc.vector.tensor_copy(to_a[:, slot, :].unsqueeze(2), rows_in[:, slot, :, C:C + 1].bitcast(I32)
                                      ).then_inc(s.to_ready, 1)

            def finish(turn, place):
                i, slot, uses = block_at(turn, place)
                e = expert_of(dve, i)
                dve.wait_ge(s.y_psum2, i + 1)
                at_least(dve, sent[slot], uses * (16 * SUBS))
                b2_row = w_all[:, e, WROW - C:].unsqueeze(1).broadcast_to([P, SUBS, C])
                nc.vector.tensor_tensor(y[:, slot, :, :], bank[slot][:, BLOCK:2 * BLOCK].rearrange(
                    "p (j c) -> p j c", c=C), b2_row, ALU.add).then_inc(s.y_ready2, 1)
                dve.wait_ge(s.to_ready, i + 1)
                nc.vector.tensor_copy(to_b[:, slot, :], to_a[:, slot, :]).then_inc(s.y_done, 1)

            def block_step(turn, place):
                if not is_first(turn, place):
                    finish(*previous(turn, place))
                if not is_last(turn, place):
                    keep_dest(turn, place + 1)

            keep_dest(0, 0)
            block_loop(dve, block_step)
            finish(TURNS - 1, RING - 1)

            dve.wait_ge(s.share_step, 3)

            def combine(g, par, first):
                dve.wait_ge((s.back_even, s.back_odd)[par], g * 16 + (32 - 16 * par))
                if not first:
                    dve.wait_ge((s.stored_even, s.stored_odd)[par], g * 8 - 8 * par)
                for j in range(GB):
                    b = g * GB + j
                    nc.vector.scalar_tensor_tensor(res[:, par, j, :], y_back[:, par, 0, j, :], share[:, 0, bass.ds(b, 1)],
                                                   x1[:, b, :], ALU.mult, ALU.add).then_inc(s.res_step, 1)
                dve.wait_ge(s.res_step, g * (2 * GB) + GB)
                for j in range(GB):
                    b = g * GB + j
                    nc.vector.scalar_tensor_tensor(res[:, par, j, :], y_back[:, par, 1, j, :], share[:, 1, bass.ds(b, 1)],
                                                   res[:, par, j, :], ALU.mult, ALU.add).then_inc(s.res_step, 1)

            combine(0, 0, True)
            combine(1, 1, True)
            with dve.Fori(1, BANDS // GB // 2) as i:
                combine(i * 2, 0, False)
                combine(i * 2 + 1, 1, False)

        @block.tensor
        def _(pe):
            pe.wait_ge(s.early_loaded, 16 * 4)
            pe.wait_ge(s.zeroed, N_CLEARED)
            with pe.Fori(0, IMAGES) as m:
                pe.wait_ge(s.xn8_ready, m + 1)
                for b in range(BPI):
                    last = nc.tensor.transpose(bank[b // 4][:, (b % 4) * P:(b % 4 + 1) * P], xn8[:, b, :], ident_sb[:, :])
                    if b % 4 == 3:
                        last.then_inc(s.xnT_psum, 1)
                pe.wait_ge(s.xnT_ready, m * 2 + 2)
                for h in range(2):
                    for k in range(TAPS):
                        g = k % 4
                        last = nc.tensor.matmul(
                            bank[2 + h][32 * g:32 * g + 32, :], woff_sb[:, k, :],
                            xnT[:, 16 * h + k // 3:16 * h + k // 3 + 16, k % 3:k % 3 + SIDE],
                            start=(k < 4), stop=(k + 4 >= TAPS))
                    last.then_inc(s.conv_psum, 1)
                pe.wait_ge(s.fold_free, m + 1)
                for h in range(2):
                    pe.wait_ge(s.conv_ready, m * 8 + h * 4 + 4)
                    for b in range(4):
                        c0 = (4 * h + b) * OFFS
                        last = nc.tensor.matmul(bank[5][:, c0:c0 + OFFS], conv_sb[:, h, b * P:(b + 1) * P], fold_sb[:, :], start=True, stop=True)
                last.then_inc(s.fold_psum, 1)
            pe.wait_ge(s.near_ready, 3)
            nc.tensor.matmul(bank[6][0:1, 0:1], near_n[:, :], ones[:, :], start=True, stop=True
                             ).then_inc(s.near_psum, 1)

            def transpose_hats(b, par):
                pe.wait_ge(s.hat3_ready, b + 1)
                if not isinstance(b, int) or b >= 3:
                    pe.wait_ge(s.route, (b - 3) * 6 + 1)
                for i in range(PAIRS):
                    last = nc.tensor.transpose(bank4b[0:2 * SLOT, i * P:(i + 1) * P],
                                               hat3[:, par, 2 * i:2 * i + 2, :].rearrange("p k r -> p (k r)"),
                                               identb_sb[:, :])
                last.then_inc(s.hatT_psum, 1)

            def spread_hats(b, par, u):
                pe.wait_ge(s.hatT_ready, b + 1)
                slot, n, odd = (par + u) % 2, UNITS[u], u % 2
                moving = hatT[:, 4, :] if u == 2 else hatT[:, 0:4, :].rearrange("r i t -> r (i t)")
                at_least(pe, s.y_ready, b * 3 + u - 1)
                nc.tensor.matmul(bank[slot][0:Q, 0:n], spread_sb[:, 2 * odd, :], moving,
                                 start=True, stop=True).then_inc(s.y_psum, 1)
                at_least(pe, s.S_ready, b * 3 + u - 1)
                nc.tensor.matmul(bank[2 + slot][0:Q, 0:n], spread_sb[:, 2 * odd + 1, :], moving,
                                 start=True, stop=True).then_inc(s.x_psum, 1)

            ORDER = [0, 2, 4, 6, 1, 3, 5, 7, 8]

            def sample(b, par, loads, g):
                if g == 0:
                    pe.wait_ge(s.S_ready, b * 3 + 3)
                    pe.wait_ge((s.win_even, s.win_odd)[par], loads * (16 * TILES))
                    at_least(pe, s.samp_act, b * 2)
                elif g == 1:
                    at_least(pe, s.samp_dve, b)
                else:
                    pe.wait_ge(s.samp_act, b * 2 + 1)
                weights = S[:, par, :].rearrange("q (k t p) -> q t k p", k=TAPS, t=TILES)
                for i in range(GROUPS[g]):
                    t = sum(GROUPS[:g]) + i
                    last = nc.tensor.matmul(bank[5 + (par + g) % 2][:, i * TAPS * TT:(i + 1) * TAPS * TT],
                                            xwin[:, par, t, :], weights[:, t], start=True, stop=True)
                last.then_inc(s.samp_psum, 1)

            FIRST_TAPS = 6

            def project(b, par, taps, order):
                if taps[0] == 0:
                    at_least(pe, s.x1_ready, b)
                    at_least(pe, s.place_ready, b - 1)
                for j in taps:
                    last = nc.tensor.matmul(bank[7][:, 0:C], samp[:, par, j, :], filt_sb[:, order[j], :],
                                            start=(j == 0), stop=(j == TAPS - 1))
                if taps[-1] == TAPS - 1:
                    last.then_inc(s.e_psum, 1)

            def samples_ready(b):
                pe.wait_ge(s.samp_act, b * 2 + 2)
                pe.wait_ge(s.samp_dve, b + 1)

            def transpose_tokens(b, par):
                pe.wait_ge(s.xn2_ready, b + 1)
                nc.tensor.transpose(bank[4][:, 0:P], xn2[:, par, :], ident_sb[:, :]).then_inc(s.t_psum, 1)

            def gate(b, par):
                pe.wait_ge(s.xn2T_ready, b + 1)
                nc.tensor.matmul(bank[4][:, 0:EXPERTS], xn2T[:, par, :], gw_sb[:, :],
                                 start=True, stop=True).then_inc(s.l_psum, 1)

            def count_places(b, par):
                pe.wait_ge(s.route, b * 6 + 5)
                where = bank[7][:, 256:256 + EXPERTS]
                nc.tensor.matmul(where, before_sb[:, :], both[:, par, :], start=True, stop=False)
                nc.tensor.matmul(where, every_sb[:, :], seen[:, par, :], start=False, stop=True
                                 ).then_inc(s.place_psum, 1)

            pe.wait_ge(s.consts_loaded, 16 * N_CONSTS)
            pe.wait_ge(s.tables_ready, 3)
            flag = is_far(pe)
            with pe.If(flag):
                with pe.Fori(0, BANDS // 2) as i:
                    for par in range(2):
                        b = i * 2 + par
                        pe.wait_ge(s.gsum_ready, b + 1)
                        for k in range(TAPS):
                            if k >= 2:
                                pe.wait_ge(s.samp_slow, b * TAPS + k - 1)
                            nc.tensor.transpose(bank[k % 2][:, 0:P], gsum[:, k, :], ident_sb[:, :]
                                                ).then_inc(s.g_psum, 1)
                        pe.wait_ge(s.samp_slow, b * TAPS + TAPS)
                        for j in range(TAPS):
                            last = nc.tensor.matmul(bank[7][:, 0:C], samp[:, par, j, :], filt_sb[:, j, :],
                                                    start=(j == 0), stop=(j == TAPS - 1))
                        last.then_inc(s.e_psum, 1)
                        transpose_tokens(b, par)
                        gate(b, par)
                        count_places(b, par)
            with pe.Else():
                transpose_hats(0, 0)

                def step(b, par, loads):
                    known = isinstance(b, int)
                    spread_hats(b, par, 0)
                    spread_hats(b, par, 1)
                    if not known or b >= 2:
                        transpose_tokens(b - 2, par)
                    if not known or b >= 1:
                        samples_ready(b - 1)
                        project(b - 1, 1 - par, range(FIRST_TAPS), ORDER)
                    if not known or b >= 2:
                        gate(b - 2, par)
                    spread_hats(b, par, 2)
                    if not known or b >= 1:
                        project(b - 1, 1 - par, range(FIRST_TAPS, TAPS), ORDER)
                    sample(b, par, loads, 0)
                    if not known or b + 1 < BANDS:
                        transpose_hats(b + 1, 1 - par)
                    sample(b, par, loads, 1)
                    sample(b, par, loads, 2)
                    if not known or b >= 2:
                        pe.wait_ge(s.x1_ready, b)
                        count_places(b - 2, par)

                for b in range(HEAD):
                    step(b, b % 2, b // 2 + 1)
                with pe.Fori(0, PAIRS_OF_BANDS) as i:
                    step(i * 2 + HEAD, 0, i + 3)
                    step(i * 2 + HEAD + 1, 1, i + 3)
                for b in range(TAIL, BANDS):
                    step(b, b % 2, b // 2 + 1)
                samples_ready(BANDS - 1)
                project(BANDS - 1, 1, range(TAPS), ORDER)
                transpose_tokens(BANDS - 2, 0)
                gate(BANDS - 2, 0)
                pe.wait_ge(s.x1_ready, BANDS)
                count_places(BANDS - 2, 0)
                pe.wait_ge(s.route, (BANDS - 2) * 6 + 1)
                transpose_tokens(BANDS - 1, 1)
                gate(BANDS - 1, 1)
                pe.wait_ge(s.place_ready, BANDS - 1)
                count_places(BANDS - 1, 1)

            pe.wait_ge(s.route, BANDS * 6)
            nc.tensor.matmul(bank[6][:, 0:EXPERTS], every_sb[:, :], seen[:, 0, :], start=True, stop=True
                             ).then_inc(s.count_psum, 1)

            def transpose_rows(turn, place):
                i, slot, uses = block_at(turn, place)
                pe.wait_ge(rows_arrived[slot], uses * 16 + 16)
                at_least(pe, s.y_ready2, i - 2)
                for j in range(SUBS):
                    last = nc.tensor.transpose(bank[slot][:, j * P:(j + 1) * P], rows_in[:, slot, j, 0:C], ident_sb[:, :])
                last.then_inc(s.rowsT_psum, 1)

            def up(turn, place):
                i, slot, uses = block_at(turn, place)
                pe.wait_ge(w_arrived[slot], uses * 16 + 16)
                pe.wait_ge(s.rowsT_ready, i + 1)
                at_least(pe, s.h_ready, (i - 2) * HALVES)
                for h in range(HALVES):
                    last = nc.tensor.matmul(bank[3 + slot][:, h * BLOCK:(h + 1) * BLOCK],
                                            w_blk[:, slot, h * P:(h + 1) * P], rowsT[:, slot, :], start=True, stop=True)
                last.then_inc(s.h_psum, 1)

            def down(turn, place):
                i, slot, uses = block_at(turn, place)
                e = expert_of(pe, i)
                pe.wait_ge(s.h_ready, i * HALVES + HALVES)
                for j in range(SUBS):
                    for h in range(HALVES):
                        last = nc.tensor.matmul(bank[slot][:, BLOCK + j * C:BLOCK + (j + 1) * C],
                                                hid[:, slot, h, j * P:(j + 1) * P],
                                                w_all[:, e, W_UP + h * C:W_UP + (h + 1) * C],
                                                start=(h == 0), stop=(h == HALVES - 1))
                last.then_inc(s.y_psum2, 1)

            def block_step(turn, place):
                up(turn, place)
                if not is_last(turn, place):
                    transpose_rows(turn, place + 1)
                if not is_first(turn, place):
                    down(*previous(turn, place))

            transpose_rows(0, 0)
            block_loop(pe, block_step)
            down(TURNS - 1, RING - 1)


def kernel(x, L0_conv_w_offset, L0_conv_b_offset, L0_conv_filt, L0_ffn_gate_w, L0_ffn_gate_b,
           L0_ffn_W1, L0_ffn_b1, L0_ffn_W2, L0_ffn_b2):
    import numpy as np
    import concourse.bacc as bacc
    from concourse.bass_utils import run_bass_kernel_spmd

    x = np.asarray(x)
    rows = x.reshape(BANDS, P, C)
    tiles = x.reshape(BANDS, TILE, TILES, TILE, C).transpose(0, 2, 1, 3, 4).reshape(BANDS, P, C)
    w2 = np.asarray(L0_ffn_W2).reshape(EXPERTS, HALVES, P, C).transpose(2, 0, 1, 3)
    experts = np.concatenate([
        np.asarray(L0_ffn_W1).transpose(1, 0, 2),
        np.asarray(L0_ffn_b1).reshape(EXPERTS, HALVES, P).transpose(2, 0, 1),
        w2.reshape(P, EXPERTS, HALVES * C),
        np.broadcast_to(np.asarray(L0_ffn_b2), (P, EXPERTS, C)),
    ], axis=2)
    arrays = {
        "x_rows": rows,
        "x_tiles": tiles,
        "w_offset": np.asarray(L0_conv_w_offset),
        "b_offset": np.asarray(L0_conv_b_offset),
        "filt": np.asarray(L0_conv_filt).reshape(C, C, TAPS).transpose(1, 2, 0),
        "gate_w": np.asarray(L0_ffn_gate_w),
        "gate_b": np.asarray(L0_ffn_gate_b),
        "experts": experts,
        **window_constants(),
    }
    arrays = {k: np.ascontiguousarray(v) for k, v in arrays.items()}
    nc = bacc.Bacc("TRN2", target_bir_lowering=False, num_devices=1)
    args = {k: nc.dram_tensor(f"in_{k}", v.shape, mybir.dt.from_np(v.dtype), kind="ExternalInput").ap()
            for k, v in arrays.items()}
    out = nc.dram_tensor("out_tiles", (BANDS, P, C), F32, kind="ExternalOutput").ap()
    program(nc, **args, out=out)
    result = run_bass_kernel_spmd(nc, [{f"in_{k}": v for k, v in arrays.items()}], core_ids=[0])
    got = result.results[0]["out_tiles"]
    return got.reshape(BANDS, TILES, TILE, TILE, C).transpose(0, 2, 1, 3, 4).reshape(IMAGES, SIDE, SIDE, C)
```

```python
from contextlib import ExitStack

import concourse.bass as bass
from concourse import mybir

F32 = mybir.dt.float32
BF16 = mybir.dt.bfloat16
I32 = mybir.dt.int32
U32 = mybir.dt.uint32
ALU = mybir.AluOpType
ACT = mybir.ActivationFunctionType
AX_X = mybir.AxisListType.X

P = 128
IMAGES, SIDE = 4, 32
C = 128
TAPS = 9
OFFS = 3 * TAPS
TILE = 4
TILES = SIDE // TILE
BANDS = IMAGES * SIDE // TILE
BPI = BANDS // IMAGES
REACH = 2
HALO = REACH + 1
WIN = TILE + 2 * HALO
Q = WIN * WIN
PADDED = SIDE + 2 * HALO
BORDER_ROWS = PADDED - 1
HATS = 2 * WIN
PARTS = 3
SLOT = PARTS * HATS
PAIRS = (TAPS + 1) // 2
TT = TILE * TILE
UNITS = [512, 512, 128]
GROUPS = [3, 3, 2]
EXPERTS, HID = 8, 256
HALVES = HID // P
BLOCK = 256
SUBS = BLOCK // P
IDLE = P * BANDS + BLOCK
REGION_BITS = 13
REGION = 1 << REGION_BITS
IDLE_ROW = (EXPERTS - 1) * REGION + IDLE
assert IDLE + BLOCK <= REGION
BLOCKS = (2 * P * BANDS + EXPERTS * (BLOCK - 1)) // BLOCK
ROW = C + 1
W_UP = HID + HALVES
WROW = W_UP + HALVES * C + C
RING = 4
SP_PADS = EXPERTS // 2
GB = 4
BACK = 4
T_RANK, T_REGION, T_THRESH = 0, EXPERTS, 2 * EXPERTS
T_TRI = T_THRESH + P * BANDS // BLOCK
T_BLK = T_TRI + EXPERTS * EXPERTS
T_BLKROW = T_BLK + BLOCKS
T_COLS = T_BLKROW + BLOCKS
LN_C_EPS, LN_T_EPS = 1e-6, 1e-5
N_CONSTS = 9
N_CLEARED = 10
SLOW_LINKS = 55


def window_constants():
    import numpy as np

    p = np.arange(P)
    dy, dx = (p % TT) // TILE, p % TILE
    tile = p // TT
    k = np.arange(TAPS)
    ky, kx = k // 3 - 1, k % 3 - 1
    j = np.arange(WIN)
    rel = np.zeros((P, TAPS, 2, WIN), np.float32)
    rel[:, :, 0, :] = (dy[:, None] + ky[None, :] + HALO)[:, :, None] - j
    rel[:, :, 1, :] = (dx[:, None] + kx[None, :] + HALO)[:, :, None] - j
    spread = np.zeros((2, PARTS, 2, WIN, 2, 2, Q), np.float32)
    q = np.arange(Q)
    for odd in range(2):
        for part in range(PARTS):
            spread[odd, part, 0, q // WIN, odd, 0, q] = 1
            spread[odd, part, 1, q % WIN, odd, 1, q] = 1
    spread = spread.reshape(2 * SLOT, 4 * Q)
    fold = np.zeros((4, 32, OFFS), np.float32)
    fold[:, np.arange(OFFS), np.arange(OFFS)] = 1
    base = np.zeros((BANDS, P, 2 * TAPS + 2), np.float32)
    for b in range(BANDS):
        base[b, :, 0:TAPS] = (TILE * (b % BPI) + dy)[:, None] + ky + HALO
        base[b, :, TAPS:2 * TAPS] = (TILE * tile + dx)[:, None] + kx + HALO
        base[b, :, 2 * TAPS:] = (b // BPI) * PADDED * PADDED
    e = np.arange(EXPERTS)
    table = np.concatenate([
        e, e * REGION, np.arange(P * BANDS // BLOCK) * BLOCK, np.tril(np.ones((EXPERTS, EXPERTS))).ravel(),
        np.arange(BLOCKS), np.arange(BLOCKS) * BLOCK]).astype(np.float32)
    token = np.arange(BANDS)[None, :, None] * P + p[:, None, None]
    dest = (token + np.arange(2) * (P * BANDS)).astype(np.int32)
    padding = np.zeros((P, SUBS, ROW), np.int32)
    padding[:, :, C] = 2 * P * BANDS + np.arange(SUBS) * P + p[:, None]
    return {
        "rel": rel.reshape(P, TAPS * HATS),
        "spread": spread,
        "fold": fold.reshape(P, OFFS),
        "base": base,
        "ident": np.eye(P, dtype=np.float32),
        "before": np.triu(np.ones((P, P), np.float32), 1),
        "table": np.broadcast_to(table, (P, T_COLS)).copy(),
        "dest": dest,
        "padding": padding,
    }


def program(nc, x_rows, x_tiles, w_offset, b_offset, filt, gate_w, gate_b, experts,
            rel, spread, fold, base, ident, before, table, dest, padding, out):
    with ExitStack() as ctx:
        def sb(name, shape, dt=F32):
            return ctx.enter_context(nc.sbuf_tensor(name, shape, dt))

        def sem(name):
            return ctx.enter_context(nc.semaphore(name))

        xpad = nc.dram_tensor("xpad", [IMAGES, PADDED, PADDED, C], F32, kind="Internal").ap()
        routed = nc.dram_tensor("routed", [EXPERTS * REGION, ROW], F32, kind="Internal").ap()
        result = nc.dram_tensor("result", [2 * P * BANDS + BLOCK, C], F32, kind="Internal").ap()

        rel_sb = sb("rel_sb", [P, TAPS * HATS])
        spread_f = sb("spread_f", [2 * SLOT, 4, Q])
        spread_sb = sb("spread_sb", [2 * SLOT, 4, Q], BF16)
        fold_sb = sb("fold_sb", [P, OFFS])
        ident_sb = sb("ident_sb", [P, P])
        identb_sb = sb("identb_sb", [P, P], BF16)
        before_f = sb("before_f", [P, P])
        before_sb = sb("before_sb", [P, P], BF16)
        every_sb = sb("every_sb", [P, P], BF16)
        table_sb = sb("table_sb", [P, T_COLS])
        dest_sb = sb("dest_sb", [P, BANDS, 2], I32)
        padding_sb = sb("padding_sb", [P, SUBS, ROW], I32)
        woff_sb = sb("woff_sb", [C, TAPS, 32])
        boff_sb = sb("boff_sb", [P, OFFS])
        filt_sb = sb("filt_sb", [C, TAPS, C])
        gw_sb = sb("gw_sb", [C, EXPERTS])
        gb_sb = sb("gb_sb", [P, EXPERTS])
        w_all = sb("w_all", [P, EXPERTS, WROW])
        eps_c = sb("eps_c", [P, 1])
        eps_t = sb("eps_t", [P, 1])
        ones = sb("ones", [P, 1])
        warm = sb("warm", [P, 1])
        zero = sb("zero", [BORDER_ROWS, 2 * HALO * C])

        wide = sb("wide", [P, 4 * TAPS * C])
        x_nat = wide[:, 0:BANDS * C].rearrange("p (b c) -> p b c", c=C)
        x1 = sb("x1", [P, BANDS, C])
        xnT = sb("xnT", [C, 2, SIDE + 2, SIDE + 2])
        offs = sb("offs", [P, BANDS, OFFS])
        mask = sb("mask", [P, BANDS, TAPS, 2])
        top_all = sb("top_all", [P, BANDS, EXPERTS])

        st8 = sb("st8", [P, BANDS, 6])
        mv8 = sb("mv8", [P, BANDS, 2])
        sd8 = sb("sd8", [P, BANDS])
        rs8 = sb("rs8", [P, BANDS])
        conv_sb = sb("conv_sb", [P, 2, 512])
        near = sb("near", [P, BANDS * 2 * TAPS])
        near_n = sb("near_n", [P, IMAGES])
        far = sb("far", [1, 1], I32)
        dist = sb("dist", [P, 2, TAPS * HATS])
        tent = sb("tent", [P, 2, TAPS * HATS])
        hat = sb("hat", [P, 2, TAPS * HATS])
        rest = sb("rest", [P, 2, TAPS * HATS])
        hat3 = sb("hat3", [P, 2, TAPS + 1, SLOT], BF16)
        hatT = sb("hatT", [2 * SLOT, PAIRS, P], BF16)
        ysp = sb("ysp", [Q, 2, 512])
        S = sb("S", [Q, 2, TAPS * P])
        xwin = sb("xwin", [Q, 2, TILES, C])
        samp = sb("samp", [C, 2, TAPS, P])
        st1 = sb("st1", [P, 2, 6])
        mv1 = sb("mv1", [P, 2, 2])
        sd1 = sb("sd1", [P, 2])
        rs1 = sb("rs1", [P, 2])
        xn2 = sb("xn2", [P, 2, C])
        xn2T = sb("xn2T", [C, 2, P])

        base_sb = sb("base_sb", [P, 2 * TAPS + 2])
        pos = sb("pos", [P, 2 * TAPS])
        posi = sb("posi", [P, 2 * TAPS], I32)
        posf = sb("posf", [P, 2 * TAPS])
        over = sb("over", [P, 2 * TAPS])
        low = sb("low", [P, 2 * TAPS])
        frac = sb("frac", [P, 2, 2, TAPS])
        line = sb("line", [P, TAPS])
        cell = sb("cell", [P, 4, TAPS])
        idx = sb("idx", [P, 4, TAPS], U32)
        wx = sb("wx", [P, 2, TAPS])
        cw = sb("cw", [P, 4, TAPS])
        corner = wide[:, :].rearrange("p (q k c) -> p q k c", q=4, k=TAPS)
        gsum = sb("gsum", [P, TAPS, C])

        lg = sb("lg", [P, 2, EXPERTS])
        top = sb("top", [P, 2, EXPERTS])
        topi = sb("topi", [P, 2, EXPERTS], U32)
        chosen = sb("chosen", [P, 2, 2, EXPERTS])
        both = sb("both", [P, 2, EXPERTS], BF16)
        seen = sb("seen", [P, 2, EXPERTS], BF16)
        place = sb("place", [P, EXPERTS])
        placed = sb("placed", [P, 2, EXPERTS])
        slot_f = sb("slot_f", [P, 2])
        slot = sb("slot", [P, 2, 2], U32)
        payload = sb("payload", [P, 2, 2, ROW])
        e_all = sb("e_all", [P, BANDS, EXPERTS])
        e_sum = sb("e_sum", [P, BANDS])
        share = sb("share", [P, 2, BANDS])
        count = sb("count", [1, EXPERTS])
        over_t = sb("over_t", [1, EXPERTS, P * BANDS // BLOCK])
        nblk = sb("nblk", [1, EXPERTS])
        tri_t = sb("tri_t", [1, EXPERTS, EXPERTS])
        upto = sb("upto", [1, EXPERTS])
        past = sb("past", [1, BLOCKS, EXPERTS])
        past_n = sb("past_n", [1, BLOCKS, EXPERTS])
        blk_e = sb("blk_e", [1, BLOCKS])
        blk_first = sb("blk_first", [1, BLOCKS])
        blk_row = sb("blk_row", [1, BLOCKS])
        blk_i = sb("blk_i", [1, BLOCKS], I32)
        pad_row = sb("pad_row", [1, EXPERTS], I32)

        w_blk = sb("w_blk", [P, RING, WROW])
        rows_in = sb("rows_in", [P, RING, SUBS, ROW])
        to = sb("to", [P, RING, SUBS], I32)
        rowsT = sb("rowsT", [C, RING, BLOCK])
        hid = sb("hid", [P, RING, HALVES, BLOCK])
        y = sb("y", [P, RING, SUBS, C])
        y_back = wide[:, 0:BACK * 2 * GB * C].rearrange("p (r c2 b c) -> p r c2 b c", r=BACK, c2=2, b=GB)
        res = sb("res", [P, BACK, GB, C])

        bank = [ctx.enter_context(nc.psum_tensor(f"bank{n}", [P, 512], F32)) for n in range(8)]
        bank4b = bank[4][:, :].bitcast(BF16)

        S_ = {}
        for name in (
            "settled tables_ready zeroed border_written x_in_0 x_in_1 x_in_2 x_in_3 x1_loaded experts_loaded early_loaded consts_loaded "
            "stats8 std8 rstd8 xn_ready xn_stored_first xn_stored_rest xnT_psum xnT_ready conv_psum conv_ready fold_psum "
            "offs_ready mask_ready near_ready near_psum far_ready dve_stat8 dve_hat dve_stat dve_rstd dve_slow "
            "pool_step dist_ready hat_ready hi_ready hat3_ready hatT_psum hatT_ready y_psum x_psum y_ready S_ready "
            "win_even win_odd samp_psum samp_act e_psum x1_ready std1_ready mean1_ready xn2_ready "
            "t_psum xn2T_ready l_psum base_free base_loaded idx_ready gathered gsum_ready g_psum samp_slow "
            "route stashed place_psum place_ready placed_ready slot_f_ready slot_ready payload_ready scat_even scat_odd "
            "exp_in exp_out warmed share_step count_psum plan_step pad_ready plan_ready idle_written pads_written "
            "rows_in_0 rows_in_1 rows_in_2 rows_in_3 w_in_0 w_in_1 w_in_2 w_in_3 rowsT_psum rowsT_ready h_psum h_ready y_psum2 to_ready y_done "
            "back_0 back_1 back_2 back_3 sent_0 sent_1 sent_2 sent_3 scaled res_step res_ready stored_0 stored_1 stored_2 stored_3"
        ).split():
            S_[name] = sem(name)
        s = type("Sems", (), S_)

        block = ctx.enter_context(nc.Block())

        def image_view(bank_ap):
            return bank_ap.rearrange("c (r w) -> c r w", w=SIDE)

        HEAD, STRIDE = 4, 4
        STRIDES = (BANDS - HEAD - 3) // STRIDE
        TAIL = HEAD + STRIDE * STRIDES

        def band_loop(eng, step):
            for b in range(HEAD):
                step(b, b % 2, b // 2 + 1)
            with eng.Fori(0, STRIDES) as i:
                for place in range(STRIDE):
                    step(i * STRIDE + (HEAD + place), place % 2, i * 2 + ((HEAD + place) // 2 + 1))
            for b in range(TAIL, BANDS):
                step(b, b % 2, b // 2 + 1)

        def settle(eng):
            eng.sem_inc(s.settled, 1)

        def block_at(turn, place):
            return turn * RING + place, place % RING, turn + place // RING

        TURNS = BLOCKS // RING
        REST = BLOCKS - TURNS * RING

        def block_loop(eng, step):
            for place in range(RING):
                step(0, place)
            with eng.Fori(1, TURNS) as turn:
                for place in range(RING):
                    step(turn, place)
            for place in range(REST):
                step(TURNS, place)

        def previous(turn, place):
            return (turn - 1, RING - 1) if place == 0 else (turn, place - 1)

        def is_first(turn, place):
            return isinstance(turn, int) and turn * RING + place == 0

        def is_last(turn, place):
            return isinstance(turn, int) and turn * RING + place == BLOCKS - 1

        rows_arrived = (s.rows_in_0, s.rows_in_1, s.rows_in_2, s.rows_in_3)
        w_arrived = (s.w_in_0, s.w_in_1, s.w_in_2, s.w_in_3)
        sent = (s.sent_0, s.sent_1, s.sent_2, s.sent_3)
        back_arrived = (s.back_0, s.back_1, s.back_2, s.back_3)
        stored = (s.stored_0, s.stored_1, s.stored_2, s.stored_3)

        x_arrived = (s.x_in_0, s.x_in_1, s.x_in_2, s.x_in_3)

        def image_rows(m):
            return x_nat[:, m * BPI:(m + 1) * BPI, :]

        def rows_of(ap, n):
            return ap.rearrange("(one o) -> one o", one=1).broadcast_to([P, n])

        def write_padding(eng, e):
            row = eng.value_load(pad_row[0:1, e:e + 1], min_val=e * REGION, max_val=e * REGION + P * BANDS)
            eng.dma_start(routed[bass.ds(row, BLOCK), :].rearrange("(j p) w -> p j w", p=P),
                          padding_sb[:, :, :].bitcast(F32)).then_inc(s.pads_written, 16)

        def is_far(eng):
            eng.wait_ge(s.far_ready, 1)
            return eng.value_load(far[0:1, 0:1], min_val=0, max_val=1)

        def at_least(eng, semaphore, value):
            if not isinstance(value, int) or value > 0:
                eng.wait_ge(semaphore, value)

        @block.sync
        def _(sp):
            def load(dst, src):
                sp.dma_start(dst, src).then_inc(s.consts_loaded, 16)

            def load_consts():
                load(rel_sb[:, :], rel)
                load(spread_f[:, :, :], spread.rearrange("r (f q) -> r f q", f=4))
                load(before_f[:, :], before)
                load(table_sb[:, :], table)
                load(dest_sb[:, :, :], dest)
                load(padding_sb[:, :, :], padding)
                load(filt_sb[:, :, :], filt)
                load(gw_sb[:, :], gate_w)
                load(gb_sb[:, :], rows_of(gate_b, EXPERTS))

            for m in range(IMAGES):
                sp.dma_start(image_rows(m), x_rows[m * BPI:(m + 1) * BPI].rearrange("b p c -> p b c")
                             ).then_inc(x_arrived[m], 16)
            sp.wait_ge(s.zeroed, 1)
            flat = xpad.rearrange("m r w c -> (m r w c)")
            row, edge = PADDED * C, HALO * C
            rest = HALO * row - edge
            for m in range(IMAGES):
                first = m * PADDED * row + HALO * row - edge
                sp.dma_start(flat[first:first + (SIDE + 1) * row].rearrange("(r n) -> r n", n=row)[:, 0:2 * edge],
                             zero[0:SIDE + 1, :]).then_inc(s.border_written, 16)
            for m in range(IMAGES + 1):
                lo = max(m * PADDED * row - rest, 0)
                hi = min(m * PADDED * row + rest, IMAGES * PADDED * row)
                sp.dma_start(flat[lo:hi].rearrange("(r n) -> r n", r=BORDER_ROWS), zero[:, 0:(hi - lo) // BORDER_ROWS]
                             ).then_inc(s.border_written, 16)
            for m in range(IMAGES):
                sp.wait_ge(s.xn_ready, (m + 1) * BPI)
                rows = xpad[m, HALO:HALO + SIDE, HALO:HALO + SIDE, :].rearrange("(b r) w c -> r w b c", r=TILE)
                for r in range(TILE):
                    sp.dma_start(rows[r], image_rows(m)[SIDE * r:SIDE * (r + 1)]
                                 ).then_inc(s.xn_stored_first if m == 0 else s.xn_stored_rest, 16)
                if m == 0:
                    load_consts()
            sp.wait_ge(s.border_written, 16 * (2 * IMAGES + 1))
            sp.wait_ge(s.xn_stored_first, 16 * TILE)

            def load_windows(b, par, image, row):
                at_least(sp, s.samp_psum, 3 * (b - 1))
                for t in range(TILES):
                    sp.dma_start(xwin[:, par, t, :], xpad[image, bass.ds(row, WIN), TILE * t:TILE * t + WIN, :]
                                 ).then_inc((s.win_even, s.win_odd)[par], 16)

            load_windows(0, 0, 0, 0)
            load_windows(1, 1, 0, TILE)
            sp.dma_start(x1[:, :, :], x_tiles.rearrange("b p c -> p b c")).then_inc(s.x1_loaded, 16)
            sp.wait_ge(s.xn_stored_rest, 16 * TILE * (IMAGES - 1))

            sp.wait_ge(s.consts_loaded, 16 * N_CONSTS)
            sp.dma_start(routed[IDLE_ROW:IDLE_ROW + BLOCK, :].rearrange("(j p) w -> p j w", p=P),
                         padding_sb[:, :, :].bitcast(F32)).then_inc(s.idle_written, 16)

            def load_experts(e):
                sp.dma_start(w_all[:, bass.ds(e, 2), :], experts[:, bass.ds(e, 2), :]).then_inc(s.experts_loaded, 16)

            load_experts(0)
            flag = is_far(sp)
            with sp.If(flag):
                with sp.Fori(0, BANDS) as b:
                    sp.wait_ge(s.base_free, b + 1)
                    sp.dma_start(base_sb[:, :], base[b]).then_inc(s.base_loaded, 16)
                with sp.Fori(1, IMAGES) as m:
                    load_experts(m * 2)
            with sp.Else():
                for b in range(2, BPI):
                    load_windows(b, b % 2, 0, TILE * b)
                with sp.Fori(1, IMAGES) as m:
                    load_experts(m * 2)
                    for r in range(BPI):
                        load_windows(m * BPI + r, r % 2, m, TILE * r)

            sp.wait_ge(s.pad_ready, 1)
            for e in range(SP_PADS):
                write_padding(sp, e)

            def first_row(turn, place):
                i = turn * RING + place
                return sp.value_load(blk_i[0:1, bass.ds(i, 1)], min_val=0, max_val=IDLE_ROW)

            def load_weights(turn, place, row):
                i, slot, uses = block_at(turn, place)
                expert = nc.s_assert_within(row >> REGION_BITS, 0, EXPERTS - 1)
                at_least(sp, s.y_done, i - (RING - 1))
                sp.dma_start(w_blk[:, slot, :], w_all[:, expert, :]).then_inc(w_arrived[slot], 16)

            def load_rows(turn, place, row):
                i, slot, uses = block_at(turn, place)
                at_least(sp, s.rowsT_psum, i - (RING - 1))
                at_least(sp, s.to_ready, i - (RING - 1))
                sp.dma_start(rows_in[:, slot, :, :], routed[bass.ds(row, BLOCK), :].rearrange("(j p) w -> p j w", p=P)
                             ).then_inc(rows_arrived[slot], 16)

            def load_blocks(turn, places):
                row = first_row(turn, places[0])
                for place in places:
                    after = None if is_last(turn, place) else first_row(turn, place + 1)
                    load_weights(turn, place, row)
                    if after is not None:
                        load_rows(turn, place + 1, after)
                    row = after

            sp.wait_ge(s.experts_loaded, 16 * (EXPERTS // 2))
            sp.wait_ge(s.plan_ready, 1)
            row = first_row(0, 0)
            load_weights(0, 0, row)
            sp.wait_ge(s.idle_written, 16)
            sp.wait_ge(s.scat_even, 32 * (BANDS // 2))
            sp.wait_ge(s.scat_odd, 32 * (BANDS // 2))
            sp.wait_ge(s.pads_written, 16 * EXPERTS)
            load_rows(0, 0, row)
            load_rows(0, 1, first_row(0, 1))
            load_blocks(0, range(1, RING))
            assert TURNS % 2 == 1
            with sp.Fori(0, TURNS // 2) as i:
                load_blocks(i * 2 + 1, range(2 * RING))
            load_blocks(TURNS, range(REST))

            for slot in range(RING):
                sp.wait_ge(sent[slot], 16 * SUBS * (TURNS + (slot < REST)))
            back = result[0:2 * P * BANDS, :].rearrange("(c g b p) d -> c g p b d", c=2, b=GB, p=P)
            out_v = out.rearrange("(g b) p c -> g p b c", b=GB)

            def load_back(g):
                for c2 in range(2):
                    sp.dma_start(y_back[:, g % BACK, c2], back[c2, g]).then_inc(back_arrived[g % BACK], 16)

            for g in range(BACK):
                load_back(g)
            for g in range(BANDS // GB):
                sp.wait_ge(s.res_ready, g + 1)
                sp.dma_start(out_v[g], res[:, g % BACK, :, :]).then_inc(stored[g % BACK], 16)
                if g + BACK < BANDS // GB:
                    load_back(g + BACK)
            for slot in range(BACK):
                sp.wait_ge(stored[slot], 16 * (BANDS // GB // BACK))

        @block.gpsimd
        def _(pool):
            nc.gpsimd.memset(zero[:, :], 0.0).then_inc(s.zeroed, 1)
            nc.gpsimd.memset(woff_sb[:, :, :], 0.0).then_inc(s.zeroed, 1)
            nc.gpsimd.memset(eps_c[:, :], LN_C_EPS).then_inc(s.zeroed, 1)
            nc.gpsimd.memset(ones[:, :], 1.0).then_inc(s.zeroed, 1)
            nc.gpsimd.memset(xnT[:, :, :, :], 0.0).then_inc(s.zeroed, 1)
            nc.gpsimd.memset(eps_t[:, :], LN_T_EPS).then_inc(s.zeroed, 1)
            nc.gpsimd.memset(mask[:, :, :, :], 1.0).then_inc(s.zeroed, 1)
            nc.gpsimd.memset(hat3[:, :, TAPS, :], 0.0).then_inc(s.zeroed, 1)
            nc.gpsimd.memset(every_sb[:, :], 1.0).then_inc(s.zeroed, 1)
            nc.gpsimd.memset(seen[:, 0, :], 0.0).then_inc(s.zeroed, 1)

            pool.wait_ge(s.early_loaded, 16 * 4)
            pool.wait_ge(s.consts_loaded, 16 * N_CONSTS)
            nc.gpsimd.tensor_copy(spread_sb[:, :, :], spread_f[:, :, :]).then_inc(s.tables_ready, 1)
            nc.gpsimd.tensor_copy(identb_sb[:, :], ident_sb[:, :]).then_inc(s.tables_ready, 1)
            nc.gpsimd.tensor_copy(before_sb[:, :], before_f[:, :]).then_inc(s.tables_ready, 1)

            def distances(b, par):
                o = offs[:, b, 0:2 * TAPS].rearrange("p (yx k one) -> p k yx one", yx=2, one=1)
                d = dist[:, par, :].rearrange("p (k yx j) -> p k yx j", k=TAPS, yx=2)
                r = rel_sb[:, :].rearrange("p (k yx j) -> p k yx j", k=TAPS, yx=2)
                nc.gpsimd.tensor_tensor(d, o.broadcast_to([P, TAPS, 2, WIN]), r, ALU.add
                                        ).then_inc(s.dist_ready, 1)

            def split(b, par):
                h3 = hat3[:, par, 0:TAPS, :].rearrange("p k (part h) -> p part k h", part=PARTS)
                h = hat[:, par, :].rearrange("p (k h) -> p k h", k=TAPS)
                r = rest[:, par, :].rearrange("p (k h) -> p k h", k=TAPS)
                pool.wait_ge(s.hi_ready, b + 1)
                nc.gpsimd.tensor_tensor(r, h, h3[:, 0], ALU.subtract).then_inc(s.pool_step, 1)
                nc.gpsimd.tensor_tensor(h3[:, 1], h, h3[:, 0], ALU.subtract).then_inc(s.pool_step, 1)
                pool.wait_ge(s.pool_step, b * 2 + 2)
                nc.gpsimd.tensor_tensor(h3[:, 2], r, h3[:, 1], ALU.subtract).then_inc(s.hat3_ready, 1)

            def pack(b, par):
                pool.wait_ge(s.xn2_ready, b + 1)
                settle(pool)
                at_least(pool, (s.scat_even, s.scat_odd)[par], (b // 2) * 32 if isinstance(b, int) else (b - par) * 16)
                if not isinstance(b, int):
                    settle(pool)
                nc.gpsimd.tensor_copy(payload[:, par, :, 0:C], xn2[:, par, :].unsqueeze(1).broadcast_to([P, 2, C])
                                      ).then_inc(s.payload_ready, 1)
                nc.gpsimd.tensor_copy(payload[:, par, :, C:C + 1].bitcast(I32), dest_sb[:, b, :].unsqueeze(2)
                                      ).then_inc(s.payload_ready, 1)

            def scatter(b, par):
                pool.wait_ge(s.slot_ready, b + 1)
                settle(pool)
                pool.wait_ge(s.payload_ready, b * 2 + 2)
                settle(pool)
                for c2 in range(2):
                    nc.gpsimd.indirect_dma_start(
                        routed, bass.IndirectOffsetOnAxis(slot[:, par, c2:c2 + 1], 0), payload[:, par, c2, :], None
                    ).then_inc((s.scat_even, s.scat_odd)[par], 16)

            pool.wait_ge(s.offs_ready, 1)
            distances(0, 0)
            distances(1, 1)
            split(0, 0)
            split(1, 1)
            pool.wait_ge(s.offs_ready, IMAGES)
            flag = is_far(pool)
            with pool.If(flag):
                def gather(b, par):
                    pool.wait_ge(s.idx_ready, b + 1)
                    settle(pool)
                    for c4 in range(4):
                        for k in range(TAPS):
                            nc.gpsimd.indirect_dma_start(
                                corner[:, c4, k, :], None, xpad.rearrange("m r w c -> (m r w) c"),
                                bass.IndirectOffsetOnAxis(idx[:, c4, k:k + 1], 0)).then_inc(s.gathered, 16)
                    pack(b, par)
                    scatter(b, par)

                for b in range(2):
                    gather(b, b)
                with pool.Fori(1, BANDS // 2) as i:
                    gather(i * 2, 0)
                    gather(i * 2 + 1, 1)
            with pool.Else():
                distances(2, 0)

                def step(b, par, _):
                    known = isinstance(b, int)
                    if not known or b + 2 < BANDS:
                        split(b + 2, par)
                    if not known or b + 3 < BANDS:
                        distances(b + 3, 1 - par)
                    if not known or b >= 3:
                        scatter(b - 3, 1 - par)
                    if not known or b >= 2:
                        pack(b - 2, par)

                band_loop(pool, step)
                scatter(BANDS - 3, 1)
                pack(BANDS - 2, 0)
                pack(BANDS - 1, 1)
                scatter(BANDS - 2, 0)
                scatter(BANDS - 1, 1)

            def send(turn, place):
                i, slot, uses = block_at(turn, place)
                pool.wait_ge(s.y_done, i + 1)
                pool.wait_ge(s.to_ready, i + 1)
                settle(pool)
                for j in range(SUBS):
                    nc.gpsimd.indirect_dma_start(
                        result, bass.IndirectOffsetOnAxis(to[:, slot, j:j + 1].bitcast(U32), 0), y[:, slot, j, :],
                        None, bounds_check=2 * P * BANDS - 1, oob_is_err=False
                    ).then_inc(sent[slot], 16)

            with pool.Fori(0, TURNS) as turn:
                for place in range(RING):
                    send(turn, place)
            for place in range(REST):
                send(TURNS, place)

        @block.scalar
        def _(act):
            def load(dst, src, loaded):
                act.dma_start(dst, src).then_inc(loaded, 16)

            early = s.early_loaded
            load(ident_sb[:, :], ident, early)
            act.wait_ge(s.zeroed, 2)
            load(woff_sb[:, :, 0:OFFS], w_offset.rearrange("a b c o -> c (a b) o"), early)
            load(boff_sb[:, :], rows_of(b_offset, OFFS), early)
            load(fold_sb[:, :], fold, early)

            def std_image(m):
                act.wait_ge(s.stats8, m * BPI + BPI)
                bands = slice(m * BPI, (m + 1) * BPI)
                nc.scalar.activation(sd8[:, bands], mv8[:, bands, 1], ACT.Sqrt, bias=eps_c[:, :]).then_inc(s.std8, 1)

            def evacuate_xnT(m):
                at_least(act, s.conv_psum, (m - 1) * 2)
                for h in range(2):
                    act.wait_ge(s.xnT_psum, m * 2 + h + 1)
                    nc.scalar.activation(xnT[:, m % 2, 1 + 16 * h:17 + 16 * h, 1:1 + SIDE], image_view(bank[h][:, :]),
                                         ACT.Copy).then_inc(s.xnT_ready, 1)

            def evacuate_conv(m, h):
                at_least(act, s.fold_psum, m * 2 + h - 1)
                act.wait_ge(s.conv_psum, m * 2 + h + 1)
                for b in range(4):
                    nc.scalar.activation(
                        conv_sb[:, h, b * P:(b + 1) * P].rearrange("g (t dy dx) -> g t dy dx", t=TILES, dy=TILE),
                        bank[2 + h][:, b * P:(b + 1) * P].rearrange("g (dy t dx) -> g t dy dx", dy=TILE, t=TILES),
                        ACT.Copy).then_inc(s.conv_ready, 1)

            def mask_image(m):
                act.wait_ge(s.offs_ready, m + 1)
                bands = slice(m * BPI, (m + 1) * BPI)
                nc.scalar.activation(mask[:, bands, :, 1], offs[:, bands, 2 * TAPS:], ACT.Sigmoid).then_inc(s.mask_ready, 1)

            act.wait_ge(s.zeroed, 4)
            nc.scalar.activation(warm[:, :], ones[:, :], ACT.Sqrt).then_inc(s.warmed, 1)
            std_image(0)
            act.wait_ge(s.zeroed, N_CLEARED)
            evacuate_xnT(0)
            std_image(1)
            for m in range(IMAGES):
                if m + 2 < IMAGES:
                    std_image(m + 2)
                evacuate_conv(m, 0)
                evacuate_conv(m, 1)
                if m + 1 < IMAGES:
                    evacuate_xnT(m + 1)
                if m == IMAGES - 2:
                    mask_image(0)

            def hi_part(b, par):
                act.wait_ge(s.hat_ready, b + 1)
                nc.scalar.activation(hat3[:, par, 0:TAPS, 0:HATS],
                                     hat[:, par, :].rearrange("p (k h) -> p k h", k=TAPS),
                                     ACT.Copy).then_inc(s.hi_ready, 1)

            def evacuate_hatT(b):
                act.wait_ge(s.hatT_psum, b + 1)
                nc.scalar.activation(hatT[:, :, :],
                                     bank4b[0:2 * SLOT, 0:PAIRS * P].rearrange("r (i t) -> r i t", i=PAIRS),
                                     ACT.Copy).then_inc(s.hatT_ready, 1)

            def copy_y(b, par, u):
                act.wait_ge(s.y_psum, b * 3 + u + 1)
                at_least(act, s.S_ready, b * 3 + u - 1)
                slot, n = (par + u) % 2, UNITS[u]
                nc.scalar.activation(ysp[:, slot, 0:n], bank[slot][0:Q, 0:n], ACT.Copy).then_inc(s.y_ready, 1)

            def sample_view(par, g):
                t0 = sum(GROUPS[:g])
                return samp[:, par, :, :].rearrange("c k (t p) -> c t k p", t=TILES)[:, t0:t0 + GROUPS[g]]

            def evacuate_samples(b, par, g):
                at_least(act, s.e_psum, b - 1)
                act.wait_ge(s.samp_psum, b * 3 + g + 1)
                nc.scalar.activation(
                    sample_view(par, g),
                    bank[5 + (par + g) % 2][:, 0:GROUPS[g] * TAPS * TT].rearrange(
                        "c (t k p) -> c t k p", k=TAPS, p=TT), ACT.Copy).then_inc(s.samp_act, 1)

            def std_band(b, par):
                act.wait_ge(s.mean1_ready, b + 1)
                nc.scalar.activation(sd1[:, par:par + 1], mv1[:, par, 1:2], ACT.Sqrt,
                                     bias=eps_t[:, :]).then_inc(s.std1_ready, 1)

            def evacuate_tokens(b, par):
                act.wait_ge(s.t_psum, b + 1)
                nc.scalar.activation(xn2T[:, par, :], bank[4][:, 0:P], ACT.Copy).then_inc(s.xn2T_ready, 1)

            hi_part(0, 0)
            hi_part(1, 1)
            evacuate_hatT(0)
            for m in range(1, IMAGES):
                mask_image(m)
            flag = is_far(act)
            with act.If(flag):
                with act.Fori(0, BANDS // 2) as i:
                    for par in range(2):
                        b = i * 2 + par
                        for k in range(TAPS):
                            act.wait_ge(s.g_psum, b * TAPS + k + 1)
                            nc.scalar.activation(samp[:, par, k, :], bank[k % 2][:, 0:P], ACT.Copy
                                                 ).then_inc(s.samp_slow, 1)
                        std_band(b, par)
                        evacuate_tokens(b, par)
            with act.Else():
                def step(b, par, _):
                    known = isinstance(b, int)
                    copy_y(b, par, 0)
                    copy_y(b, par, 1)
                    if not known or b >= 2:
                        evacuate_tokens(b - 2, par)
                    copy_y(b, par, 2)
                    evacuate_samples(b, par, 0)
                    if not known or b + 1 < BANDS:
                        evacuate_hatT(b + 1)
                    if not known or b >= 1:
                        std_band(b - 1, 1 - par)
                    evacuate_samples(b, par, 1)
                    if not known or b + 2 < BANDS:
                        hi_part(b + 2, par)
                    evacuate_samples(b, par, 2)

                band_loop(act, step)
                evacuate_tokens(BANDS - 2, 0)
                std_band(BANDS - 1, 1)
                evacuate_tokens(BANDS - 1, 1)

            act.wait_ge(s.pad_ready, 1)
            for e in range(SP_PADS, EXPERTS):
                write_padding(act, e)

            def evacuate_rows(turn, place):
                i, slot, uses = block_at(turn, place)
                act.wait_ge(s.rowsT_psum, i + 1)
                at_least(act, s.h_psum, i - (RING - 1))
                nc.scalar.activation(rowsT[:, slot, :], bank[slot][:, 0:BLOCK], ACT.Copy).then_inc(s.rowsT_ready, 1)

            def gelu(turn, place):
                i, slot, uses = block_at(turn, place)
                act.wait_ge(s.h_psum, i + 1)
                at_least(act, s.y_psum2, i - (RING - 1))
                for h in range(HALVES):
                    nc.scalar.activation(hid[:, slot, h, :], bank[RING + slot][:, h * BLOCK:(h + 1) * BLOCK], ACT.Gelu,
                                         bias=w_blk[:, slot, HID + h:HID + h + 1]).then_inc(s.h_ready, 1)

            def block_step(turn, place):
                if not is_last(turn, place):
                    evacuate_rows(turn, place + 1)
                gelu(turn, place)

            act.wait_ge(s.exp_in, 1)
            nc.scalar.activation(e_all[:, :, :], e_all[:, :, :], ACT.Exp).then_inc(s.exp_out, 1)
            nc.scalar.activation(warm[:, :], ones[:, :], ACT.Gelu).then_inc(s.warmed, 1)
            evacuate_rows(0, 0)
            block_loop(act, block_step)

            act.wait_ge(s.share_step, 3)
            for g in range(BANDS // GB):
                act.wait_ge(back_arrived[g % BACK], 32 * (g // BACK + 1))
                for j in range(GB):
                    second = y_back[:, g % BACK, 1, j, :]
                    nc.scalar.activation(second, second, ACT.Copy, scale=share[:, 1, g * GB + j:g * GB + j + 1]
                                         ).then_inc(s.scaled, 1)

        @block.vector
        def _(dve):
            def stats_image(m):
                dve.wait_ge(x_arrived[m], 16)
                bands = range(m * BPI, (m + 1) * BPI)
                for b in bands:
                    last = nc.vector.bn_stats(st8[:, b, :], x_nat[:, b, :])
                last.then_inc(s.dve_stat8, 1)
                dve.wait_ge(s.dve_stat8, m + 1)
                for b in bands:
                    nc.vector.bn_aggr(mv8[:, b, :], st8[:, b, :]).then_inc(s.stats8, 1)

            def normalise_image(m):
                bands = range(m * BPI, (m + 1) * BPI)
                dve.wait_ge(s.std8, m + 1)
                nc.vector.reciprocal(rs8[:, bands[0]:bands[-1] + 1], sd8[:, bands[0]:bands[-1] + 1]).then_inc(s.rstd8, 1)
                dve.wait_ge(s.rstd8, m + 1)
                for b in bands:
                    nc.vector.tensor_scalar(x_nat[:, b, :], x_nat[:, b, :], mv8[:, b, 0:1],
                                            rs8[:, b:b + 1], ALU.subtract, ALU.mult).then_inc(s.xn_ready, 1)

            def offsets_image(m):
                dve.wait_ge(s.fold_psum, m * 2 + 2)
                bands = slice(m * BPI, (m + 1) * BPI)
                nc.vector.tensor_tensor(
                    offs[:, bands, :], bank[5][:, 0:BPI * OFFS].rearrange("p (b o) -> p b o", o=OFFS),
                    boff_sb[:, :].unsqueeze(1).broadcast_to([P, BPI, OFFS]), ALU.add).then_inc(s.offs_ready, 1)
                dve.wait_ge(s.offs_ready, m + 1)
                n = BPI * 2 * TAPS
                within = near[:, m * n:(m + 1) * n]
                o = offs[:, bands, 0:2 * TAPS]
                nc.vector.tensor_tensor(within.rearrange("p (b o) -> p b o", b=BPI), o, o, ALU.mult
                                        ).then_inc(s.near_ready, 1)
                dve.wait_ge(s.near_ready, 3 * m + 1)
                nc.vector.tensor_scalar(within, within, float(REACH * REACH), None, ALU.is_le
                                        ).then_inc(s.near_ready, 1)
                dve.wait_ge(s.near_ready, 3 * m + 2)
                nc.vector.tensor_reduce(near_n[:, m:m + 1], within, AX_X, ALU.add).then_inc(s.near_ready, 1)

            def hats(b, par, link):
                if link == 0:
                    dve.wait_ge(s.dist_ready, b + 1)
                    nc.vector.scalar_tensor_tensor(tent[:, par, :], dist[:, par, :], -1.0, dist[:, par, :],
                                                   ALU.mult, ALU.max).then_inc(s.dve_hat, 1)
                elif link == 1:
                    dve.wait_ge(s.dve_hat, b * 2 + 1)
                    nc.vector.tensor_scalar(tent[:, par, :], tent[:, par, :], -1.0, 0.0, ALU.add, ALU.min
                                            ).then_inc(s.dve_hat, 1)
                else:
                    dve.wait_ge(s.dve_hat, b * 2 + 2)
                    nc.vector.tensor_tensor(
                        hat[:, par, :].rearrange("p (k j) -> p k j", j=WIN),
                        tent[:, par, :].rearrange("p (k j) -> p k j", j=WIN),
                        mask[:, b, :, :].rearrange("p k yx -> p (k yx)").unsqueeze(2).broadcast_to([P, 2 * TAPS, WIN]),
                        ALU.mult).then_inc(s.hat_ready, 1)

            def multiply(b, par, u):
                at_least(dve, s.samp_psum, (b - 1) * 3)
                dve.wait_ge(s.y_ready, b * 3 + u + 1)
                dve.wait_ge(s.x_psum, b * 3 + u + 1)
                slot, n, c0 = (par + u) % 2, UNITS[u], sum(UNITS[:u])
                nc.vector.tensor_tensor(S[:, par, c0:c0 + n], ysp[:, slot, 0:n], bank[2 + slot][0:Q, 0:n],
                                        ALU.mult).then_inc(s.S_ready, 1)

            def residual(b, par, link):
                if link == 0:
                    dve.wait_ge(s.e_psum, b + 1)
                    nc.vector.tensor_tensor(x1[:, b, :], x1[:, b, :], bank[7][:, 0:C], ALU.add).then_inc(s.x1_ready, 1)
                elif link == 1:
                    dve.wait_ge(s.x1_ready, b + 1)
                    settle(dve)
                    nc.vector.bn_stats(st1[:, par, :], x1[:, b, :]).then_inc(s.dve_stat, 1)
                else:
                    dve.wait_ge(s.dve_stat, b + 1)
                    settle(dve)
                    nc.vector.bn_aggr(mv1[:, par, :], st1[:, par, :]).then_inc(s.mean1_ready, 1)

            def normalise(b, par):
                dve.wait_ge(s.std1_ready, b + 1)
                nc.vector.reciprocal(rs1[:, par:par + 1], sd1[:, par:par + 1]).then_inc(s.dve_rstd, 1)
                dve.wait_ge(s.dve_rstd, b + 1)
                at_least(dve, s.t_psum, b - 1)
                at_least(dve, s.payload_ready, 2 * (b - 1))
                nc.vector.tensor_scalar(xn2[:, par, :], x1[:, b, :], mv1[:, par, 0:1], rs1[:, par:par + 1],
                                        ALU.subtract, ALU.mult).then_inc(s.xn2_ready, 1)

            CHAIN = 6

            def choose(b, par, link):
                if link == 0:
                    dve.wait_ge(s.l_psum, b + 1)
                    nc.vector.tensor_tensor(lg[:, par, :], bank[4][:, 0:EXPERTS], gb_sb[:, :], ALU.add
                                            ).then_inc(s.route, 1)
                    return
                dve.wait_ge(s.route, b * CHAIN + link)
                if link == 1:
                    settle(dve)
                    nc.vector.max(top[:, par, :], lg[:, par, :]).then_inc(s.route, 1)
                elif link == 2:
                    settle(dve)
                    nc.vector.max_index(topi[:, par, :], top[:, par, :], lg[:, par, :]).then_inc(s.route, 1)
                    nc.vector.tensor_copy(top_all[:, b, :], top[:, par, :]).then_inc(s.stashed, 1)
                elif link == 3:
                    nc.vector.tensor_tensor(
                        chosen[:, par, :, :],
                        table_sb[:, T_RANK:T_RANK + EXPERTS].unsqueeze(1).broadcast_to([P, 2, EXPERTS]),
                        topi[:, par, 0:2].unsqueeze(2).broadcast_to([P, 2, EXPERTS]), ALU.is_equal
                    ).then_inc(s.route, 1)
                elif link == 4:
                    nc.vector.tensor_tensor(both[:, par, :], chosen[:, par, 0, :], chosen[:, par, 1, :], ALU.add
                                            ).then_inc(s.route, 1)
                else:
                    at_least(dve, s.place_psum, b)
                    nc.vector.tensor_tensor(seen[:, 1 - par, :], seen[:, par, :], both[:, par, :], ALU.add
                                            ).then_inc(s.route, 1)

            def place_rows(b, par, link):
                if link == 0:
                    dve.wait_ge(s.place_psum, b + 1)
                    nc.vector.tensor_tensor(place[:, :], bank[7][:, 256:256 + EXPERTS],
                                            table_sb[:, T_REGION:T_REGION + EXPERTS], ALU.add).then_inc(s.place_ready, 1)
                elif link == 1:
                    dve.wait_ge(s.place_ready, b + 1)
                    nc.vector.tensor_tensor(placed[:, :, :], chosen[:, par, :, :],
                                            place[:, :].unsqueeze(1).broadcast_to([P, 2, EXPERTS]), ALU.mult
                                            ).then_inc(s.placed_ready, 1)
                elif link == 2:
                    dve.wait_ge(s.placed_ready, b + 1)
                    at_least(dve, s.slot_ready, b)
                    nc.vector.tensor_reduce(slot_f[:, :], placed[:, :, :], AX_X, ALU.add).then_inc(s.slot_f_ready, 1)
                else:
                    dve.wait_ge(s.slot_f_ready, b + 1)
                    if not isinstance(b, int) or b >= 2:
                        dve.wait_ge((s.scat_even, s.scat_odd)[par],
                                    (b // 2) * 32 if isinstance(b, int) else (b - par) * 16)
                    nc.vector.tensor_copy(slot[:, par, :], slot_f[:, :]).then_inc(s.slot_ready, 1)

            def run(chain, b, par, links):
                for link in links:
                    chain(b, par, link)

            for m in range(IMAGES):
                stats_image(m)
                normalise_image(m)
            dve.wait_ge(s.early_loaded, 16 * 4)
            for m in range(IMAGES - 1):
                offsets_image(m)
            dve.wait_ge(s.mask_ready, 1)
            dve.wait_ge(s.zeroed, N_CLEARED)
            for b in range(2):
                for link in range(3):
                    hats(b, b, link)
            offsets_image(IMAGES - 1)
            dve.wait_ge(s.near_psum, 1)
            nc.vector.tensor_scalar(far[:, :], bank[6][0:1, 0:1], float(P * BANDS * 2 * TAPS), None,
                                    ALU.is_lt).then_inc(s.far_ready, 1)
            dve.wait_ge(s.mask_ready, IMAGES)
            dve.wait_ge(s.consts_loaded, 16 * N_CONSTS)
            dve.wait_ge(s.x1_loaded, 16)
            flag = is_far(dve)
            with dve.If(flag):
                def gathered_band(b, par):
                    n = [0]

                    def link(ins, total=SLOW_LINKS):
                        ins.then_inc(s.dve_slow, 1)
                        n[0] += 1
                        dve.wait_ge(s.dve_slow, b * total + n[0])

                    dve.wait_ge(s.base_loaded, b * 16 + 16)
                    link(nc.vector.tensor_tensor(pos[:, :], offs[:, b, 0:2 * TAPS], base_sb[:, 0:2 * TAPS], ALU.add))
                    link(nc.vector.tensor_scalar(pos[:, :], pos[:, :], 1.0, float(PADDED - 2), ALU.max, ALU.min))
                    link(nc.vector.tensor_copy(posi[:, :], pos[:, :]))
                    link(nc.vector.tensor_copy(posf[:, :], posi[:, :]))
                    link(nc.vector.tensor_tensor(over[:, :], posf[:, :], pos[:, :], ALU.is_gt))
                    link(nc.vector.tensor_tensor(low[:, :], posf[:, :], over[:, :], ALU.subtract))
                    fr1 = frac[:, :, 1, :]
                    link(nc.vector.tensor_tensor(fr1, pos[:, :].rearrange("p (a k) -> p a k", a=2),
                                                 low[:, :].rearrange("p (a k) -> p a k", a=2), ALU.subtract))
                    link(nc.vector.tensor_scalar(frac[:, :, 0, :], fr1, -1.0, 1.0, ALU.mult, ALU.add))
                    link(nc.vector.scalar_tensor_tensor(line[:, :], low[:, 0:TAPS], float(PADDED),
                                                        low[:, TAPS:2 * TAPS], ALU.mult, ALU.add))
                    for c4 in range(4):
                        link(nc.vector.tensor_scalar(cell[:, c4, :], line[:, :], base_sb[:, 2 * TAPS:2 * TAPS + 1],
                                                     float((c4 // 2) * PADDED + c4 % 2), ALU.add, ALU.add))
                    nc.vector.tensor_copy(idx[:, :, :], cell[:, :, :]).then_inc(s.idx_ready, 1)
                    for a in range(2):
                        link(nc.vector.tensor_tensor(wx[:, a, :], frac[:, 1, a, :], mask[:, b, :, 1], ALU.mult))
                    for c4 in range(4):
                        link(nc.vector.tensor_tensor(cw[:, c4, :], frac[:, 0, c4 // 2, :], wx[:, c4 % 2, :], ALU.mult))
                    dve.wait_ge(s.gathered, b * (16 * 4 * TAPS) + 16 * 4 * TAPS)
                    for k in range(TAPS):
                        link(nc.vector.tensor_scalar(gsum[:, k, :], corner[:, 0, k, :], cw[:, 0, k:k + 1], None,
                                                     ALU.mult))
                    for c4 in range(1, 4):
                        for k in range(TAPS):
                            link(nc.vector.scalar_tensor_tensor(gsum[:, k, :], corner[:, c4, k, :],
                                                                cw[:, c4, k:k + 1], gsum[:, k, :],
                                                                ALU.mult, ALU.add))
                    assert n[0] == SLOW_LINKS
                    nc.vector.tensor_copy(over[:, 0:1], gsum[:, 0, 0:1]).then_inc(s.gsum_ready, 1)
                    dve.sem_inc(s.base_free, 1)
                    run(residual, b, par, range(3))
                    normalise(b, par)
                    run(choose, b, par, range(CHAIN))
                    run(place_rows, b, par, range(4))

                dve.sem_inc(s.base_free, 1)
                for b in range(2):
                    gathered_band(b, b)
                with dve.Fori(1, BANDS // 2) as i:
                    gathered_band(i * 2, 0)
                    gathered_band(i * 2 + 1, 1)
            with dve.Else():
                def step(b, par, _):
                    known = isinstance(b, int)
                    placing = (lambda link: place_rows(b - 3, 1 - par, link)) if not known or b >= 3 else (lambda link: None)
                    choosing = (lambda link: choose(b - 2, par, link)) if not known or b >= 2 else (lambda link: None)
                    adding = (lambda link: residual(b - 1, 1 - par, link)) if not known or b >= 1 else (lambda link: None)
                    hatting = (lambda link: hats(b + 2, par, link)) if not known or b + 2 < BANDS else (lambda link: None)
                    placing(0)
                    multiply(b, par, 0)
                    placing(1)
                    multiply(b, par, 1)
                    placing(2)
                    multiply(b, par, 2)
                    placing(3)
                    adding(0)
                    choosing(0)
                    hatting(0)
                    adding(1)
                    choosing(1)
                    hatting(1)
                    choosing(2)
                    hatting(2)
                    choosing(3)
                    adding(2)
                    choosing(4)
                    choosing(5)
                    if not known or b >= 1:
                        normalise(b - 1, 1 - par)

                band_loop(dve, step)
                b = BANDS - 1
                run(place_rows, b - 2, 1, range(4))
                choose(b - 1, 0, 0)
                run(residual, b, 1, range(3))
                run(choose, b - 1, 0, range(1, CHAIN))
                normalise(b, 1)
                run(place_rows, b - 1, 0, range(4))
                run(choose, b, 1, range(CHAIN))
                run(place_rows, b, 1, range(4))

            m = [0]

            def then(ins):
                ins.then_inc(s.plan_step, 1)
                m[0] += 1
                dve.wait_ge(s.plan_step, m[0])

            def row_of(first, n):
                return table_sb[0:1, first:first + n]

            n_thr = P * BANDS // BLOCK
            dve.wait_ge(s.count_psum, 1)
            then(nc.vector.tensor_copy(count[:, :], bank[6][0:1, 0:EXPERTS]))
            nc.vector.tensor_tensor(pad_row[:, :], count[:, :], row_of(T_REGION, EXPERTS), ALU.add
                                    ).then_inc(s.pad_ready, 1)
            then(nc.vector.tensor_tensor(over_t[:, :, :], count[:, :].unsqueeze(2).broadcast_to([1, EXPERTS, n_thr]),
                                         row_of(T_THRESH, n_thr).unsqueeze(1).broadcast_to([1, EXPERTS, n_thr]),
                                         ALU.is_gt))
            then(nc.vector.tensor_reduce(nblk[:, :], over_t[:, :, :], AX_X, ALU.add))
            then(nc.vector.tensor_tensor(tri_t[:, :, :], nblk[:, :].unsqueeze(1).broadcast_to([1, EXPERTS, EXPERTS]),
                                         row_of(T_TRI, EXPERTS * EXPERTS).rearrange("o (a b) -> o a b", a=EXPERTS),
                                         ALU.mult))
            then(nc.vector.tensor_reduce(upto[:, :], tri_t[:, :, :], AX_X, ALU.add))
            then(nc.vector.tensor_tensor(past[:, :, :], row_of(T_BLK, BLOCKS).unsqueeze(2).broadcast_to([1, BLOCKS, EXPERTS]),
                                         upto[:, :].unsqueeze(1).broadcast_to([1, BLOCKS, EXPERTS]), ALU.is_ge))
            then(nc.vector.tensor_reduce(blk_e[:, :], past[:, :, :], AX_X, ALU.add))
            then(nc.vector.tensor_tensor(past_n[:, :, :], past[:, :, :],
                                         nblk[:, :].unsqueeze(1).broadcast_to([1, BLOCKS, EXPERTS]), ALU.mult))
            then(nc.vector.tensor_reduce(blk_first[:, :], past_n[:, :, :], AX_X, ALU.add))
            then(nc.vector.scalar_tensor_tensor(blk_row[:, :], blk_first[:, :], -float(BLOCK), row_of(T_BLKROW, BLOCKS),
                                                ALU.mult, ALU.add))
            then(nc.vector.scalar_tensor_tensor(blk_row[:, :], blk_e[:, :], float(REGION), blk_row[:, :],
                                                ALU.mult, ALU.add))
            nc.vector.tensor_scalar(blk_i[:, :], blk_row[:, :], float(IDLE_ROW), None, ALU.min
                                    ).then_inc(s.plan_ready, 1)

            dve.wait_ge(s.stashed, BANDS)
            nc.vector.tensor_tensor(e_all[:, :, :], top_all[:, :, :],
                                    top_all[:, :, 0:1].broadcast_to([P, BANDS, EXPERTS]), ALU.subtract
                                    ).then_inc(s.exp_in, 1)
            dve.wait_ge(s.exp_out, 1)
            nc.vector.tensor_reduce(e_sum[:, :], e_all[:, :, :], AX_X, ALU.add).then_inc(s.share_step, 1)
            dve.wait_ge(s.share_step, 1)
            nc.vector.reciprocal(share[:, 0, :], e_sum[:, :]).then_inc(s.share_step, 1)
            dve.wait_ge(s.share_step, 2)
            nc.vector.tensor_tensor(share[:, 1, :], e_all[:, :, 1], share[:, 0, :], ALU.mult).then_inc(s.share_step, 1)

            def keep_dest(turn, place):
                i, slot, uses = block_at(turn, place)
                dve.wait_ge(rows_arrived[slot], uses * 16 + 16)
                if not isinstance(i, int):
                    settle(dve)
                at_least(dve, sent[slot], uses * (16 * SUBS))
                if not isinstance(i, int):
                    settle(dve)
                nc.vector.tensor_copy(to[:, slot, :].unsqueeze(2), rows_in[:, slot, :, C:C + 1].bitcast(I32)
                                      ).then_inc(s.to_ready, 1)

            def finish(turn, place):
                i, slot, uses = block_at(turn, place)
                dve.wait_ge(s.y_psum2, i + 1)
                at_least(dve, sent[slot], uses * (16 * SUBS))
                b2_row = w_blk[:, slot, WROW - C:].unsqueeze(1).broadcast_to([P, SUBS, C])
                nc.vector.tensor_tensor(y[:, slot, :, :], bank[slot][:, BLOCK:2 * BLOCK].rearrange(
                    "p (j c) -> p j c", c=C), b2_row, ALU.add).then_inc(s.y_done, 1)

            def block_step(turn, place):
                finish(turn, place)
                if not is_last(turn, place):
                    keep_dest(turn, place + 1)

            keep_dest(0, 0)
            block_loop(dve, block_step)

            dve.wait_ge(s.share_step, 3)

            for g in range(BANDS // GB):
                group_slot, uses = g % BACK, g // BACK
                dve.wait_ge(back_arrived[group_slot], 32 * (uses + 1))
                at_least(dve, stored[group_slot], 16 * uses)
                for j in range(GB):
                    b = g * GB + j
                    nc.vector.scalar_tensor_tensor(res[:, group_slot, j, :], y_back[:, group_slot, 0, j, :], share[:, 0, b:b + 1],
                                                   x1[:, b, :], ALU.mult, ALU.add).then_inc(s.res_step, 1)
                dve.wait_ge(s.res_step, g * GB + GB)
                dve.wait_ge(s.scaled, g * GB + GB)
                nc.vector.tensor_tensor(res[:, group_slot, :, :], res[:, group_slot, :, :], y_back[:, group_slot, 1, :, :], ALU.add
                                        ).then_inc(s.res_ready, 1)

        @block.tensor
        def _(pe):
            pe.wait_ge(s.early_loaded, 16 * 4)
            pe.wait_ge(s.zeroed, N_CLEARED)

            def transpose_image(m):
                at_least(pe, s.xnT_ready, m * 2)
                for b in range(BPI):
                    pe.wait_ge(s.xn_ready, m * BPI + b + 1)
                    last = nc.tensor.transpose(bank[b // 4][:, (b % 4) * P:(b % 4 + 1) * P],
                                               x_nat[:, m * BPI + b, :], ident_sb[:, :])
                    if b % 4 == 3:
                        last.then_inc(s.xnT_psum, 1)

            def convolve(m, h):
                pe.wait_ge(s.xnT_ready, m * 2 + 2)
                at_least(pe, s.conv_ready, (m * 2 + h - 1) * 4)
                for k in range(TAPS):
                    g = (k + h) % 4
                    last = nc.tensor.matmul(
                        bank[2 + h][32 * g:32 * g + 32, :], woff_sb[:, k, :],
                        xnT[:, m % 2, 16 * h + k // 3:16 * h + k // 3 + 16, k % 3:k % 3 + SIDE],
                        start=(k < 4), stop=(k + 4 >= TAPS))
                last.then_inc(s.conv_psum, 1)

            def fold_groups(m, h):
                pe.wait_ge(s.conv_ready, (m * 2 + h + 1) * 4)
                if h == 0:
                    at_least(pe, s.offs_ready, m)
                for b in range(4):
                    c0 = (4 * h + b) * OFFS
                    last = nc.tensor.matmul(bank[5][:, c0:c0 + OFFS], conv_sb[:, h, b * P:(b + 1) * P], fold_sb[:, :],
                                            start=True, stop=True)
                last.then_inc(s.fold_psum, 1)

            transpose_image(0)
            for m in range(IMAGES):
                convolve(m, 0)
                convolve(m, 1)
                if m + 1 < IMAGES:
                    transpose_image(m + 1)
                fold_groups(m, 0)
                fold_groups(m, 1)
            pe.wait_ge(s.near_ready, 3 * IMAGES)
            for m in range(IMAGES):
                last = nc.tensor.matmul(bank[6][0:1, 0:1], near_n[:, m:m + 1], ones[:, :],
                                        start=(m == 0), stop=(m == IMAGES - 1))
            last.then_inc(s.near_psum, 1)

            def transpose_hats(b, par):
                pe.wait_ge(s.hat3_ready, b + 1)
                if not isinstance(b, int) or b >= 3:
                    pe.wait_ge(s.route, (b - 3) * 6 + 1)
                for i in range(PAIRS):
                    last = nc.tensor.transpose(bank4b[0:2 * SLOT, i * P:(i + 1) * P],
                                               hat3[:, par, 2 * i:2 * i + 2, :].rearrange("p k r -> p (k r)"),
                                               identb_sb[:, :])
                last.then_inc(s.hatT_psum, 1)

            def spread_hats(b, par, u):
                pe.wait_ge(s.hatT_ready, b + 1)
                slot, n, odd = (par + u) % 2, UNITS[u], u % 2
                moving = hatT[:, 4, :] if u == 2 else hatT[:, 0:4, :].rearrange("r i t -> r (i t)")
                at_least(pe, s.y_ready, b * 3 + u - 1)
                nc.tensor.matmul(bank[slot][0:Q, 0:n], spread_sb[:, 2 * odd, :], moving,
                                 start=True, stop=True).then_inc(s.y_psum, 1)
                at_least(pe, s.S_ready, b * 3 + u - 1)
                nc.tensor.matmul(bank[2 + slot][0:Q, 0:n], spread_sb[:, 2 * odd + 1, :], moving,
                                 start=True, stop=True).then_inc(s.x_psum, 1)

            ORDER = [0, 2, 4, 6, 1, 3, 5, 7, 8]

            def sample(b, par, loads, g):
                if g == 0:
                    pe.wait_ge(s.S_ready, b * 3 + 3)
                    pe.wait_ge((s.win_even, s.win_odd)[par], loads * (16 * TILES))
                at_least(pe, s.samp_act, b * 3 + g - 1)
                weights = S[:, par, :].rearrange("q (k t p) -> q t k p", k=TAPS, t=TILES)
                for i in range(GROUPS[g]):
                    t = sum(GROUPS[:g]) + i
                    last = nc.tensor.matmul(bank[5 + (par + g) % 2][:, i * TAPS * TT:(i + 1) * TAPS * TT],
                                            xwin[:, par, t, :], weights[:, t], start=True, stop=True)
                last.then_inc(s.samp_psum, 1)

            FIRST_TAPS = 5

            def project(b, par, taps, order):
                if taps[0] == 0:
                    at_least(pe, s.x1_ready, b)
                    at_least(pe, s.place_ready, b - 1)
                for j in taps:
                    last = nc.tensor.matmul(bank[7][:, 0:C], samp[:, par, j, :], filt_sb[:, order[j], :],
                                            start=(j == 0), stop=(j == TAPS - 1))
                if taps[-1] == TAPS - 1:
                    last.then_inc(s.e_psum, 1)

            def samples_ready(b):
                pe.wait_ge(s.samp_act, b * 3 + 3)

            def transpose_tokens(b, par):
                pe.wait_ge(s.xn2_ready, b + 1)
                nc.tensor.transpose(bank[4][:, 0:P], xn2[:, par, :], ident_sb[:, :]).then_inc(s.t_psum, 1)

            def gate(b, par):
                pe.wait_ge(s.xn2T_ready, b + 1)
                nc.tensor.matmul(bank[4][:, 0:EXPERTS], xn2T[:, par, :], gw_sb[:, :],
                                 start=True, stop=True).then_inc(s.l_psum, 1)

            def count_places(b, par):
                pe.wait_ge(s.route, b * 6 + 5)
                where = bank[7][:, 256:256 + EXPERTS]
                nc.tensor.matmul(where, before_sb[:, :], both[:, par, :], start=True, stop=False)
                nc.tensor.matmul(where, every_sb[:, :], seen[:, par, :], start=False, stop=True
                                 ).then_inc(s.place_psum, 1)

            pe.wait_ge(s.consts_loaded, 16 * N_CONSTS)
            pe.wait_ge(s.tables_ready, 3)
            transpose_hats(0, 0)
            flag = is_far(pe)
            with pe.If(flag):
                pe.wait_ge(s.win_even, 16 * TILES)
                pe.wait_ge(s.win_odd, 16 * TILES)
                with pe.Fori(0, BANDS // 2) as i:
                    for par in range(2):
                        b = i * 2 + par
                        pe.wait_ge(s.gsum_ready, b + 1)
                        for k in range(TAPS):
                            if k >= 2:
                                pe.wait_ge(s.samp_slow, b * TAPS + k - 1)
                            nc.tensor.transpose(bank[k % 2][:, 0:P], gsum[:, k, :], ident_sb[:, :]
                                                ).then_inc(s.g_psum, 1)
                        pe.wait_ge(s.samp_slow, b * TAPS + TAPS)
                        for j in range(TAPS):
                            last = nc.tensor.matmul(bank[7][:, 0:C], samp[:, par, j, :], filt_sb[:, j, :],
                                                    start=(j == 0), stop=(j == TAPS - 1))
                        last.then_inc(s.e_psum, 1)
                        transpose_tokens(b, par)
                        gate(b, par)
                        count_places(b, par)
            with pe.Else():
                def step(b, par, loads):
                    known = isinstance(b, int)
                    spread_hats(b, par, 0)
                    if not known or b >= 3:
                        pe.wait_ge(s.x1_ready, b - 1)
                        count_places(b - 3, 1 - par)
                    spread_hats(b, par, 1)
                    if not known or b >= 1:
                        samples_ready(b - 1)
                        project(b - 1, 1 - par, range(FIRST_TAPS), ORDER)
                    if not known or b >= 2:
                        transpose_tokens(b - 2, par)
                    spread_hats(b, par, 2)
                    if not known or b >= 1:
                        project(b - 1, 1 - par, range(FIRST_TAPS, TAPS), ORDER)
                    if not known or b >= 2:
                        gate(b - 2, par)
                    sample(b, par, loads, 0)
                    if not known or b + 1 < BANDS:
                        transpose_hats(b + 1, 1 - par)
                    sample(b, par, loads, 1)
                    sample(b, par, loads, 2)

                band_loop(pe, step)
                b = BANDS - 1
                pe.wait_ge(s.x1_ready, b)
                count_places(b - 2, 1)
                pe.wait_ge(s.route, (b - 2) * 6 + 1)
                transpose_tokens(b - 1, 0)
                samples_ready(b)
                project(b, 1, range(TAPS), ORDER)
                gate(b - 1, 0)
                pe.wait_ge(s.x1_ready, b + 1)
                count_places(b - 1, 0)
                pe.wait_ge(s.route, (b - 1) * 6 + 1)
                transpose_tokens(b, 1)
                gate(b, 1)
                pe.wait_ge(s.place_ready, b)
                count_places(b, 1)

            pe.wait_ge(s.route, BANDS * 6)
            nc.tensor.matmul(bank[6][:, 0:EXPERTS], every_sb[:, :], seen[:, 0, :], start=True, stop=True
                             ).then_inc(s.count_psum, 1)

            def transpose_rows(turn, place):
                i, slot, uses = block_at(turn, place)
                pe.wait_ge(rows_arrived[slot], uses * 16 + 16)
                at_least(pe, s.y_done, i - (RING - 1))
                for j in range(SUBS):
                    last = nc.tensor.transpose(bank[slot][:, j * P:(j + 1) * P], rows_in[:, slot, j, 0:C], ident_sb[:, :])
                last.then_inc(s.rowsT_psum, 1)

            def up(turn, place):
                i, slot, uses = block_at(turn, place)
                pe.wait_ge(w_arrived[slot], uses * 16 + 16)
                pe.wait_ge(s.rowsT_ready, i + 1)
                at_least(pe, s.h_ready, (i - (RING - 1)) * HALVES)
                for h in range(HALVES):
                    last = nc.tensor.matmul(bank[RING + slot][:, h * BLOCK:(h + 1) * BLOCK],
                                            w_blk[:, slot, h * P:(h + 1) * P], rowsT[:, slot, :], start=True, stop=True)
                last.then_inc(s.h_psum, 1)

            def down(turn, place):
                i, slot, uses = block_at(turn, place)
                pe.wait_ge(s.h_ready, i * HALVES + HALVES)
                for j in range(SUBS):
                    for h in range(HALVES):
                        last = nc.tensor.matmul(bank[slot][:, BLOCK + j * C:BLOCK + (j + 1) * C],
                                                hid[:, slot, h, j * P:(j + 1) * P],
                                                w_blk[:, slot, W_UP + h * C:W_UP + (h + 1) * C],
                                                start=(h == 0), stop=(h == HALVES - 1))
                last.then_inc(s.y_psum2, 1)

            def block_step(turn, place):
                up(turn, place)
                if not is_last(turn, place):
                    transpose_rows(turn, place + 1)
                if not is_first(turn, place):
                    down(*previous(turn, place))

            transpose_rows(0, 0)
            block_loop(pe, block_step)
            down(TURNS, REST - 1)


def kernel(x, L0_conv_w_offset, L0_conv_b_offset, L0_conv_filt, L0_ffn_gate_w, L0_ffn_gate_b,
           L0_ffn_W1, L0_ffn_b1, L0_ffn_W2, L0_ffn_b2):
    import numpy as np
    import concourse.bacc as bacc
    from concourse.bass_utils import run_bass_kernel_spmd

    x = np.asarray(x)
    rows = x.reshape(BANDS, P, C)
    tiles = x.reshape(BANDS, TILE, TILES, TILE, C).transpose(0, 2, 1, 3, 4).reshape(BANDS, P, C)
    w2 = np.asarray(L0_ffn_W2).reshape(EXPERTS, HALVES, P, C).transpose(2, 0, 1, 3)
    experts = np.concatenate([
        np.asarray(L0_ffn_W1).transpose(1, 0, 2),
        np.asarray(L0_ffn_b1).reshape(EXPERTS, HALVES, P).transpose(2, 0, 1),
        w2.reshape(P, EXPERTS, HALVES * C),
        np.broadcast_to(np.asarray(L0_ffn_b2), (P, EXPERTS, C)),
    ], axis=2)
    arrays = {
        "x_rows": rows,
        "x_tiles": tiles,
        "w_offset": np.asarray(L0_conv_w_offset),
        "b_offset": np.asarray(L0_conv_b_offset),
        "filt": np.asarray(L0_conv_filt).reshape(C, C, TAPS).transpose(1, 2, 0),
        "gate_w": np.asarray(L0_ffn_gate_w),
        "gate_b": np.asarray(L0_ffn_gate_b),
        "experts": experts,
        **window_constants(),
    }
    arrays = {k: np.ascontiguousarray(v) for k, v in arrays.items()}
    nc = bacc.Bacc("TRN2", target_bir_lowering=False, num_devices=1)
    args = {k: nc.dram_tensor(f"in_{k}", v.shape, mybir.dt.from_np(v.dtype), kind="ExternalInput").ap()
            for k, v in arrays.items()}
    out = nc.dram_tensor("out_tiles", (BANDS, P, C), F32, kind="ExternalOutput").ap()
    program(nc, **args, out=out)
    result = run_bass_kernel_spmd(nc, [{f"in_{k}": v for k, v in arrays.items()}], core_ids=[0])
    got = result.results[0]["out_tiles"]
    return got.reshape(BANDS, TILES, TILE, TILE, C).transpose(0, 2, 1, 3, 4).reshape(IMAGES, SIDE, SIDE, C)
```
